# Optimizing a Trainium2 kernel written in Bass

```python
import numpy as np
import jax
import jax.numpy as jnp

def _softmax(x, axis=-1):
    return jax.nn.softmax(x, axis=axis)

def _gelu(x):
    return jax.nn.gelu(x, approximate=True)

def _silu(x):
    return jax.nn.silu(x)

def _sigmoid(x):
    return jax.nn.sigmoid(x)

def _layernorm(x, axis=-1, eps=1e-05):
    m = jnp.mean(x, axis=axis, keepdims=True)
    v = jnp.var(x, axis=axis, keepdims=True)
    return (x - m) / jnp.sqrt(v + eps)

def _scatter_add(tgt, idx, src, axis=0):
    return tgt.at[idx].add(src)

def _segment_sum(src, seg, n):
    return jax.ops.segment_sum(src, seg, n)
kernel_name = 'mk_seq_postln_d4_jaxref_r8_954798'

def setup_inputs(seed: int=0):
    np.random.seed(seed)
    _w = jnp.asarray

    def _L0_attn_setup():
        import jax, jax.numpy as jnp
        import numpy as np
        B, N, D, H = (4, 512, 128, 16)
        HD = D // H

        def _kernel(x):
            return jax.nn.elu(x) + 1.0
        key = jax.random.key(seed)
        k1, k2, k3, k4 = jax.random.split(key, 4)
        x = jax.random.normal(k1, (B, N, D), dtype=jnp.float32)
        w_qkv = jax.random.normal(k2, (3 * D, D), dtype=jnp.float32) * (1.0 / np.sqrt(D))
        w_out = jax.random.normal(k3, (D, D), dtype=jnp.float32) * (1.0 / np.sqrt(D))
        b_out = jax.random.normal(k4, (D,), dtype=jnp.float32) * 0.01
        return {'x': x, 'w_qkv': w_qkv, 'w_out': w_out, 'b_out': b_out}
    _L0_attn_in = _L0_attn_setup()

    def _L0_ffn_setup():
        import jax, jax.numpy as jnp
        import numpy as np
        L, H, NH, NKV, HD, FF, E, K = (4, 128, 16, 4, 64, 256, 8, 2)
        B, S = (2, 256)
        THETA, EPS = (10000.0, 1e-05)

        def _rms(x, w):
            return x * jax.lax.rsqrt(jnp.mean(x * x, axis=-1, keepdims=True) + EPS) * w

        def _rope_cos_sin(seq_len, head_dim, theta):
            inv = 1.0 / theta ** (jnp.arange(0, head_dim, 2, dtype=jnp.float32) / head_dim)
            f = jnp.arange(seq_len, dtype=jnp.float32)[:, None] * inv
            emb = jnp.concatenate([f, f], axis=-1)
            return (jnp.cos(emb), jnp.sin(emb))

        def _rot_half(x):
            h = x.shape[-1] // 2
            return jnp.concatenate([-x[..., h:], x[..., :h]], axis=-1)

        def _attention(x, wq, wk, wv, wo, cos, sin, causal_bias):
            b, s, _ = x.shape
            q = (x @ wq).reshape(b, s, NH, HD).transpose(0, 2, 1, 3)
            k = (x @ wk).reshape(b, s, NKV, HD).transpose(0, 2, 1, 3)
            v = (x @ wv).reshape(b, s, NKV, HD).transpose(0, 2, 1, 3)
            c = cos[None, None]
            sn = sin[None, None]
            q = q * c + _rot_half(q) * sn
            k = k * c + _rot_half(k) * sn
            rep = NH // NKV
            k = jnp.repeat(k, rep, axis=1)
            v = jnp.repeat(v, rep, axis=1)
            scores = jnp.einsum('bhqd,bhkd->bhqk', q, k) / jnp.sqrt(jnp.asarray(HD, x.dtype))
            scores = scores + causal_bias
            attn = jax.nn.softmax(scores, axis=-1)
            out = jnp.einsum('bhqk,bhkd->bhqd', attn, v)
            out = out.transpose(0, 2, 1, 3).reshape(b, s, NH * HD)
            return out @ wo

        def _moe(x, wr, wg, wu, wd):
            logits = x @ wr
            probs = jax.nn.softmax(logits, axis=-1)
            topv, topi = jax.lax.top_k(probs, K)
            topv = topv / jnp.sum(topv, axis=-1, keepdims=True)
            comb = jnp.sum(jax.nn.one_hot(topi, E, dtype=x.dtype) * topv[..., None], axis=-2)
            out = jnp.zeros_like(x)
            for e in range(E):
                h = jax.nn.silu(x @ wg[e]) * (x @ wu[e])
                out = out + comb[..., e:e + 1] * (h @ wd[e])
            return out
        key = jax.random.key(seed)
        ks = jax.random.split(key, 12)
        sc = 0.02
        inp = {'hidden_states': jax.random.normal(ks[0], (B, S, H), jnp.float32), 'ln1_w': jnp.ones((L, H), jnp.float32), 'ln2_w': jnp.ones((L, H), jnp.float32), 'wq': jax.random.normal(ks[1], (L, H, NH * HD), jnp.float32) * sc, 'wk': jax.random.normal(ks[2], (L, H, NKV * HD), jnp.float32) * sc, 'wv': jax.random.normal(ks[3], (L, H, NKV * HD), jnp.float32) * sc, 'wo': jax.random.normal(ks[4], (L, NH * HD, H), jnp.float32) * sc, 'wr': jax.random.normal(ks[5], (L, H, E), jnp.float32) * sc, 'wg': jax.random.normal(ks[6], (L, E, H, FF), jnp.float32) * sc, 'wu': jax.random.normal(ks[7], (L, E, H, FF), jnp.float32) * sc, 'wd': jax.random.normal(ks[8], (L, E, FF, H), jnp.float32) * sc}
        return inp
    _L0_ffn_in = _L0_ffn_setup()

    def _L1_attn_setup():
        import jax, jax.numpy as jnp
        import numpy as np
        L, H, D_MODEL, FFN = (2, 8, 128, 512)
        HD = D_MODEL // H
        SCALE_BASE = 64
        EPS = 1e-05

        def _layernorm(x, w, b):
            mu = x.mean(-1, keepdims=True)
            var = ((x - mu) ** 2).mean(-1, keepdims=True)
            return (x - mu) * jax.lax.rsqrt(var + EPS) * w + b

        def _groupnorm(y, w, b):
            B, S, _ = y.shape
            yg = y.reshape(B, S, H, HD)
            mu = yg.mean(-1, keepdims=True)
            var = ((yg - mu) ** 2).mean(-1, keepdims=True)
            yn = ((yg - mu) * jax.lax.rsqrt(var + EPS)).reshape(B, S, H * HD)
            return yn * w + b

        def _xpos_tables(S):
            scale_vec = (np.arange(0, HD, 2) + 0.4 * HD) / (1.4 * HD)
            power = (np.arange(S, dtype=np.float64) / SCALE_BASE)[:, None]
            scale = scale_vec[None, :] ** power
            half = HD // 2
            inv_freq = 1.0 / 10000.0 ** (np.arange(half, dtype=np.float64) / half)
            ang = np.arange(S, dtype=np.float64)[:, None] * inv_freq[None, :]
            sin, cos = (np.sin(ang), np.cos(ang))
            dup = lambda m: jnp.asarray(np.repeat(m, 2, axis=-1).astype(np.float32))
            return (dup(sin * scale), dup(cos * scale), dup(sin / scale), dup(cos / scale))

        def _rotate_every_two(x):
            x1, x2 = (x[..., ::2], x[..., 1::2])
            return jnp.stack((-x2, x1), axis=-1).reshape(x.shape)

        def _decay_mask(S):
            gammas = 1.0 - np.exp(np.linspace(np.log(1.0 / 32), np.log(1.0 / 64), H))
            n = np.arange(S)[:, None]
            m = np.arange(S)[None, :]
            diff = (n - m).astype(np.float64)
            D = np.where(n >= m, gammas[:, None, None] ** diff[None], 0.0)
            return jnp.asarray(D.astype(np.float32))
        key = jax.random.key(seed)
        ks = jax.random.split(key, 8)
        B, S = (2, 256)
        rn = lambda k, shape, s: jax.random.normal(k, shape, dtype=jnp.float32) * s
        return {'X': rn(ks[0], (B, S, D_MODEL), 1.0), 'ln1_w': jnp.ones((L, D_MODEL), jnp.float32), 'ln1_b': jnp.zeros((L, D_MODEL), jnp.float32), 'ln2_w': jnp.ones((L, D_MODEL), jnp.float32), 'ln2_b': jnp.zeros((L, D_MODEL), jnp.float32), 'WQ': rn(ks[1], (L, H, D_MODEL, HD), 1.0 / D_MODEL), 'WK': rn(ks[2], (L, H, D_MODEL, HD), 1.0 / D_MODEL), 'WV': rn(ks[3], (L, H, D_MODEL, HD), 1.0 / D_MODEL), 'gn_w': jnp.ones((L, D_MODEL), jnp.float32), 'gn_b': jnp.zeros((L, D_MODEL), jnp.float32), 'WG': rn(ks[4], (L, D_MODEL, D_MODEL), 1.0 / D_MODEL), 'WO': rn(ks[5], (L, D_MODEL, D_MODEL), 1.0 / D_MODEL), 'ffn_w1': rn(ks[6], (L, D_MODEL, FFN), 1.0 / np.sqrt(D_MODEL)), 'ffn_b1': jnp.zeros((L, FFN), jnp.float32), 'ffn_w2': rn(ks[7], (L, FFN, D_MODEL), 1.0 / np.sqrt(FFN)), 'ffn_b2': jnp.zeros((L, D_MODEL), jnp.float32)}
    _L1_attn_in = _L1_attn_setup()

    def _L1_ffn_setup():
        import jax, jax.numpy as jnp
        import numpy as np
        E, K, H, F, R = (8, 2, 128, 256, 64)
        B, S = (2, 256)
        key = jax.random.key(seed)
        k0, k1, k2, k3, k4 = jax.random.split(key, 5)
        return {'hidden_states': jax.random.normal(k0, (B, S, H), dtype=jnp.float32), 'W_A': jax.random.normal(k1, (E, R, H), dtype=jnp.float32) * 0.02, 'W_B': jax.random.normal(k2, (E, F, R), dtype=jnp.float32) * 0.02, 'W_up': jax.random.normal(k3, (E, F, H), dtype=jnp.float32) * 0.02, 'W_down': jax.random.normal(k4, (E, H, F), dtype=jnp.float32) * 0.02}
    _L1_ffn_in = _L1_ffn_setup()

    def _L2_attn_setup():
        import jax, jax.numpy as jnp
        import numpy as np
        D_MODEL, N_HEADS, D_HEAD = (128, 16, 64)
        QKV = N_HEADS * D_HEAD
        EPS = 1e-05

        def _layernorm(x, gamma, beta):
            mu = jnp.mean(x, axis=-1, keepdims=True)
            var = jnp.mean((x - mu) ** 2, axis=-1, keepdims=True)
            return (x - mu) * jax.lax.rsqrt(var + EPS) * gamma + beta
        key = jax.random.key(seed)
        ks = jax.random.split(key, 5)
        B, T = (1, 256)
        s_in = 1.0 / np.sqrt(D_MODEL)
        s_qkv = 1.0 / np.sqrt(QKV)
        return {'x': jax.random.normal(ks[0], (B, T, D_MODEL), dtype=jnp.float32), 'Wq': jax.random.normal(ks[1], (QKV, D_MODEL), dtype=jnp.float32) * s_in, 'Wk': jax.random.normal(ks[2], (QKV, D_MODEL), dtype=jnp.float32) * s_in, 'Wv': jax.random.normal(ks[3], (QKV, D_MODEL), dtype=jnp.float32) * s_in, 'Wo': jax.random.normal(ks[4], (D_MODEL, QKV), dtype=jnp.float32) * s_qkv, 'q_gamma': jnp.ones((D_HEAD,), dtype=jnp.float32), 'q_beta': jnp.zeros((D_HEAD,), dtype=jnp.float32), 'k_gamma': jnp.ones((D_HEAD,), dtype=jnp.float32), 'k_beta': jnp.zeros((D_HEAD,), dtype=jnp.float32)}
    _L2_attn_in = _L2_attn_setup()

    def _L2_ffn_setup():
        import jax, jax.numpy as jnp
        import numpy as np
        B, S, D, H, F, E = (2, 128, 128, 16, 512, 8)
        HD = D // H
        EPS = 1e-06

        def _layernorm(x, g, b):
            m = jnp.mean(x, axis=-1, keepdims=True)
            v = jnp.var(x, axis=-1, keepdims=True)
            return (x - m) / jnp.sqrt(v + EPS) * g + b
        key = jax.random.key(seed)
        ks = jax.random.split(key, 10)
        sc = 0.02
        x = jax.random.normal(ks[0], (B, S, D), jnp.float32)
        Wq = jax.random.normal(ks[1], (D, D), jnp.float32) * sc
        Wk = jax.random.normal(ks[2], (D, D), jnp.float32) * sc
        Wv = jax.random.normal(ks[3], (D, D), jnp.float32) * sc
        Wo = jax.random.normal(ks[4], (D, D), jnp.float32) * sc
        bo = jnp.zeros((D,), jnp.float32)
        Wr = jax.random.normal(ks[5], (D, E), jnp.float32) * sc
        We1 = jax.random.normal(ks[6], (E, D, F), jnp.float32) * sc
        be1 = jnp.zeros((E, F), jnp.float32)
        We2 = jax.random.normal(ks[7], (E, F, D), jnp.float32) * sc
        be2 = jnp.zeros((E, D), jnp.float32)
        ln1_g = jnp.ones((D,), jnp.float32)
        ln1_b = jnp.zeros((D,), jnp.float32)
        ln2_g = jnp.ones((D,), jnp.float32)
        ln2_b = jnp.zeros((D,), jnp.float32)
        return {'x': x, 'Wq': Wq, 'Wk': Wk, 'Wv': Wv, 'Wo': Wo, 'bo': bo, 'Wr': Wr, 'We1': We1, 'be1': be1, 'We2': We2, 'be2': be2, 'ln1_g': ln1_g, 'ln1_b': ln1_b, 'ln2_g': ln2_g, 'ln2_b': ln2_b}
    _L2_ffn_in = _L2_ffn_setup()

    def _L3_attn_setup():
        import jax, jax.numpy as jnp
        import numpy as np
        HIDDEN = 128
        HEADS = 16
        BATCH = 2
        SEQ = 256
        key = jax.random.key(seed)
        k1, k2, k3 = jax.random.split(key, 3)
        x = jax.random.normal(k1, (BATCH, SEQ, HIDDEN), dtype=jnp.float32)
        w_qkv = jax.random.normal(k2, (3 * HIDDEN, HIDDEN), dtype=jnp.float32)
        w_o = jax.random.normal(k3, (HIDDEN, HIDDEN), dtype=jnp.float32)
        return {'x': x, 'w_qkv': w_qkv, 'w_o': w_o}
    _L3_attn_in = _L3_attn_setup()

    def _L3_ffn_setup():
        import jax, jax.numpy as jnp
        import numpy as np
        MAX_VAL = 100.0
        key = jax.random.key(seed)
        k1, k2, k3 = jax.random.split(key, 3)
        B, S, D_IN, D_OUT = (4, 1024, 128, 128)
        x = jax.random.normal(k1, (B, S, D_IN), dtype=jnp.float32)
        weights = jax.random.normal(k2, (D_OUT, D_IN), dtype=jnp.float32)
        scale = jnp.ones((D_OUT,), dtype=jnp.float32)
        bias = jax.random.normal(k3, (D_OUT,), dtype=jnp.float32)
        return {'x': x, 'weights': weights, 'scale': scale, 'bias': bias}
    _L3_ffn_in = _L3_ffn_setup()
    _d = {'L0_attn_x': _L0_attn_in['x'], 'L0_attn_w_qkv': _L0_attn_in['w_qkv'], 'L0_attn_w_out': _L0_attn_in['w_out'], 'L0_attn_b_out': _L0_attn_in['b_out'], 'L0_ffn_ln1_w': _L0_ffn_in['ln1_w'], 'L0_ffn_ln2_w': _L0_ffn_in['ln2_w'], 'L0_ffn_wq': _L0_ffn_in['wq'], 'L0_ffn_wk': _L0_ffn_in['wk'], 'L0_ffn_wv': _L0_ffn_in['wv'], 'L0_ffn_wo': _L0_ffn_in['wo'], 'L0_ffn_wr': _L0_ffn_in['wr'], 'L0_ffn_wg': _L0_ffn_in['wg'], 'L0_ffn_wu': _L0_ffn_in['wu'], 'L0_ffn_wd': _L0_ffn_in['wd'], 'L1_attn_ln1_w': _L1_attn_in['ln1_w'], 'L1_attn_ln1_b': _L1_attn_in['ln1_b'], 'L1_attn_ln2_w': _L1_attn_in['ln2_w'], 'L1_attn_ln2_b': _L1_attn_in['ln2_b'], 'L1_attn_WQ': _L1_attn_in['WQ'], 'L1_attn_WK': _L1_attn_in['WK'], 'L1_attn_WV': _L1_attn_in['WV'], 'L1_attn_gn_w': _L1_attn_in['gn_w'], 'L1_attn_gn_b': _L1_attn_in['gn_b'], 'L1_attn_WG': _L1_attn_in['WG'], 'L1_attn_WO': _L1_attn_in['WO'], 'L1_attn_ffn_w1': _L1_attn_in['ffn_w1'], 'L1_attn_ffn_b1': _L1_attn_in['ffn_b1'], 'L1_attn_ffn_w2': _L1_attn_in['ffn_w2'], 'L1_attn_ffn_b2': _L1_attn_in['ffn_b2'], 'L1_ffn_W_A': _L1_ffn_in['W_A'], 'L1_ffn_W_B': _L1_ffn_in['W_B'], 'L1_ffn_W_up': _L1_ffn_in['W_up'], 'L1_ffn_W_down': _L1_ffn_in['W_down'], 'L2_attn_Wq': _L2_attn_in['Wq'], 'L2_attn_Wk': _L2_attn_in['Wk'], 'L2_attn_Wv': _L2_attn_in['Wv'], 'L2_attn_Wo': _L2_attn_in['Wo'], 'L2_attn_q_gamma': _L2_attn_in['q_gamma'], 'L2_attn_q_beta': _L2_attn_in['q_beta'], 'L2_attn_k_gamma': _L2_attn_in['k_gamma'], 'L2_attn_k_beta': _L2_attn_in['k_beta'], 'L2_ffn_Wq': _L2_ffn_in['Wq'], 'L2_ffn_Wk': _L2_ffn_in['Wk'], 'L2_ffn_Wv': _L2_ffn_in['Wv'], 'L2_ffn_Wo': _L2_ffn_in['Wo'], 'L2_ffn_bo': _L2_ffn_in['bo'], 'L2_ffn_Wr': _L2_ffn_in['Wr'], 'L2_ffn_We1': _L2_ffn_in['We1'], 'L2_ffn_be1': _L2_ffn_in['be1'], 'L2_ffn_We2': _L2_ffn_in['We2'], 'L2_ffn_be2': _L2_ffn_in['be2'], 'L2_ffn_ln1_g': _L2_ffn_in['ln1_g'], 'L2_ffn_ln1_b': _L2_ffn_in['ln1_b'], 'L2_ffn_ln2_g': _L2_ffn_in['ln2_g'], 'L2_ffn_ln2_b': _L2_ffn_in['ln2_b'], 'L3_attn_w_qkv': _L3_attn_in['w_qkv'], 'L3_attn_w_o': _L3_attn_in['w_o'], 'L3_ffn_weights': _L3_ffn_in['weights'], 'L3_ffn_scale': _L3_ffn_in['scale'], 'L3_ffn_bias': _L3_ffn_in['bias']}
    _x0 = _d['L0_attn_x']
    _d['L0_attn_x'] = jax.random.normal(jax.random.fold_in(jax.random.key(seed), 1), (4, 512, 128), dtype=_x0.dtype)
    del _x0
    return _d

def reference(L0_attn_x, L0_attn_w_qkv, L0_attn_w_out, L0_attn_b_out, L0_ffn_ln1_w, L0_ffn_ln2_w, L0_ffn_wq, L0_ffn_wk, L0_ffn_wv, L0_ffn_wo, L0_ffn_wr, L0_ffn_wg, L0_ffn_wu, L0_ffn_wd, L1_attn_ln1_w, L1_attn_ln1_b, L1_attn_ln2_w, L1_attn_ln2_b, L1_attn_WQ, L1_attn_WK, L1_attn_WV, L1_attn_gn_w, L1_attn_gn_b, L1_attn_WG, L1_attn_WO, L1_attn_ffn_w1, L1_attn_ffn_b1, L1_attn_ffn_w2, L1_attn_ffn_b2, L1_ffn_W_A, L1_ffn_W_B, L1_ffn_W_up, L1_ffn_W_down, L2_attn_Wq, L2_attn_Wk, L2_attn_Wv, L2_attn_Wo, L2_attn_q_gamma, L2_attn_q_beta, L2_attn_k_gamma, L2_attn_k_beta, L2_ffn_Wq, L2_ffn_Wk, L2_ffn_Wv, L2_ffn_Wo, L2_ffn_bo, L2_ffn_Wr, L2_ffn_We1, L2_ffn_be1, L2_ffn_We2, L2_ffn_be2, L2_ffn_ln1_g, L2_ffn_ln1_b, L2_ffn_ln2_g, L2_ffn_ln2_b, L3_attn_w_qkv, L3_attn_w_o, L3_ffn_weights, L3_ffn_scale, L3_ffn_bias):

    def _L0_attn_ref(x, w_qkv, w_out, b_out):
        import jax, jax.numpy as jnp
        import numpy as np
        B, N, D, H = (4, 512, 128, 16)
        HD = D // H

        def _kernel(x):
            return jax.nn.elu(x) + 1.0
        b, n, d = x.shape
        qkv = x @ w_qkv.T
        qkv = qkv.reshape(b, n, 3, H, HD)
        q, k, v = (qkv[:, :, 0], qkv[:, :, 1], qkv[:, :, 2])
        q = _kernel(q)
        k = _kernel(k)
        kv = jnp.einsum('bnhd,bnhm->bhdm', k, v)
        z = 1.0 / (jnp.einsum('bnhd,bhd->bnh', q, k.sum(axis=1)) + 1e-06)
        out = jnp.einsum('bnhd,bhdm,bnh->bnhm', q, kv, z)
        out = out.reshape(b, n, d)
        return out @ w_out.T + b_out

    def _L0_ffn_ref(hidden_states, ln1_w, ln2_w, wq, wk, wv, wo, wr, wg, wu, wd):
        import jax, jax.numpy as jnp
        import numpy as np
        L, H, NH, NKV, HD, FF, E, K = (4, 128, 16, 4, 64, 256, 8, 2)
        B, S = (2, 256)
        THETA, EPS = (10000.0, 1e-05)

        def _rms(x, w):
            return x * jax.lax.rsqrt(jnp.mean(x * x, axis=-1, keepdims=True) + EPS) * w

        def _rope_cos_sin(seq_len, head_dim, theta):
            inv = 1.0 / theta ** (jnp.arange(0, head_dim, 2, dtype=jnp.float32) / head_dim)
            f = jnp.arange(seq_len, dtype=jnp.float32)[:, None] * inv
            emb = jnp.concatenate([f, f], axis=-1)
            return (jnp.cos(emb), jnp.sin(emb))

        def _rot_half(x):
            h = x.shape[-1] // 2
            return jnp.concatenate([-x[..., h:], x[..., :h]], axis=-1)

        def _attention(x, wq, wk, wv, wo, cos, sin, causal_bias):
            b, s, _ = x.shape
            q = (x @ wq).reshape(b, s, NH, HD).transpose(0, 2, 1, 3)
            k = (x @ wk).reshape(b, s, NKV, HD).transpose(0, 2, 1, 3)
            v = (x @ wv).reshape(b, s, NKV, HD).transpose(0, 2, 1, 3)
            c = cos[None, None]
            sn = sin[None, None]
            q = q * c + _rot_half(q) * sn
            k = k * c + _rot_half(k) * sn
            rep = NH // NKV
            k = jnp.repeat(k, rep, axis=1)
            v = jnp.repeat(v, rep, axis=1)
            scores = jnp.einsum('bhqd,bhkd->bhqk', q, k) / jnp.sqrt(jnp.asarray(HD, x.dtype))
            scores = scores + causal_bias
            attn = jax.nn.softmax(scores, axis=-1)
            out = jnp.einsum('bhqk,bhkd->bhqd', attn, v)
            out = out.transpose(0, 2, 1, 3).reshape(b, s, NH * HD)
            return out @ wo

        def _moe(x, wr, wg, wu, wd):
            logits = x @ wr
            probs = jax.nn.softmax(logits, axis=-1)
            topv, topi = jax.lax.top_k(probs, K)
            topv = topv / jnp.sum(topv, axis=-1, keepdims=True)
            comb = jnp.sum(jax.nn.one_hot(topi, E, dtype=x.dtype) * topv[..., None], axis=-2)
            out = jnp.zeros_like(x)
            for e in range(E):
                h = jax.nn.silu(x @ wg[e]) * (x @ wu[e])
                out = out + comb[..., e:e + 1] * (h @ wd[e])
            return out
        s = hidden_states.shape[1]
        cos, sin = _rope_cos_sin(s, HD, THETA)
        causal_bias = jnp.where(jnp.tril(jnp.ones((s, s), bool))[None, None], 0.0, -1000000000.0).astype(hidden_states.dtype)
        x = hidden_states
        for l in range(L):
            res = x
            h = _rms(x, ln1_w[l])
            h = _attention(h, wq[l], wk[l], wv[l], wo[l], cos, sin, causal_bias)
            x = jnp.clip(res + h, -100.0, 100.0)
            res = x
            h = _rms(x, ln2_w[l])
            h = _moe(h, wr[l], wg[l], wu[l], wd[l])
            x = jnp.clip(res + h, -100.0, 100.0)
        return x

    def _L1_attn_ref(X, ln1_w, ln1_b, ln2_w, ln2_b, WQ, WK, WV, gn_w, gn_b, WG, WO, ffn_w1, ffn_b1, ffn_w2, ffn_b2):
        import jax, jax.numpy as jnp
        import numpy as np
        L, H, D_MODEL, FFN = (2, 8, 128, 512)
        HD = D_MODEL // H
        SCALE_BASE = 64
        EPS = 1e-05

        def _layernorm(x, w, b):
            mu = x.mean(-1, keepdims=True)
            var = ((x - mu) ** 2).mean(-1, keepdims=True)
            return (x - mu) * jax.lax.rsqrt(var + EPS) * w + b

        def _groupnorm(y, w, b):
            B, S, _ = y.shape
            yg = y.reshape(B, S, H, HD)
            mu = yg.mean(-1, keepdims=True)
            var = ((yg - mu) ** 2).mean(-1, keepdims=True)
            yn = ((yg - mu) * jax.lax.rsqrt(var + EPS)).reshape(B, S, H * HD)
            return yn * w + b

        def _xpos_tables(S):
            scale_vec = (np.arange(0, HD, 2) + 0.4 * HD) / (1.4 * HD)
            power = (np.arange(S, dtype=np.float64) / SCALE_BASE)[:, None]
            scale = scale_vec[None, :] ** power
            half = HD // 2
            inv_freq = 1.0 / 10000.0 ** (np.arange(half, dtype=np.float64) / half)
            ang = np.arange(S, dtype=np.float64)[:, None] * inv_freq[None, :]
            sin, cos = (np.sin(ang), np.cos(ang))
            dup = lambda m: jnp.asarray(np.repeat(m, 2, axis=-1).astype(np.float32))
            return (dup(sin * scale), dup(cos * scale), dup(sin / scale), dup(cos / scale))

        def _rotate_every_two(x):
            x1, x2 = (x[..., ::2], x[..., 1::2])
            return jnp.stack((-x2, x1), axis=-1).reshape(x.shape)

        def _decay_mask(S):
            gammas = 1.0 - np.exp(np.linspace(np.log(1.0 / 32), np.log(1.0 / 64), H))
            n = np.arange(S)[:, None]
            m = np.arange(S)[None, :]
            diff = (n - m).astype(np.float64)
            D = np.where(n >= m, gammas[:, None, None] ** diff[None], 0.0)
            return jnp.asarray(D.astype(np.float32))
        B, S, _ = X.shape
        sinq, cosq, sink, cosk = _xpos_tables(S)
        Dm = _decay_mask(S)
        for i in range(L):
            Xn = _layernorm(X, ln1_w[i], ln1_b[i])
            Q = jnp.einsum('bsd,hdk->bhsk', Xn, WQ[i])
            K = jnp.einsum('bsd,hdk->bhsk', Xn, WK[i])
            V = jnp.einsum('bsd,hdk->bhsk', Xn, WV[i])
            Q = Q * cosq + _rotate_every_two(Q) * sinq
            K = K * cosk + _rotate_every_two(K) * sink
            scores = jnp.einsum('bhsk,bhtk->bhst', Q, K) * Dm[None]
            Yh = jnp.einsum('bhst,bhtk->bhsk', scores, V)
            Y = Yh.transpose(0, 2, 1, 3).reshape(B, S, H * HD)
            Y = _groupnorm(Y, gn_w[i], gn_b[i])
            G = jax.nn.silu(Xn @ WG[i])
            Y = G * Y @ WO[i] + X
            Yn = _layernorm(Y, ln2_w[i], ln2_b[i])
            X = jax.nn.silu(Yn @ ffn_w1[i] + ffn_b1[i]) @ ffn_w2[i] + ffn_b2[i] + Y
        return X

    def _L1_ffn_ref(hidden_states, W_A, W_B, W_up, W_down):
        import jax, jax.numpy as jnp
        import numpy as np
        E, K, H, F, R = (8, 2, 128, 256, 64)
        B, S = (2, 256)
        orig_shape = hidden_states.shape
        x = hidden_states.reshape(-1, orig_shape[-1])
        num_experts = W_A.shape[0]
        gate_hidden = jnp.einsum('nh,erh->ner', x, W_A)
        scores = jnp.sqrt(jnp.sum(gate_hidden * gate_hidden, axis=-1))
        topk_scores, topk_idx = jax.lax.top_k(scores, K)
        topk_w = jax.nn.softmax(topk_scores, axis=-1)
        w_full = jnp.sum(jax.nn.one_hot(topk_idx, num_experts, dtype=topk_w.dtype) * topk_w[..., None], axis=1)
        g = jnp.einsum('ner,efr->nef', gate_hidden, W_B)
        up = jnp.einsum('nh,efh->nef', x, W_up)
        y = jnp.einsum('nef,ehf->neh', jax.nn.silu(g) * up, W_down)
        out = jnp.einsum('neh,ne->nh', y, w_full)
        return out.reshape(orig_shape)

    def _L2_attn_ref(x, Wq, Wk, Wv, Wo, q_gamma, q_beta, k_gamma, k_beta):
        import jax, jax.numpy as jnp
        import numpy as np
        D_MODEL, N_HEADS, D_HEAD = (128, 16, 64)
        QKV = N_HEADS * D_HEAD
        EPS = 1e-05

        def _layernorm(x, gamma, beta):
            mu = jnp.mean(x, axis=-1, keepdims=True)
            var = jnp.mean((x - mu) ** 2, axis=-1, keepdims=True)
            return (x - mu) * jax.lax.rsqrt(var + EPS) * gamma + beta
        B, T, _ = x.shape

        def split_heads(y):
            return y.reshape(B, T, N_HEADS, D_HEAD).transpose(0, 2, 1, 3)
        q = split_heads(x @ Wq.T)
        k = split_heads(x @ Wk.T)
        v = split_heads(x @ Wv.T)
        q = _layernorm(q, q_gamma, q_beta)
        k = _layernorm(k, k_gamma, k_beta)
        kv = k[..., :, None] * v[..., None, :]
        S = jnp.cumsum(kv, axis=2)
        o = jnp.einsum('bhtd,bhtde->bhte', q, S)
        o = o.transpose(0, 2, 1, 3).reshape(B, T, QKV)
        return o @ Wo.T

    def _L2_ffn_ref(x, Wq, Wk, Wv, Wo, bo, Wr, We1, be1, We2, be2, ln1_g, ln1_b, ln2_g, ln2_b):
        import jax, jax.numpy as jnp
        import numpy as np
        B, S, D, H, F, E = (2, 128, 128, 16, 512, 8)
        HD = D // H
        EPS = 1e-06

        def _layernorm(x, g, b):
            m = jnp.mean(x, axis=-1, keepdims=True)
            v = jnp.var(x, axis=-1, keepdims=True)
            return (x - m) / jnp.sqrt(v + EPS) * g + b
        b, s, d = x.shape

        def split_heads(t):
            return t.reshape(b, s, H, HD).transpose(0, 2, 1, 3)
        q = split_heads(x @ Wq)
        k = split_heads(x @ Wk)
        v = split_heads(x @ Wv)
        scores = jnp.einsum('bhqd,bhkd->bhqk', q, k) / jnp.sqrt(jnp.float32(HD))
        attn_w = jax.nn.softmax(scores, axis=-1)
        ctx = jnp.einsum('bhqk,bhkd->bhqd', attn_w, v)
        ctx = ctx.transpose(0, 2, 1, 3).reshape(b, s, d)
        attn_out = ctx @ Wo + bo
        out1 = _layernorm(x + attn_out, ln1_g, ln1_b)
        router_probs = jax.nn.softmax(out1 @ Wr, axis=-1)
        top_g, top_i = jax.lax.top_k(router_probs, 2)
        top_g = jax.nn.softmax(top_g, axis=-1)
        acc = jnp.zeros_like(out1)
        for e in range(E):
            sel = top_i == e
            msk = jnp.any(sel, axis=-1)[..., None].astype(out1.dtype)
            h = jax.nn.gelu(out1 * msk @ We1[e] + be1[e], approximate=False)
            o = h @ We2[e] + be2[e]
            gate = jnp.sum(top_g * sel.astype(top_g.dtype), axis=-1, keepdims=True)
            acc = acc + o * gate
        return _layernorm(out1 + acc, ln2_g, ln2_b)

    def _L3_attn_ref(x, w_qkv, w_o):
        import jax, jax.numpy as jnp
        import numpy as np
        HIDDEN = 128
        HEADS = 16
        BATCH = 2
        SEQ = 256
        b, s, hid = x.shape
        heads = HEADS
        d = hid // heads
        qkv = x @ w_qkv.T * hid ** (-0.5)
        qkv = qkv.reshape(b, s, 3, heads, d)
        q = jnp.transpose(qkv[:, :, 0], (0, 2, 1, 3))
        k = jnp.transpose(qkv[:, :, 1], (0, 2, 1, 3))
        v = jnp.transpose(qkv[:, :, 2], (0, 2, 1, 3))
        scores = jnp.einsum('bhqd,bhkd->bhqk', q, k) * d ** (-0.5)
        attn = jax.nn.softmax(scores, axis=-1) * (s / np.sqrt(s - 1.0))
        out = jnp.einsum('bhqk,bhkd->bhqd', attn, v) * s ** (-0.5)
        out = jnp.transpose(out, (0, 2, 1, 3)).reshape(b, s, hid)
        return out @ w_o.T * hid ** (-0.5)

    def _L3_ffn_ref(x, weights, scale, bias):
        import jax, jax.numpy as jnp
        import numpy as np
        MAX_VAL = 100.0
        w = (weights >= 0.0).astype(x.dtype) * 2.0 - 1.0
        y = jnp.einsum('bsi,oi->bso', x, w)
        y = y * scale + bias
        y = jnp.clip(y, -MAX_VAL, MAX_VAL)
        return y
    x = L0_attn_x
    x = _layernorm(x + _L0_attn_ref(x, L0_attn_w_qkv, L0_attn_w_out, L0_attn_b_out), axis=-1)
    x = _layernorm(x + _L0_ffn_ref(x, L0_ffn_ln1_w, L0_ffn_ln2_w, L0_ffn_wq, L0_ffn_wk, L0_ffn_wv, L0_ffn_wo, L0_ffn_wr, L0_ffn_wg, L0_ffn_wu, L0_ffn_wd), axis=-1)
    x = _layernorm(x + _L1_attn_ref(x, L1_attn_ln1_w, L1_attn_ln1_b, L1_attn_ln2_w, L1_attn_ln2_b, L1_attn_WQ, L1_attn_WK, L1_attn_WV, L1_attn_gn_w, L1_attn_gn_b, L1_attn_WG, L1_attn_WO, L1_attn_ffn_w1, L1_attn_ffn_b1, L1_attn_ffn_w2, L1_attn_ffn_b2), axis=-1)
    x = _layernorm(x + _L1_ffn_ref(x, L1_ffn_W_A, L1_ffn_W_B, L1_ffn_W_up, L1_ffn_W_down), axis=-1)
    x = _layernorm(x + _L2_attn_ref(x, L2_attn_Wq, L2_attn_Wk, L2_attn_Wv, L2_attn_Wo, L2_attn_q_gamma, L2_attn_q_beta, L2_attn_k_gamma, L2_attn_k_beta), axis=-1)
    x = _layernorm(x + _L2_ffn_ref(x, L2_ffn_Wq, L2_ffn_Wk, L2_ffn_Wv, L2_ffn_Wo, L2_ffn_bo, L2_ffn_Wr, L2_ffn_We1, L2_ffn_be1, L2_ffn_We2, L2_ffn_be2, L2_ffn_ln1_g, L2_ffn_ln1_b, L2_ffn_ln2_g, L2_ffn_ln2_b), axis=-1)
    x = _layernorm(x + _L3_attn_ref(x, L3_attn_w_qkv, L3_attn_w_o), axis=-1)
    x = _layernorm(x + _L3_ffn_ref(x, L3_ffn_weights, L3_ffn_scale, L3_ffn_bias), axis=-1)
    return x

_drawn_inputs = setup_inputs


def setup_inputs(seed=0):
    import zlib

    import numpy as np

    out = dict(_drawn_inputs(seed))
    spreads = {'L0_ffn_ln1_w': (1.0, 0.6),
     'L0_ffn_ln2_w': (1.0, 0.6),
     'L1_attn_ln1_w': (1.0, 0.6),
     'L1_attn_ln1_b': (0.0, 0.8),
     'L1_attn_ln2_w': (1.0, 0.2),
     'L1_attn_ln2_b': (0.0, 0.1),
     'L1_attn_gn_w': (1.0, 0.6),
     'L1_attn_gn_b': (0.0, 0.8),
     'L1_attn_ffn_b1': (0.0, 0.1),
     'L1_attn_ffn_b2': (0.0, 0.1),
     'L2_attn_q_gamma': (1.0, 0.2),
     'L2_attn_q_beta': (0.0, 0.1),
     'L2_attn_k_gamma': (1.0, 0.2),
     'L2_attn_k_beta': (0.0, 0.1),
     'L2_ffn_bo': (0.0, 0.1),
     'L2_ffn_be1': (0.0, 0.8),
     'L2_ffn_be2': (0.0, 0.1),
     'L2_ffn_ln1_g': (1.0, 0.2),
     'L2_ffn_ln1_b': (0.0, 0.1),
     'L2_ffn_ln2_g': (1.0, 0.2),
     'L2_ffn_ln2_b': (0.0, 0.1),
     'L3_ffn_scale': (1.0, 0.2)}
    factors = {'L0_ffn_wq': 8.0,
     'L0_ffn_wk': 8.0,
     'L0_ffn_wr': 7.271,
     'L0_ffn_wg': 6.36,
     'L0_ffn_wu': 6.296,
     'L0_ffn_wd': 6.202,
     'L1_attn_WQ': 8.0,
     'L1_attn_WK': 8.0,
     'L1_attn_WV': 8.0,
     'L1_attn_WG': 8.0,
     'L1_attn_WO': 8.0,
     'L1_ffn_W_A': 8.0,
     'L1_ffn_W_B': 8.0,
     'L1_ffn_W_up': 8.0,
     'L1_ffn_W_down': 8.0,
     'L2_ffn_Wq': 8.0,
     'L2_ffn_Wk': 8.0,
     'L2_ffn_Wv': 8.0,
     'L2_ffn_Wo': 7.912,
     'L2_ffn_We1': 2.982}
    for name, (base, spread) in spreads.items():
        noise = np.random.default_rng([zlib.crc32(name.encode()), seed]).standard_normal(out[name].shape)
        drawn = base * np.exp(spread * noise) if base else spread * noise
        out[name] = jnp.asarray(drawn.astype(out[name].dtype))
    for name, factor in factors.items():
        out[name] = (out[name] * factor).astype(out[name].dtype)
    return out
```

```python
import numpy as np
import concourse.bass as bass
from concourse import mybir
from contextlib import ExitStack, contextmanager, nullcontext

F32 = mybir.dt.float32
BF16 = mybir.dt.bfloat16
ACT = mybir.ActivationFunctionType
ALU = mybir.AluOpType
AX = mybir.AxisListType

B, S, D = 4, 512, 128
T = B * S
CH = 512
NC = T // CH
P = 128
L0_LAYERS, L1_LAYERS = 4, 2


class Memory:
    pass


@contextmanager
def stage(nc, names):
    with ExitStack() as held:
        sems = {n: held.enter_context(nc.semaphore(n)) for n in names.split()}
        with nc.Block() as block:
            yield block, sems
        for sem in sems.values():
            nc.gpsimd.sem_clear(sem)
        nc.all_engine_barrier()


class Chain:

    def __init__(self, eng, sem, per_round=0, round_=0):
        self.eng, self.sem, self.n, self.base = eng, sem, 0, round_ * per_round
        self.per_round = per_round

    def add(self, ins):
        ins.then_inc(self.sem, 1)
        self.n += 1
        return self.n

    def wait(self, n=None):
        self.eng.wait_ge(self.sem, self.base + (self.n if n is None else n))

    def link(self, ins):
        self.add(ins)
        self.wait()

    def close(self):
        assert self.n == self.per_round, (self.n, self.per_round)


def load_columns(nc, pairs):
    with stage(nc, "loaded") as (block, s):
        @block.sync
        def _(sp):
            for out, src in pairs:
                sp.dma_start(out, src).then_inc(s["loaded"], 16)
            sp.wait_ge(s["loaded"], 16 * len(pairs))


def norm_stage(nc, m, src, dst, eps, rms=False, weight=None, bias=None, clip=None,
               residual=None, add=None):
    pre = clip or residual is not None or add is not None
    xc, sq, rstd = m.tmp1, m.tmp2, m.tmp3
    mean_bank, var_bank = (lambda c: m.psum[:, c, :]), (lambda c: m.psum[:, 4 + c, :])
    col = lambda t, c: t[:, c * CH:(c + 1) * CH]
    with stage(nc, "clipped mean_ready centred squared var_ready log_ready rstd_ready v_step") as (block, s):
        @block.tensor
        def _(pe):
            if not rms:
                for c in range(NC):
                    if pre:
                        pe.wait_ge(s["clipped"], c + 1)
                    nc.tensor.matmul(mean_bank(c), m.mean_w[:], col(src, c), start=True, stop=True)\
                        .then_inc(s["mean_ready"], 1)
            for c in range(NC):
                pe.wait_ge(s["squared"], c + 1)
                nc.tensor.matmul(var_bank(c), m.mean_w[:], col(sq, c), start=True, stop=True)\
                    .then_inc(s["var_ready"], 1)

        @block.scalar
        def _(act):
            for c in range(NC):
                if rms and clip:
                    act.wait_ge(s["clipped"], c + 1)
                elif not rms:
                    act.wait_ge(s["centred"], c + 1)
                nc.scalar.activation(col(sq, c), col(src if rms else xc, c), ACT.Square).then_inc(s["squared"], 1)
            for c in range(NC):
                act.wait_ge(s["var_ready"], c + 1)
                nc.scalar.activation(col(rstd, c), var_bank(c), ACT.Ln, bias=m.eps[eps]).then_inc(s["log_ready"], 1)
                act.wait_ge(s["log_ready"], c + 1)
                nc.scalar.activation(col(rstd, c), col(rstd, c), ACT.Exp, scale=-0.5).then_inc(s["rstd_ready"], 1)

        @block.vector
        def _(dve):
            step = Chain(dve, s["v_step"])
            if pre:
                for c in range(NC):
                    if clip:
                        last = nc.vector.tensor_scalar(col(src, c), col(src, c), clip, -clip, ALU.min, ALU.max)
                    if clip and residual is not None:
                        step.link(last)
                    if residual is not None:
                        last = nc.vector.tensor_tensor(col(src, c), col(src, c), col(residual, c), ALU.add)
                    if add is not None:
                        last = nc.vector.tensor_scalar(col(src, c), col(src, c), add, None, ALU.add)
                    last.then_inc(s["clipped"], 1)
            for c in range(NC):
                if not rms:
                    dve.wait_ge(s["mean_ready"], c + 1)
                    nc.vector.tensor_tensor(col(xc, c), col(src, c), mean_bank(c), ALU.subtract)\
                        .then_inc(s["centred"], 1)
            if pre:
                dve.wait_ge(s["clipped"], NC)
            if not rms:
                dve.wait_ge(s["centred"], NC)
            for c in range(NC):
                dve.wait_ge(s["rstd_ready"], c + 1)
                if rms:
                    nc.vector.scalar_tensor_tensor(col(dst, c), col(src, c), weight, col(rstd, c), ALU.mult, ALU.mult)
                elif weight is None:
                    nc.vector.tensor_tensor(col(dst, c), col(xc, c), col(rstd, c), ALU.mult)
                else:
                    step.link(nc.vector.tensor_tensor(col(rstd, c), col(xc, c), col(rstd, c), ALU.mult))
                    nc.vector.tensor_scalar(col(dst, c), col(rstd, c), weight, bias, ALU.mult, ALU.add)


def linear_attention_stage(nc, m, a):
    H, HD = 16, 8
    NT = S // P
    w, wo, bo = m.big[:, 0:384], m.big[:, 384:512], m.cols[:, 0:1]
    q = m.tmp1[:, 0:CH]
    qe = m.tmp1[:, CH:2 * CH]
    kv = m.tmp2[:].rearrange("p (t n) -> p t n", t=8)
    ke = m.tmp3[:, 0:CH].rearrange("p (t n) -> p t n", t=NT)
    kvm = m.tmp3[:, 512:640]
    ksm = m.tmp3[:, 640:768]
    rden = m.tmp3[:, 1024:1536]
    o = m.tmp3[:, 1536:2048]
    load_columns(nc, [(w, a["l0a_wqkv"]), (wo, a["l0a_wout"]), (bo, a["l0a_bout"])])
    with stage(nc, "q_ps kv_ps q_min q_exp k_min k_exp q_done k_done v_step sums_ps sums_done "
                   "num_ps o_done y_ps y_done") as (block, s):
        @block.tensor
        def _(pe):
            for b in range(B):
                x = m.x[:, b * CH:(b + 1) * CH]
                if b:
                    pe.wait_ge(s["q_done"], b)
                nc.tensor.matmul(m.psum[:, 0, :], w[:, 0:128], x, start=True, stop=True).then_inc(s["q_ps"], 1)
                if b:
                    pe.wait_ge(s["k_done"], b)
                for t in range(NT):
                    last = nc.tensor.matmul(m.psum[:, 1 + t // 2, (t % 2) * 256:(t % 2) * 256 + 256],
                                            x[:, t * P:(t + 1) * P], w[:, 128:384], start=True, stop=True)
                last.then_inc(s["kv_ps"], 1)
                pe.wait_ge(s["k_done"], b + 1)
                for t in range(NT):
                    nc.tensor.matmul(m.psum[:, 3, 0:128], kv[:, t, 0:128], kv[:, t, 128:256],
                                     start=t == 0, stop=t == NT - 1)
                for t in range(NT):
                    last = nc.tensor.matmul(m.psum[:, 4, 0:128], kv[:, t, 0:128], m.ones[:],
                                            start=t == 0, stop=t == NT - 1)
                last.then_inc(s["sums_ps"], 1)
                pe.wait_ge(s["sums_done"], b + 1)
                pe.wait_ge(s["q_done"], b + 1)
                nc.tensor.matmul(m.psum[:, 5, :], ksm, q, start=True, stop=True)
                nc.tensor.matmul(m.psum[:, 6, :], kvm, q, start=True, stop=True).then_inc(s["num_ps"], 1)
                pe.wait_ge(s["o_done"], b + 1)
                nc.tensor.matmul(m.psum[:, 7, :], wo, o, start=True, stop=True).then_inc(s["y_ps"], 1)

        @block.scalar
        def _(act):
            for b in range(B):
                act.wait_ge(s["q_min"], b + 1)
                nc.scalar.activation(qe, qe, ACT.Exp).then_inc(s["q_exp"], 1)
                act.wait_ge(s["k_min"], b + 1)
                nc.scalar.activation(ke, ke, ACT.Exp).then_inc(s["k_exp"], 1)

        @block.vector
        def _(dve):
            step = Chain(dve, s["v_step"])
            kps = m.psum[:, 1:3, :].rearrange("p g (t n) -> p (g t) n", t=2)
            for b in range(B):
                dve.wait_ge(s["q_ps"], b + 1)
                if b:
                    dve.wait_ge(s["num_ps"], b)
                nc.vector.tensor_scalar(qe, m.psum[:, 0, :], 0.0, None, ALU.min).then_inc(s["q_min"], 1)
                dve.wait_ge(s["kv_ps"], b + 1)
                nc.vector.tensor_scalar(ke, kps[:, :, 0:128], 0.0, None, ALU.min).then_inc(s["k_min"], 1)
                nc.vector.tensor_copy(kv[:, 0:NT, 128:256], kps[:, :, 128:256])
                dve.wait_ge(s["q_exp"], b + 1)
                nc.vector.scalar_tensor_tensor(q, m.psum[:, 0, :], 0.0, qe, ALU.max, ALU.add).then_inc(s["q_done"], 1)
                dve.wait_ge(s["k_exp"], b + 1)
                nc.vector.scalar_tensor_tensor(kv[:, 0:NT, 0:128], kps[:, :, 0:128], 0.0, ke, ALU.max, ALU.add)\
                    .then_inc(s["k_done"], 1)
                dve.wait_ge(s["sums_ps"], b + 1)
                nc.vector.tensor_tensor(kvm, m.psum[:, 3, 0:128], m.block8[:], ALU.mult)
                nc.vector.tensor_tensor(ksm, m.psum[:, 4, 0:128], m.block8[:], ALU.mult).then_inc(s["sums_done"], 1)
                dve.wait_ge(s["num_ps"], b + 1)
                step.link(nc.vector.tensor_scalar(rden, m.psum[:, 5, :], 1e-6, None, ALU.add))
                step.link(nc.vector.reciprocal(rden, rden))
                if b:
                    dve.wait_ge(s["y_ps"], b)
                nc.vector.tensor_tensor(o, m.psum[:, 6, :], rden, ALU.mult).then_inc(s["o_done"], 1)
                dve.wait_ge(s["y_ps"], b + 1)
                nc.vector.scalar_tensor_tensor(m.s[:, b * CH:(b + 1) * CH], m.psum[:, 7, :], bo,
                                               m.x[:, b * CH:(b + 1) * CH], ALU.add, ALU.add)


class SoftmaxShape:

    def __init__(self, rows, stacks, causal, rope, q_scale, y_scale):
        self.rows, self.stacks, self.causal, self.rope = rows, stacks, causal, rope
        self.q_scale, self.y_scale = q_scale, y_scale
        self.per_stack = P // rows
        self.v_cols = rows if rope else P
        at = 0
        self.at = {}
        for name, width in (("k", P), ("kr", P * rope), ("q", P * stacks), ("qr", P * stacks * rope),
                            ("v", self.v_cols), ("wo", P * stacks)):
            self.at[name] = at
            at += width
        self.cols = at


GROUPS = 4
UNITS = 16


def softmax_attention_stage(nc, m, sh, weights, first_group):
    NT = S // P
    tiles = lambda u: (u % NT + 1) if sh.causal else NT
    head = lambda u: u // NT
    stack = lambda u: head(u) // sh.per_stack
    rows = lambda u: slice(head(u) % sh.per_stack * sh.rows, (head(u) % sh.per_stack + 1) * sh.rows)
    per_stack_units = sh.per_stack * NT
    PROJ = sh.stacks + 2
    V_STEPS = (1 + sh.stacks) * (1 if sh.rope else 0)
    T_BANK, O_BANK, W_BANK = 3, 5, 6
    steps = GROUPS * B
    FREE = 4
    TL, VL = 3, 4
    PROJ_AT = [8, 10, 12, 14][-PROJ:]

    def col(slot, name, k=0, width=P):
        return m.w[:, slot, sh.at[name] + k * P:sh.at[name] + k * P + width]

    hb = lambda slot: m.hb[:, slot, :]
    kT = lambda slot: m.tmp1[:, slot * CH:(slot + 1) * CH]
    qT = lambda slot, k: m.tmp2[:, (2 * slot + k) * CH:(2 * slot + k + 1) * CH]
    v = lambda slot: m.tmp1[:, 1024 + slot * CH:1024 + slot * CH + NT * sh.v_cols].rearrange("p (t n) -> p t n", t=NT)
    ropes = lambda i: m.tmp3[:, i * CH:(i + 1) * CH]
    oT = lambda k: m.tmp4[:, k * CH:(k + 1) * CH]
    pT = lambda u: m.tmp4[:, 1024 + u % 2 * CH:1024 + u % 2 * CH + tiles(u) * P]
    bank = lambda u: u % 3 if u < UNITS - 1 else 1
    s_before = lambda u: next(d for d in range(1, UNITS) if bank((u - d) % UNITS) == bank(u))
    scores_ps = lambda u: m.psum[:, bank(u), 0:tiles(u) * P]
    p = lambda u: m.p[:, u % 4, 0:tiles(u) * P]
    neg_max, row_sum, row_inv = m.small[:, 0:16], m.small[:, 16:32], m.small[:, 32:48]

    with stage(nc, "loaded0 loaded1 proj_ps proj_done s_ready max_ready exp_done inv_ready p_ready t_ready "
                   "pt_by_act pt_by_dve pv_done o_done y_ready y_done v_step") as (block, s):
        loaded = (s["loaded0"], s["loaded1"])

        def unit_of(n, j):
            return (n, j) if j < UNITS else (n + 1, j - UNITS)

        def wait_pt(eng, n, u):
            eng.wait_ge((s["pt_by_act"], s["pt_by_dve"])[u % 2], n * (UNITS // 2) + u // 2 + 1 + FREE)

        @block.sync
        def _(sp):
            def load(g, b, slot):
                sp.dma_start(m.w[:, slot, 0:sh.cols], weights[bass.ds(first_group + g, 1)].rearrange("o p n -> p (o n)"))\
                    .then_inc(loaded[slot], 16)
                sp.dma_start(hb(slot), m.h[:, bass.ds(b * CH, CH)]).then_inc(loaded[slot], 16)

            for slot in range(2):
                load(0, slot, slot)
            with sp.Fori(0, GROUPS) as g:
                for slot in range(2):
                    sp.wait_ge(s["y_ready"], 4 * g + slot + 1 + 1)
                    load(g, 2 + slot, slot)
                for slot in range(2):
                    sp.wait_ge(s["y_ready"], 4 * g + slot + 3 + 1)
                    load(g + 1, slot, slot)
            for slot in range(2):
                sp.wait_ge(loaded[slot], 32 * (2 * GROUPS + 1))

        @block.tensor
        def _(pe):
            def project(n, r, slot, k):
                if k == 0:
                    pe.wait_ge(loaded[slot], 32 * r + 32)
                    if not isinstance(n, int):
                        pe.wait_ge(s["y_done"], n)
                else:
                    pe.wait_ge(s["proj_done"], PROJ * n + k)
                if k == PROJ - 1:
                    for t in range(NT):
                        last = nc.tensor.matmul(m.psum[:, W_BANK, t * sh.v_cols:(t + 1) * sh.v_cols],
                                                hb(slot)[:, t * P:(t + 1) * P],
                                                col(slot, "v", width=sh.v_cols), start=True, stop=True)
                else:
                    a, b = ("k", 0) if k == 0 else ("q", k - 1)
                    last = nc.tensor.matmul(m.psum[:, W_BANK, :], col(slot, a, b), hb(slot), start=True, stop=True)
                    if sh.rope:
                        last = nc.tensor.matmul(m.psum[:, W_BANK + 1, :], col(slot, a + "r", b), hb(slot),
                                                start=True, stop=True)
                last.then_inc(s["proj_ps"], 1)

            def scores(n, u, slot):
                if u == 0:
                    pe.wait_ge(s["proj_done"], PROJ * n + PROJ)
                pe.wait_ge(s["exp_done"], UNITS * n + u - s_before(u) + 1 + FREE)
                out, w = scores_ps(u), tiles(u) * P
                last = nc.tensor.matmul(out, qT(slot, stack(u))[rows(u), u % NT * P:(u % NT + 1) * P],
                                        kT(slot)[rows(u), 0:w], start=True, stop=not sh.causal)
                if sh.causal:
                    last = nc.tensor.matmul(out[:, w - P:w], m.ident_bf[:], m.causal_bf[:], start=False, stop=True)
                last.then_inc(s["s_ready"], 1)

            def transposes(n, u):
                pe.wait_ge(s["p_ready"], UNITS * n + u + 1)
                pe.wait_ge((s["pt_by_act"], s["pt_by_dve"])[u % 2], n * (UNITS // 2) + u // 2 + FREE)
                for t in range(tiles(u)):
                    last = nc.tensor.transpose(m.psum[:, T_BANK + u % 2, t * P:(t + 1) * P],
                                               p(u)[:, t * P:(t + 1) * P], m.ident[:])
                last.then_inc(s["t_ready"], 1)

            def values(n, u, slot):
                if u % per_stack_units == 0:
                    pe.wait_ge(s["o_done"], sh.stacks * n + stack(u) + 1)
                wait_pt(pe, n, u)
                c = slice(0, sh.rows) if sh.rope else rows(u)
                for t in range(tiles(u)):
                    last = nc.tensor.matmul(m.psum[rows(u), O_BANK, u % NT * P:(u % NT + 1) * P],
                                            v(slot)[:, t, c], pT(u)[:, t * P:(t + 1) * P],
                                            start=t == 0, stop=t == tiles(u) - 1)
                last.then_inc(s["pv_done"], 1)

            for k in range(PROJ):
                project(0, 0, 0, k)
            for j in range(VL):
                scores(0, j, 0)
                if j >= TL:
                    transposes(0, j - TL)
            with pe.Fori(0, steps // 2) as r:
                for slot in range(2):
                    n = 2 * r + slot
                    for j in range(VL, UNITS + VL):
                        n_j, u = unit_of(n, j)
                        scores(n_j, u, slot if j < UNITS else 1 - slot)
                        transposes(*unit_of(n, j - TL))
                        values(n, j - VL, slot)
                        if j in PROJ_AT:
                            project(n + 1, r + slot, 1 - slot, PROJ_AT.index(j))
                    for k in range(sh.stacks):
                        pe.wait_ge(s["o_done"], sh.stacks * n + k + 2)
                        last = nc.tensor.matmul(m.psum[:, W_BANK, :], col(slot, "wo", k), oT(k),
                                                start=k == 0, stop=k == sh.stacks - 1)
                    last.then_inc(s["y_ready"], 1)

        @block.scalar
        def _(act):
            def exponential(n, u):
                act.wait_ge(s["max_ready"], UNITS * n + u + 1)
                act.wait_ge(s["t_ready"], UNITS * n + u - 3 + FREE)
                nc.scalar.activation(p(u), scores_ps(u), ACT.Exp,
                                     bias=neg_max[:, u:u + 1], accum_out=row_sum[:, u:u + 1])\
                    .then_inc(s["exp_done"], 1)

            def evacuate(n, u):
                act.wait_ge(s["t_ready"], UNITS * n + u + 1 + FREE)
                act.wait_ge(s["pv_done"], UNITS * n + u - 1 + FREE)
                nc.scalar.copy(pT(u), m.psum[:, T_BANK + u % 2, 0:tiles(u) * P]).then_inc(s["pt_by_act"], 1)

            act.sem_inc(s["exp_done"], FREE)
            act.sem_inc(s["pt_by_act"], FREE)
            for j in range(VL):
                exponential(0, j)
                if j >= TL and (j - TL) % 2 == 0:
                    evacuate(0, j - TL)
            with act.Fori(0, steps // 2) as r:
                for slot in range(2):
                    n = 2 * r + slot
                    for j in range(VL, UNITS + VL):
                        exponential(*unit_of(n, j))
                        if (j - TL) % 2 == 0:
                            evacuate(*unit_of(n, j - TL))

        @block.gpsimd
        def _(pool):
            def normalise(n, u):
                pool.wait_ge(s["inv_ready"], UNITS * n + u + 1)
                nc.gpsimd.tensor_tensor(p(u), p(u), row_inv[:, u:u + 1].to_broadcast([P, tiles(u) * P]), ALU.mult)\
                    .then_inc(s["p_ready"], 1)

            for j in range(VL - 1):
                normalise(0, j)
            with pool.Fori(0, steps // 2) as r:
                for slot in range(2):
                    for j in range(VL - 1, UNITS + VL - 1):
                        normalise(*unit_of(2 * r + slot, j))

        @block.vector
        def _(dve):
            w0, w1 = m.psum[:, W_BANK, :], m.psum[:, W_BANK + 1, :]

            def projected(n, slot, k, chain):
                dve.wait_ge(s["proj_ps"], PROJ * n + k + 1)
                if k == PROJ - 1:
                    last = nc.vector.tensor_copy(v(slot), w0[:, 0:NT * sh.v_cols].rearrange("p (t n) -> p t n", t=NT))
                elif sh.rope:
                    out, tab = (kT(slot), 0) if k == 0 else (qT(slot, k - 1), 2)
                    nc.vector.tensor_tensor(out, w0, ropes(tab), ALU.mult)
                    chain.link(nc.vector.tensor_tensor(m.rot[:], w1, ropes(tab + 1), ALU.mult))
                    last = nc.vector.tensor_tensor(out, out, m.rot[:], ALU.add)
                elif k == 0:
                    last = nc.vector.tensor_copy(kT(slot), w0)
                else:
                    last = nc.vector.tensor_scalar(qT(slot, k - 1), w0, sh.q_scale, None, ALU.mult)
                last.then_inc(s["proj_done"], 1)

            def maximum(n, u):
                dve.wait_ge(s["s_ready"], UNITS * n + u + 1)
                nc.vector.tensor_reduce(neg_max[:, u:u + 1], scores_ps(u), AX.X, ALU.max, negate=True)\
                    .then_inc(s["max_ready"], 1)

            def inverse(n, u):
                dve.wait_ge(s["exp_done"], UNITS * n + u + 1 + FREE)
                nc.vector.reciprocal(row_inv[:, u:u + 1], row_sum[:, u:u + 1]).then_inc(s["inv_ready"], 1)

            def evacuate(n, u):
                dve.wait_ge(s["t_ready"], UNITS * n + u + 1 + FREE)
                dve.wait_ge(s["pv_done"], UNITS * n + u - 1 + FREE)
                nc.vector.tensor_copy(pT(u), m.psum[:, T_BANK + u % 2, 0:tiles(u) * P]).then_inc(s["pt_by_dve"], 1)

            def step(r, slot, b):
                n = 2 * r + slot
                chain = Chain(dve, s["v_step"], V_STEPS, n + 1)
                for j in range(VL, UNITS + VL):
                    maximum(*unit_of(n, j))
                    inverse(*unit_of(n, j - 1))
                    if (j - TL) % 2 == 1:
                        evacuate(*unit_of(n, j - TL))
                    if j - 1 in PROJ_AT:
                        projected(n + 1, 1 - slot, PROJ_AT.index(j - 1), chain)
                    last = j == UNITS + VL - 1
                    if (j - VL) % per_stack_units == 0 and j > VL or last:
                        u = UNITS - 1 if last else j - VL - 1
                        dve.wait_ge(s["pv_done"], UNITS * n + u + 1 + FREE)
                        if stack(u) == 0:
                            dve.wait_ge(s["y_ready"], n + 1)
                        nc.vector.tensor_copy(oT(stack(u)), m.psum[:, O_BANK, :]).then_inc(s["o_done"], 1)
                dve.wait_ge(s["y_ready"], n + 1 + 1)
                xb = m.x[:, bass.ds(b * CH, CH)]
                nc.vector.scalar_tensor_tensor(xb, w0, sh.y_scale, xb, ALU.mult, ALU.add).then_inc(s["y_done"], 1)
                dve.wait_ge(s["y_done"], n + 2)
                chain.close()

            for name, credit in (("o_done", 1), ("y_done", 1), ("y_ready", 1), ("t_ready", FREE), ("pv_done", FREE),
                                 ("pt_by_dve", FREE)):
                dve.sem_inc(s[name], credit)
            chain = Chain(dve, s["v_step"], V_STEPS)
            for k in range(PROJ):
                projected(0, 0, k, chain)
            chain.close()
            for j in range(VL):
                maximum(0, j)
                if j:
                    inverse(0, j - 1)
                if j >= TL and (j - TL) % 2 == 1:
                    evacuate(0, j - TL)
            with dve.Fori(0, GROUPS) as g:
                for b in range(B):
                    step(2 * g + b // 2, b % 2, b)


NE, NT_ALL = 8, T // P


def router_stage(nc, m, kind, weights, scratch):
    v3 = lambda k: m.big[:, k * 128:(k + 1) * 128].rearrange("p (t e) -> p t e", e=NE)
    lg, eq, cand, oh1, oh2, l2 = (v3(k) for k in range(6))
    comb = m.big[:, 768:896]
    col = lambda k: m.small[:, 64 + 16 * k:80 + 16 * k]
    m1, m2, first, d, w1, w2, z, p1, p2 = (col(k) for k in range(9))
    over_e = lambda c: c.rearrange("p (t o) -> p t o", o=1).to_broadcast([P, NT_ALL, NE])
    iota = m.iota8.rearrange("p (o e) -> p o e", o=1).to_broadcast([P, NT_ALL, NE])
    n_w = 512 if kind == "norm" else NE
    load_columns(nc, [(m.w[:, 0, 0:n_w], weights)])
    with stage(nc, "logits squared sums root top exps probs comb comb_t comb_s stored v_step a_step") as (block, s):
        @block.tensor
        def _(pe):
            for t in range(NT_ALL):
                out = m.psum[:, 0, t * NE:(t + 1) * NE]
                if kind == "norm":
                    out = m.psum[:, t % 4, :]
                    if t >= 4:
                        pe.wait_ge(s["squared"], t - 3)
                nc.tensor.matmul(out, m.h[:, t * P:(t + 1) * P], m.w[:, 0, 0:n_w], start=True, stop=True)\
                    .then_inc(s["logits"], 1)
            pe.wait_ge(s["comb"], 1)
            nc.tensor.transpose(m.psum[:, 4, 0:128], comb, m.ident[:]).then_inc(s["comb_t"], 1)

        @block.scalar
        def _(act):
            if kind == "norm":
                for t in range(NT_ALL):
                    act.wait_ge(s["logits"], t + 1)
                    if t >= 4:
                        act.wait_ge(s["sums"], t - 3)
                    nc.scalar.activation(m.tmp1[:, t % 4 * CH:t % 4 * CH + CH], m.psum[:, t % 4, :], ACT.Square)\
                        .then_inc(s["squared"], 1)
                act.wait_ge(s["sums"], NT_ALL)
                nc.scalar.activation(lg, lg, ACT.Sqrt).then_inc(s["root"], 1)
            act.wait_ge(s["top"], 1)
            if kind == "double":
                nc.scalar.activation(eq, eq, ACT.Exp)
            nc.scalar.activation(d, d, ACT.Exp).then_inc(s["exps"], 1)
            if kind == "double":
                act.wait_ge(s["probs"], 1)
                nc.scalar.activation(d, d, ACT.Exp).then_inc(s["exps"], 1)

        @block.vector
        def _(dve):
            link = Chain(dve, s["v_step"]).link
            if kind == "norm":
                for t in range(NT_ALL):
                    dve.wait_ge(s["squared"], t + 1)
                    sq = m.tmp1[:, t % 4 * CH:t % 4 * CH + CH].rearrange("p (e r) -> p e r", e=NE)
                    nc.vector.tensor_reduce(lg[:, t, :], sq, AX.X, ALU.add).then_inc(s["sums"], 1)
                dve.wait_ge(s["root"], 1)
            else:
                dve.wait_ge(s["logits"], NT_ALL)
                link(nc.vector.tensor_copy(lg, m.psum[:, 0, 0:128].rearrange("p (t e) -> p t e", e=NE)))

            def best(src, largest, onehot):
                link(nc.vector.tensor_reduce(largest, src, AX.X, ALU.max))
                link(nc.vector.tensor_tensor(eq, src, over_e(largest), ALU.is_ge))
                link(nc.vector.tensor_tensor(cand, eq, iota, ALU.mult))
                link(nc.vector.tensor_reduce(first, cand, AX.X, ALU.min))
                link(nc.vector.tensor_tensor(onehot, cand, over_e(first), ALU.is_equal))

            best(lg, m1, oh1)
            link(nc.vector.scalar_tensor_tensor(l2, oh1, -1e30, lg, ALU.mult, ALU.add))
            best(l2, m2, oh2)
            if kind == "double":
                link(nc.vector.tensor_tensor(eq, lg, over_e(m1), ALU.subtract))
            link(nc.vector.tensor_tensor(d, m2, m1, ALU.subtract))
            dve.sem_inc(s["top"], 1)
            dve.wait_ge(s["exps"], 1)
            if kind == "double":
                link(nc.vector.tensor_reduce(z, eq, AX.X, ALU.add))
                link(nc.vector.reciprocal(p1, z))
                link(nc.vector.tensor_tensor(p2, d, p1, ALU.mult))
                link(nc.vector.tensor_tensor(d, p2, p1, ALU.subtract))
                dve.sem_inc(s["probs"], 1)
                dve.wait_ge(s["exps"], 2)
            link(nc.vector.tensor_scalar(w1, d, 1.0, None, ALU.add))
            link(nc.vector.reciprocal(w1, w1))
            link(nc.vector.tensor_tensor(w2, d, w1, ALU.mult))
            link(nc.vector.tensor_tensor(oh1, oh1, over_e(w1), ALU.mult))
            link(nc.vector.tensor_tensor(oh2, oh2, over_e(w2), ALU.mult))
            nc.vector.tensor_tensor(comb.rearrange("p (e t) -> p t e", e=NE), oh1, oh2, ALU.add).then_inc(s["comb"], 1)
            dve.wait_ge(s["comb_t"], 1)
            nc.vector.tensor_copy(m.big[:, 896:1024], m.psum[:, 4, 0:128]).then_inc(s["comb_s"], 1)

        @block.sync
        def _(sp):
            sp.wait_ge(s["comb_s"], 1)
            sp.dma_start(scratch.rearrange("e (t k) -> (e t) k", k=P), m.big[:, 896:1024]).then_inc(s["stored"], 16)
            sp.wait_ge(s["stored"], 16)


class ExpertShape:

    def __init__(self, kind):
        self.kind = kind
        self.tiles = {"gated": 2, "lowrank": 2, "gelu": 4, "ffn": 4}[kind]
        wide = self.tiles * P
        parts = {"gated": (("g", wide), ("u", wide), ("d", wide)),
                 "lowrank": (("a", 64), ("g", wide), ("u", wide), ("d", wide)),
                 "gelu": (("g", wide), ("d", wide), ("b1", 4), ("b2", 1))}[{"ffn": "gelu"}.get(kind, kind)]
        self.at, at = {}, 0
        for name, width in parts:
            self.at[name] = at
            at += width
        self.cols = at


def experts_stage(nc, m, sh, weights, first, scratch):
    FT, LAG = sh.tiles, 2
    U = NC * FT
    PAIRS = 2 if sh.kind == "lowrank" else 3
    gelu, low = sh.kind in ("gelu", "ffn"), sh.kind == "lowrank"
    single = sh.kind == "ffn"
    SLOTS = 1 if single else 2
    rounds = lambda eng: nullcontext(0) if single else eng.Fori(0, NE // 2)
    per_load = 16 if single else 32
    w = lambda slot, name, f=0, width=P: m.w[:, slot, sh.at[name] + f * P:sh.at[name] + f * P + width]
    h = lambda c: m.h[:, c * CH:(c + 1) * CH]
    g_bank = lambda k: m.psum[:, 2 * (k % PAIRS), :]
    u_bank = lambda k: m.psum[:, 2 * (k % PAIRS) + 1, :]
    y_bank = lambda c: m.psum[:, 6 + c % 2, :]
    low_bank = lambda c: m.psum[0:64, 4 + c % 2, :]
    low_sb = lambda c: m.tmp4[0:64, c % 2 * CH:(c % 2 + 1) * CH]
    gate_act = lambda k: m.tmp1[:, k % 3 * CH:(k % 3 + 1) * CH]
    hidden = lambda k: m.tmp2[:, k % 3 * CH:(k % 3 + 1) * CH]
    part = lambda c: m.tmp3[:, c % 2 * CH:(c % 2 + 1) * CH]
    with stage(nc, "loaded0 loaded1 low_ps low_done gu_ps act_done h_done y_mm y_done acc_done") as (block, s):
        loaded = (s["loaded0"], s["loaded1"])

        @block.sync
        def _(sp):
            def load(e, slot):
                sp.dma_start(m.w[:, slot, 0:sh.cols], weights[bass.ds(first + e, 1)].rearrange("o p n -> p (o n)"))\
                    .then_inc(loaded[slot], 16)
                if single:
                    return
                sp.dma_start(m.gates[:, slot, :], scratch[bass.ds(e, 1)].to_broadcast([P, T])).then_inc(loaded[slot], 16)

            for slot in range(SLOTS):
                load(slot, slot)
            if single:
                return
            with sp.Fori(0, NE // 2 - 1) as r:
                for slot in range(2):
                    sp.wait_ge(s["acc_done"], NC * (2 * r + slot + 1) + 1)
                    load(2 * r + 2 + slot, slot)

        @block.tensor
        def _(pe):
            with rounds(pe) as r:
                for slot in range(SLOTS):
                    e = 2 * r + slot
                    pe.wait_ge(loaded[slot], per_load * r + per_load)

                    def low_rank(c):
                        if c >= 2:
                            pe.wait_ge(s["low_done"], NC * e + c - 1)
                        nc.tensor.matmul(low_bank(c), w(slot, "a", width=64), h(c), start=True, stop=True)\
                            .then_inc(s["low_ps"], 1)

                    for k in range(U + LAG):
                        c, f = k // FT, k % FT
                        if k < U:
                            if low and f == 0:
                                if c == 0:
                                    low_rank(0)
                                if c + 1 < NC:
                                    low_rank(c + 1)
                                pe.wait_ge(s["low_done"], NC * e + c + 1)
                            if k >= PAIRS:
                                pe.wait_ge(s["h_done"], U * e + k - PAIRS + 1)
                            if low:
                                last = nc.tensor.matmul(g_bank(k), w(slot, "g", f)[0:64], low_sb(c), start=True, stop=True)
                            else:
                                last = nc.tensor.matmul(g_bank(k), w(slot, "g", f), h(c), start=True, stop=True)
                            if not gelu:
                                last = nc.tensor.matmul(u_bank(k), w(slot, "u", f), h(c), start=True, stop=True)
                            last.then_inc(s["gu_ps"], 1)
                        k -= LAG
                        if k >= 0:
                            c, f = k // FT, k % FT
                            if f == 0:
                                pe.wait_ge(s["y_done"], NC * e + max(c - 1, 0) + 1)
                            pe.wait_ge(s["h_done"], U * e + k + 1)
                            nc.tensor.matmul(y_bank(c), w(slot, "d", f), hidden(k), start=f == 0, stop=f == FT - 1)\
                                .then_inc(s["y_mm"], 1)

        @block.scalar
        def _(act):
            with rounds(act) as r:
                for slot in range(SLOTS):
                    e = 2 * r + slot
                    for k in range(U):
                        act.wait_ge(s["gu_ps"], U * e + k + 1)
                        if gelu:
                            if k >= 3:
                                act.wait_ge(s["y_mm"], U * e + k - 2)
                            nc.scalar.activation(hidden(k), g_bank(k), ACT.Silu if single else ACT.Gelu, bias=w(slot, "b1")[:, k % FT:k % FT + 1])\
                                .then_inc(s["h_done"], 1)
                        else:
                            if k >= 3:
                                act.wait_ge(s["h_done"], U * e + k - 2)
                            nc.scalar.activation(gate_act(k), g_bank(k), ACT.Silu).then_inc(s["act_done"], 1)

        @block.vector
        def _(dve):
            dve.sem_inc(s["y_done"], 1)
            dve.sem_inc(s["acc_done"], 1)
            with rounds(dve) as r:
                for slot in range(SLOTS):
                    e = 2 * r + slot

                    def low_copy(c):
                        dve.wait_ge(s["low_ps"], NC * e + c + 1)
                        if c >= 2:
                            dve.wait_ge(s["gu_ps"], U * e + (c - 1) * FT)
                        nc.vector.tensor_copy(low_sb(c), low_bank(c)).then_inc(s["low_done"], 1)

                    for k in range(U + LAG):
                        if low and k < U and k % FT == 0:
                            if k == 0:
                                low_copy(0)
                            elif k // FT >= 1:
                                low_copy(k // FT)
                        if k < U and not gelu:
                            dve.wait_ge(s["act_done"], U * e + k + 1)
                            if k >= 3:
                                dve.wait_ge(s["y_mm"], U * e + k - 2)
                            nc.vector.tensor_tensor(hidden(k), gate_act(k), u_bank(k), ALU.mult).then_inc(s["h_done"], 1)
                        j = k - LAG
                        if j >= 0 and j % FT == FT - 1:
                            c = j // FT
                            dve.wait_ge(s["y_mm"], U * e + j + 1)
                            if c >= 2:
                                dve.wait_ge(s["acc_done"], NC * e + c)
                            else:
                                dve.wait_ge(s["acc_done"], NC * e + 1)
                            gate = m.gates[:, slot, c * CH:(c + 1) * CH]
                            if single:
                                last = nc.vector.tensor_scalar(part(c), y_bank(c), w(slot, "b2", width=1), None, ALU.add)
                            elif gelu:
                                last = nc.vector.scalar_tensor_tensor(part(c), y_bank(c), w(slot, "b2", width=1), gate,
                                                                      ALU.add, ALU.mult)
                            else:
                                last = nc.vector.tensor_tensor(part(c), y_bank(c), gate, ALU.mult)
                            last.then_inc(s["y_done"], 1)

        @block.gpsimd
        def _(pool):
            with rounds(pool) as r:
                for slot in range(SLOTS):
                    e = 2 * r + slot
                    for c in range(NC):
                        pool.wait_ge(s["y_done"], NC * e + c + 2)
                        acc = m.x[:, c * CH:(c + 1) * CH]
                        nc.gpsimd.tensor_tensor(acc, acc, part(c), ALU.add).then_inc(s["acc_done"], 1)


class CausalShape:

    def __init__(self, retention):
        self.retention = retention
        self.rows = 32 if retention else 64
        self.heads = P // self.rows
        self.groups = 2 if retention else 8
        names = "q qr k kr v wg wo" if retention else "q k v wo"
        self.at = {n: i * P for i, n in enumerate(names.split())}
        self.cols = len(self.at) * P + (2 if retention else 0)


def causal_attention_stage(nc, m, sh, weights, first_group, decays=None):
    NT, HEADS, G, ret = S // P, sh.heads, sh.groups, sh.retention
    U = HEADS * NT
    width = lambda u: (NT - u % NT) * P
    rows = lambda u: slice(u // NT * sh.rows, (u // NT + 1) * sh.rows)
    BANKS, O_BANK, MEAN_BANK, VAR_BANK, W_BANK = 3, 3, 4, 5, 6
    NORMS = 1 if ret else 2
    PROJ = 3 if ret else 2
    V_STEPS = 4 if ret else 2
    steps = G * B
    per_load = 48 if ret else 32
    col = lambda slot, name: m.w[:, slot, sh.at[name]:sh.at[name] + P]
    hb = lambda slot: m.hb[:, slot, :]
    part = lambda t, i: t[:, i * CH:(i + 1) * CH]
    qT, kT = (lambda slot: part(m.tmp1, slot)), (lambda slot: part(m.tmp1, 2 + slot))
    v = lambda slot: part(m.tmp2, slot).rearrange("p (t n) -> p t n", t=NT)
    oT, gate = part(m.tmp2, 2), part(m.tmp2, 3)
    sT = lambda u: m.p[:, u % 3, 0:width(u)]
    sq, rstd = part(m.tmp3, 0), part(m.tmp3, 1)
    xpos = lambda i: part(m.tmp4, i)
    table = lambda slot, u: (m.gates[:, slot, u // NT * CH:u // NT * CH + width(u)] if ret
                             else m.tri[:, 0:width(u)])
    block_mean = m.block16 if ret else m.block64
    with stage(nc, "loaded0 loaded1 proj_ps proj_done raw_ready mean_ps centred squared var_ps log_ready rstd_ready "
                   "normed s_ready s_done pv_done o_done gate_ps gate_done y_ready y_done v_step") as (block, s):
        loaded = (s["loaded0"], s["loaded1"])

        @block.sync
        def _(sp):
            def load(g, b, slot):
                sp.dma_start(m.w[:, slot, 0:sh.cols], weights[bass.ds(first_group + g, 1)].rearrange("o p n -> p (o n)"))\
                    .then_inc(loaded[slot], 16)
                sp.dma_start(hb(slot), m.h[:, bass.ds(b * CH, CH)]).then_inc(loaded[slot], 16)
                if ret:
                    sp.dma_start(m.gates[:, slot, :], decays[bass.ds(g, 1)].rearrange("o p n -> p (o n)"))\
                        .then_inc(loaded[slot], 16)

            for slot in range(2):
                load(0, slot, slot)
            with sp.Fori(0, G) as g:
                for slot in range(2):
                    sp.wait_ge(s["y_ready"], 4 * g + slot + 1)
                    load(g, 2 + slot, slot)
                for slot in range(2):
                    sp.wait_ge(s["y_ready"], 4 * g + slot + 3)
                    load(g + 1, slot, slot)
            for slot in range(2):
                sp.wait_ge(loaded[slot], per_load * (2 * G + 1))

        @block.tensor
        def _(pe):
            def norm(n, i, raw, centred):
                pe.wait_ge(s["raw_ready"], NORMS * n + i + 1)
                nc.tensor.matmul(m.psum[:, MEAN_BANK, :], block_mean, raw, start=True, stop=True).then_inc(s["mean_ps"], 1)
                pe.wait_ge(s["squared"], NORMS * n + i + 1)
                nc.tensor.matmul(m.psum[:, VAR_BANK, :], block_mean, sq, start=True, stop=True).then_inc(s["var_ps"], 1)

            with pe.Fori(0, steps // 2) as r:
                for slot in range(2):
                    n = 2 * r + slot
                    pe.wait_ge(loaded[slot], per_load * r + per_load)
                    pe.wait_ge(s["y_done"], n + 1)
                    pairs = [("q", "qr"), ("k", "kr")] if ret else [("q", "k")]
                    for i, names in enumerate(pairs):
                        if i:
                            pe.wait_ge(s["proj_done"], PROJ * n + i)
                        for j, name in enumerate(names):
                            last = nc.tensor.matmul(m.psum[:, W_BANK + j, :], col(slot, name), hb(slot),
                                                    start=True, stop=True)
                        last.then_inc(s["proj_ps"], 1)
                    pe.wait_ge(s["proj_done"], PROJ * n + PROJ - 1)
                    for t in range(NT):
                        last = nc.tensor.matmul(m.psum[:, W_BANK, t * P:(t + 1) * P], hb(slot)[:, t * P:(t + 1) * P],
                                                col(slot, "v"), start=True, stop=True)
                    last.then_inc(s["proj_ps"], 1)
                    if ret:
                        nc.tensor.matmul(m.psum[:, W_BANK + 1, :], col(slot, "wg"), hb(slot), start=True, stop=True)\
                            .then_inc(s["gate_ps"], 1)
                    else:
                        for i, x in enumerate((qT(slot), kT(slot))):
                            norm(n, i, x, x)
                        pe.wait_ge(s["normed"], NORMS * n + NORMS)
                    pe.wait_ge(s["proj_done"], PROJ * n + PROJ)
                    pe.wait_ge(s["o_done"], n + 1)
                    for u in range(U + 2):
                        if u < U:
                            if u >= BANKS:
                                pe.wait_ge(s["s_done"], U * n + u - BANKS + 1)
                            t = u % NT
                            nc.tensor.matmul(m.psum[:, u % BANKS, 0:width(u)], kT(slot)[rows(u), t * P:(t + 1) * P],
                                             qT(slot)[rows(u), t * P:CH], start=True, stop=True).then_inc(s["s_ready"], 1)
                        w = u - 2
                        if w >= 0:
                            t = w % NT
                            pe.wait_ge(s["s_done"], U * n + w + 1)
                            nc.tensor.matmul(m.psum[rows(w), O_BANK, t * P:CH], v(slot)[:, t, rows(w)], sT(w),
                                             start=t == 0, stop=t == NT - 1).then_inc(s["pv_done"], 1)
                    if ret:
                        norm(n, 0, oT, oT)
                        pe.wait_ge(s["normed"], n + 1)
                    pe.wait_ge(s["o_done"], n + 2)
                    nc.tensor.matmul(m.psum[:, W_BANK, :], col(slot, "wo"), oT, start=True, stop=True)\
                        .then_inc(s["y_ready"], 1)

        @block.scalar
        def _(act):
            with act.Fori(0, steps // 2) as r:
                for slot in range(2):
                    n = 2 * r + slot
                    if ret:
                        act.wait_ge(s["gate_ps"], n + 1)
                        nc.scalar.activation(gate, m.psum[:, W_BANK + 1, :], ACT.Silu).then_inc(s["gate_done"], 1)
                    for i in range(NORMS):
                        x = oT if ret else (qT(slot), kT(slot))[i]
                        act.wait_ge(s["centred"], NORMS * n + i + 1)
                        nc.scalar.activation(sq, x, ACT.Square).then_inc(s["squared"], 1)
                        act.wait_ge(s["var_ps"], NORMS * n + i + 1)
                        nc.scalar.activation(rstd, m.psum[:, VAR_BANK, :], ACT.Ln, bias=m.eps5).then_inc(s["log_ready"], 1)
                        act.wait_ge(s["log_ready"], NORMS * n + i + 1)
                        nc.scalar.activation(rstd, rstd, ACT.Exp, scale=-0.5).then_inc(s["rstd_ready"], 1)
                        act.wait_ge(s["normed"], NORMS * n + i + 1)

        @block.vector
        def _(dve):
            def step(r, slot, b):
                n = 2 * r + slot
                chain = Chain(dve, s["v_step"], V_STEPS, n)
                w0, w1 = m.psum[:, W_BANK, :], m.psum[:, W_BANK + 1, :]

                def norm(i, x, weight, bias):
                    dve.wait_ge(s["mean_ps"], NORMS * n + i + 1)
                    nc.vector.tensor_tensor(x, x, m.psum[:, MEAN_BANK, :], ALU.subtract).then_inc(s["centred"], 1)
                    dve.wait_ge(s["rstd_ready"], NORMS * n + i + 1)
                    chain.link(nc.vector.tensor_tensor(x, x, rstd, ALU.mult))
                    last = nc.vector.tensor_scalar(x, x, weight, bias, ALU.mult, ALU.add)
                    if ret:
                        chain.link(last)
                        last = nc.vector.tensor_tensor(x, x, gate, ALU.mult)
                    last.then_inc(s["normed"], 1)

                dve.wait_ge(s["proj_ps"], PROJ * n + 1)
                if ret:
                    for i, out in enumerate((qT(slot), kT(slot))):
                        dve.wait_ge(s["proj_ps"], PROJ * n + i + 1)
                        nc.vector.tensor_tensor(out, w0, xpos(2 * i), ALU.mult)
                        chain.link(nc.vector.tensor_tensor(m.rot[:], w1, xpos(2 * i + 1), ALU.mult))
                        nc.vector.tensor_tensor(out, out, m.rot[:], ALU.add).then_inc(s["proj_done"], 1)
                else:
                    nc.vector.tensor_copy(qT(slot), w0).then_inc(s["raw_ready"], 1)
                    nc.vector.tensor_copy(kT(slot), w1).then_inc(s["raw_ready"], 1)
                    dve.wait_ge(s["raw_ready"], NORMS * n + 2)
                    dve.sem_inc(s["proj_done"], 1)
                dve.wait_ge(s["proj_ps"], PROJ * n + PROJ)
                nc.vector.tensor_copy(v(slot), w0.rearrange("p (t n) -> p t n", t=NT)).then_inc(s["proj_done"], 1)
                if not ret:
                    for i, x in enumerate((qT(slot), kT(slot))):
                        norm(i, x, m.cols[:, 8 + 2 * i:9 + 2 * i], m.cols[:, 9 + 2 * i:10 + 2 * i])
                for u in range(U):
                    dve.wait_ge(s["s_ready"], U * n + u + 1)
                    if u >= 3:
                        dve.wait_ge(s["pv_done"], U * n + u - 2)
                    nc.vector.tensor_tensor(sT(u), m.psum[:, u % BANKS, 0:width(u)], table(slot, u), ALU.mult)\
                        .then_inc(s["s_done"], 1)
                dve.wait_ge(s["pv_done"], U * n + U)
                o_copied = nc.vector.tensor_copy(oT, m.psum[:, O_BANK, :])
                o_copied.then_inc(s["o_done"], 1)
                if ret:
                    dve.wait_ge(s["o_done"], n + 2)
                    dve.sem_inc(s["raw_ready"], 1)
                    dve.wait_ge(s["gate_done"], n + 1)
                    norm(0, oT, m.w[:, slot, 7 * P:7 * P + 1], m.w[:, slot, 7 * P + 1:7 * P + 2])
                dve.wait_ge(s["y_ready"], n + 1)
                xb = m.x[:, bass.ds(b * CH, CH)]
                nc.vector.tensor_tensor(xb, w0, xb, ALU.add).then_inc(s["y_done"], 1)
                dve.wait_ge(s["y_done"], n + 2)
                chain.close()

            dve.sem_inc(s["o_done"], 1)
            dve.sem_inc(s["y_done"], 1)
            with dve.Fori(0, G) as g:
                for b in range(B):
                    step(2 * g + b // 2, b % 2, b)


def sign_projection_stage(nc, m, a):
    w = m.big[:, 0:128]
    y = lambda c: m.tmp1[:, c * CH:(c + 1) * CH]
    x = lambda c: m.x[:, c * CH:(c + 1) * CH]
    load_columns(nc, [(w, a["l3f_w"]), (m.cols[:, 0:2], a["l3f_scale_bias"])])
    with stage(nc, "signs y_ps v_step") as (block, s):
        @block.tensor
        def _(pe):
            pe.wait_ge(s["signs"], 1)
            for c in range(NC):
                nc.tensor.matmul(m.psum[:, c, :], w, x(c), start=True, stop=True).then_inc(s["y_ps"], 1)

        @block.vector
        def _(dve):
            link = Chain(dve, s["v_step"]).link
            link(nc.vector.tensor_scalar(w, w, 0.0, 2.0, ALU.is_ge, ALU.mult))
            link(nc.vector.tensor_scalar(w, w, -1.0, None, ALU.add))
            dve.sem_inc(s["signs"], 1)
            for c in range(NC):
                dve.wait_ge(s["y_ps"], c + 1)
                link(nc.vector.tensor_scalar(y(c), m.psum[:, c, :], m.cols[:, 0:1], m.cols[:, 1:2], ALU.mult, ALU.add))
                link(nc.vector.tensor_scalar(y(c), y(c), 100.0, -100.0, ALU.min, ALU.max))
                nc.vector.tensor_tensor(m.s[:, c * CH:(c + 1) * CH], x(c), y(c), ALU.add)


def build(nc, a, first=1, stages=99):
    with ExitStack() as held:
        def sb(name, shape, dt=F32):
            return held.enter_context(nc.sbuf_tensor(name, shape, dt))
        m = Memory()
        m.x, m.s, m.h = (sb(n, [P, T]) for n in ("x", "s", "h"))
        m.tmp1, m.tmp2, m.tmp3 = (sb(n, [P, T]) for n in ("tmp1", "tmp2", "tmp3"))
        m.tmp4 = sb("tmp4", [P, T])
        m.w = sb("w", [P, 2, 1536])
        m.hb = sb("hb", [P, 2, CH])
        m.p = sb("p", [P, 4, CH])
        m.gates = sb("gates", [P, 2, T])
        m.rot = sb("rot", [P, CH])
        m.small = sb("small", [P, 512])
        m.const_bf = sb("const_bf", [P, 256], BF16)
        m.ident_bf, m.causal_bf = m.const_bf[:, 0:128], m.const_bf[:, 128:256]
        m.big = sb("big", [P, 2048])
        m.cols = sb("cols", [P, 64])
        m.const = sb("const", [P, CONST_COLS])
        m.psum = held.enter_context(nc.psum_tensor("psum", [P, 8, CH], F32))
        part = lambda name: m.const[:, CONST_AT[name]:CONST_AT[name] + dict(CONST_PARTS)[name]]
        m.mean_w, m.ones, m.ident, m.block8, m.block16, m.block64 = (
            part(n) for n in ("mean_w", "ones", "ident", "block8", "block16", "block64"))
        m.tri, m.iota8, m.eps5, m.eps6 = (part(n) for n in ("tri", "iota8", "eps5", "eps6"))
        m.eps = {1e-5: m.eps5, 1e-6: m.eps6}
        scratch = nc.dram_tensor("gates_by_expert", [NE, T], F32, kind="Internal").ap()
        load_columns(nc, [(m.x[:], a["xT"]), (m.const[:], a["const"])])
        with stage(nc, "copied") as (block, s):
            @block.vector
            def _(dve):
                nc.vector.tensor_copy(m.ident_bf[:], m.ident[:])
                nc.vector.tensor_copy(m.causal_bf[:], part("causal"))
        if first <= 1 <= stages:
            linear_attention_stage(nc, m, a)
            norm_stage(nc, m, m.s, m.x, 1e-5)
        if first <= 2 <= stages:
            sh = SoftmaxShape(64, 2, True, True, 1.0, 1.0)
            load_columns(nc, [(m.s[:], m.x[:])])
            with nc.Fori(0, L0_LAYERS) as layer:
                load_columns(nc, [(m.cols[:, 0:2], a["l0f_ln"][bass.ds(layer, 1)].rearrange("o p n -> p (o n)")),
                                  (m.tmp3[:], a["l0f_rope"])])
                norm_stage(nc, m, m.x, m.h, 1e-5, rms=True, weight=m.cols[:, 0:1], clip=100.0)
                load_columns(nc, [(m.tmp3[:], a["l0f_rope"])])
                softmax_attention_stage(nc, m, sh, a["l0f_attn"], layer * GROUPS)
                norm_stage(nc, m, m.x, m.h, 1e-5, rms=True, weight=m.cols[:, 1:2], clip=100.0)
                router_stage(nc, m, "plain", a["l0f_wr"][bass.ds(layer, 1)].rearrange("o p n -> p (o n)"), scratch)
                experts_stage(nc, m, ExpertShape("gated"), a["l0f_experts"], layer * NE, scratch)
            norm_stage(nc, m, m.x, m.x, 1e-5, clip=100.0, residual=m.s)
        flat = lambda t, i: t[bass.ds(i, 1)].rearrange("o p n -> p (o n)")
        if first <= 3 <= stages:
            load_columns(nc, [(m.s[:], m.x[:])])
            with nc.Fori(0, L1_LAYERS) as layer:
                load_columns(nc, [(m.cols[:, 0:4], flat(a["l1a_ln"], layer))])
                norm_stage(nc, m, m.x, m.h, 1e-5, weight=m.cols[:, 0:1], bias=m.cols[:, 1:2])
                load_columns(nc, [(m.tmp4[:], a["l1a_xpos"])])
                causal_attention_stage(nc, m, CausalShape(True), a["l1a_attn"], layer * 2, a["l1a_decays"])
                norm_stage(nc, m, m.x, m.h, 1e-5, weight=m.cols[:, 2:3], bias=m.cols[:, 3:4])
                experts_stage(nc, m, ExpertShape("ffn"), a["l1a_ffn"], layer, scratch)
            norm_stage(nc, m, m.x, m.x, 1e-5, residual=m.s)
        if first <= 4 <= stages:
            load_columns(nc, [(m.h[:], m.x[:])])
            router_stage(nc, m, "norm", a["l1f_wa"], scratch)
            experts_stage(nc, m, ExpertShape("lowrank"), a["l1f_experts"], 0, scratch)
            norm_stage(nc, m, m.x, m.x, 1e-5)
        if first <= 5 <= stages:
            load_columns(nc, [(m.h[:], m.x[:]), (m.cols[:, 8:12], a["l2a_qk"])])
            causal_attention_stage(nc, m, CausalShape(False), a["l2a_attn"], 0)
            norm_stage(nc, m, m.x, m.x, 1e-5)
        if first <= 6 <= stages:
            load_columns(nc, [(m.h[:], m.x[:]), (m.s[:], m.x[:]), (m.cols[:, 0:5], a["l2f_cols"])])
            sh = SoftmaxShape(32, 1, False, False, 8.0 ** -0.5, 1.0)
            softmax_attention_stage(nc, m, sh, a["l2f_attn"], 0)
            norm_stage(nc, m, m.x, m.h, 1e-6, weight=m.cols[:, 1:2], bias=m.cols[:, 2:3], add=m.cols[:, 0:1])
            load_columns(nc, [(m.x[:], m.h[:])])
            router_stage(nc, m, "double", a["l2f_wr"], scratch)
            experts_stage(nc, m, ExpertShape("gelu"), a["l2f_experts"], 0, scratch)
            norm_stage(nc, m, m.x, m.x, 1e-6, weight=m.cols[:, 3:4], bias=m.cols[:, 4:5])
            norm_stage(nc, m, m.x, m.x, 1e-5, residual=m.s)
        if first <= 7 <= stages:
            load_columns(nc, [(m.h[:], m.x[:])])
            sh = SoftmaxShape(32, 1, False, False, 8.0 ** -0.5 / D, (S / (S - 1.0)) ** 0.5 / D)
            softmax_attention_stage(nc, m, sh, a["l3a_attn"], 0)
            norm_stage(nc, m, m.x, m.x, 1e-5)
        if first <= 8 <= stages:
            sign_projection_stage(nc, m, a)
            norm_stage(nc, m, m.s, m.x, 1e-5)
        with stage(nc, "stored") as (block, s):
            @block.sync
            def _(sp):
                sp.dma_start(a["out"], m.x[:]).then_inc(s["stored"], 16)
                sp.wait_ge(s["stored"], 16)


CONST_PARTS = [("mean_w", 128), ("ones", 128), ("ident", 128), ("block8", 128), ("eps5", 1), ("eps6", 1), ("iota8", 8),
               ("block16", 128), ("block64", 128), ("tri", 512), ("causal", 128)]
CONST_AT = {n: sum(w for _, w in CONST_PARTS[:i]) for i, (n, _) in enumerate(CONST_PARTS)}
CONST_COLS = sum(w for _, w in CONST_PARTS)


def constants():
    i = np.arange(P)
    parts = {
        "mean_w": np.full((P, P), 1.0 / D), "ones": np.ones((P, P)), "ident": np.eye(P),
        "block8": (i[:, None] // 8 == i[None, :] // 8) * 1.0,
        "block16": ((i[:, None] // 32 == i[None, :] // 32) & (i[:, None] % 32 < 16) & (i[None, :] % 32 < 16)) / 16.0,
        "block64": (i[:, None] // 64 == i[None, :] // 64) / 64.0,
        "tri": (np.arange(S)[None, :] >= i[:, None]) * 1.0,
        "causal": np.where(i[None, :] > i[:, None], -1e9, 0.0),
        "iota8": np.tile(np.arange(8.0) - 8, (P, 1)),
        "eps5": np.full((P, 1), 1e-5), "eps6": np.full((P, 1), 1e-6),
    }
    return np.concatenate([parts[n].reshape(P, w) for n, w in CONST_PARTS], 1).astype(np.float32)


def layout(i):
    return {
        "xT": i["L0_attn_x"].reshape(T, D).T,
        "const": constants(),
        "l0a_wqkv": i["L0_attn_w_qkv"].T, "l0a_wout": i["L0_attn_w_out"].T,
        "l0a_bout": i["L0_attn_b_out"].reshape(P, 1),
        "l0f_ln": np.stack([i["L0_ffn_ln1_w"], i["L0_ffn_ln2_w"]], 2),
        "l1a_ln": np.stack([i["L1_attn_ln1_w"], i["L1_attn_ln1_b"], i["L1_attn_ln2_w"], i["L1_attn_ln2_b"]], 2),
        "l1a_attn": retention_weights(i), "l1a_xpos": xpos_tables(), "l1a_decays": decay_tables(),
        "l1a_ffn": biased(i["L1_attn_ffn_w1"], i["L1_attn_ffn_w2"], i["L1_attn_ffn_b1"], i["L1_attn_ffn_b2"]),
        "l1f_wa": i["L1_ffn_W_A"].transpose(2, 0, 1).reshape(D, -1), "l1f_experts": l1f_weights(i),
        "l2a_attn": l2_attention_weights(i),
        "l2a_qk": columns(*(np.tile(i["L2_attn_" + n], 2) for n in ("q_gamma", "q_beta", "k_gamma", "k_beta"))),
        "l2f_attn": padded_attention_weights(i["L2_ffn_Wq"], i["L2_ffn_Wk"], i["L2_ffn_Wv"], i["L2_ffn_Wo"]),
        "l2f_cols": columns(*(i["L2_ffn_" + n] for n in ("bo", "ln1_g", "ln1_b", "ln2_g", "ln2_b"))),
        "l2f_wr": i["L2_ffn_Wr"],
        "l2f_experts": biased(i["L2_ffn_We1"], i["L2_ffn_We2"], i["L2_ffn_be1"], i["L2_ffn_be2"]),
        "l3a_attn": padded_attention_weights(*(i["L3_attn_w_qkv"].T[:, k * D:(k + 1) * D] for k in range(3)),
                                             i["L3_attn_w_o"].T),
        "l3f_w": i["L3_ffn_weights"].T, "l3f_scale_bias": columns(i["L3_ffn_scale"], i["L3_ffn_bias"]),
        "l0f_wr": i["L0_ffn_wr"],
        "l0f_experts": np.concatenate([i["L0_ffn_wg"], i["L0_ffn_wu"], rows_to_columns(i["L0_ffn_wd"])], 3)
        .reshape(L0_LAYERS * NE, P, -1),
        "l0f_attn": l0f_attention_weights(i), "l0f_rope": l0f_rope_tables(),
    }


def rows_to_columns(w):
    w = w.reshape(*w.shape[:-2], -1, P, w.shape[-1])
    return np.moveaxis(w, -3, -2).reshape(*w.shape[:-3], P, -1)


def l0f_attention_weights(i):
    L, HD = L0_LAYERS, 64
    d = np.arange(HD)
    turned = (d + HD // 2) % HD
    wq = i["L0_ffn_wq"].reshape(L, D, GROUPS, 4, HD)
    wk = i["L0_ffn_wk"].reshape(L, D, GROUPS, 1, HD)
    wv = i["L0_ffn_wv"].reshape(L, D, GROUPS, 1, HD)
    wo = i["L0_ffn_wo"].reshape(L, GROUPS, 2, 2 * HD, D).transpose(0, 3, 1, 2, 4)
    kk = np.concatenate([wk, wk], 3)
    parts = [kk, kk[..., turned], wq, wq[..., turned], wv]
    flat = [w.transpose(0, 2, 1, 3, 4).reshape(L * GROUPS, D, -1) for w in parts]
    flat.append(wo.transpose(0, 2, 1, 3, 4).reshape(L * GROUPS, P, -1))
    out = np.concatenate(flat, 2)
    return np.concatenate([out, out[:1]], 0)


def l0f_rope_tables():
    d = np.arange(P) % 64
    inv = (1.0 / np.float32(10000.0) ** (np.arange(0, 64, 2, dtype=np.float32) / np.float32(64))).astype(np.float32)
    ang = (np.arange(S, dtype=np.float32)[None, :] * inv[d % 32][:, None]).astype(np.float32)
    cos, sin = np.cos(ang), np.sin(ang) * np.where(d < 32, -1, 1)[:, None]
    return np.concatenate([cos, sin, cos / 8, sin / 8], 1).astype(np.float32)


def pad_heads(w, heads, head_dim, rows):
    w = w.reshape(*w.shape[:-1], heads, head_dim)
    w = np.concatenate([w, np.zeros((*w.shape[:-1], rows - head_dim), w.dtype)], -1)
    w = w.reshape(*w.shape[:-2], heads * rows // P, P)
    return np.moveaxis(w, -2, 0)


def padded_attention_weights(wq, wk, wv, wo):
    k, q, v = (pad_heads(w, 16, 8, 32) for w in (wk, wq, wv))
    o = np.moveaxis(pad_heads(wo.T, 16, 8, 32), -1, -2)
    out = np.concatenate([k, q, v, o], 2)
    return np.concatenate([out, out[:1]], 0)


def retention_weights(i):
    L = L1_LAYERS
    turned = np.arange(16) ^ 1
    flat = lambda w: w.transpose(0, 2, 1, 3)
    q, k, v = flat(i["L1_attn_WQ"]), flat(i["L1_attn_WK"]), flat(i["L1_attn_WV"])
    pad = lambda w: pad_heads(w.reshape(L, -1, D), 8, 16, 32)
    parts = [pad(q), pad(q[..., turned]), pad(k), pad(k[..., turned]), pad(v), pad(i["L1_attn_WG"]),
             pad(i["L1_attn_WO"].transpose(0, 2, 1)).swapaxes(-1, -2),
             pad(i["L1_attn_gn_w"][:, None]).swapaxes(-1, -2), pad(i["L1_attn_gn_b"][:, None]).swapaxes(-1, -2)]
    out = np.concatenate(parts, 3).transpose(1, 0, 2, 3).reshape(L * 2, P, -1)
    return np.concatenate([out, out[:1]], 0)


def xpos_tables():
    HD, half = 16, 8
    scale_vec = (np.arange(0, HD, 2) + 0.4 * HD) / (1.4 * HD)
    scale = scale_vec[None, :] ** (np.arange(S, dtype=np.float64) / 64)[:, None]
    ang = np.arange(S)[:, None] / 10000.0 ** (np.arange(half) / half)[None, :]
    sin, cos = np.sin(ang), np.cos(ang)
    sign = np.where(np.arange(HD) % 2 == 0, -1.0, 1.0)
    out = []
    for t, sg in ((cos * scale, 1), (sin * scale, sign), (cos / scale, 1), (sin / scale, sign)):
        t = (np.repeat(t, 2, axis=-1).astype(np.float32) * sg).T
        out.append(np.tile(np.concatenate([t, np.zeros((16, S))], 0), (4, 1)))
    return np.concatenate(out, 1).astype(np.float32)


def decay_tables():
    gammas = 1.0 - np.exp(np.linspace(np.log(1.0 / 32), np.log(1.0 / 64), 8))
    diff = (np.arange(S)[None, :] - np.arange(P)[:, None]).astype(np.float64)
    d = np.where(diff >= 0, gammas[:, None, None] ** np.maximum(diff, 0), 0.0)
    d = d.reshape(2, 4, P, S).transpose(0, 2, 1, 3).reshape(2, P, 4 * S).astype(np.float32)
    return np.concatenate([d, d[:1]], 0)


def l2_attention_weights(i):
    split = lambda w: w.T.reshape(D, 8, P).transpose(1, 0, 2)
    wo = i["L2_attn_Wo"].T.reshape(8, P, D)
    out = np.concatenate([split(i["L2_attn_Wq"]), split(i["L2_attn_Wk"]), split(i["L2_attn_Wv"]), wo], 2)
    return np.concatenate([out, out[:1]], 0)


def columns(*vectors):
    return np.stack([np.asarray(v).reshape(P) for v in vectors], 1)


def l1f_weights(i):
    swap = lambda w: w.transpose(0, 2, 1)
    wb = swap(i["L1_ffn_W_B"])
    wb = np.concatenate([wb, np.zeros_like(wb)], 1)
    return np.concatenate([swap(i["L1_ffn_W_A"]), wb, swap(i["L1_ffn_W_up"]),
                           rows_to_columns(swap(i["L1_ffn_W_down"]))], 2)


def biased(w1, w2, b1, b2):
    return np.concatenate([w1, rows_to_columns(w2), b1.reshape(-1, 4, P).transpose(0, 2, 1), b2[:, :, None]], 2)


STAGES = 99
FIRST = 1


def kernel(**inputs):
    import concourse.bacc as bacc
    from concourse.bass_utils import run_bass_kernel_spmd
    nc = bacc.Bacc("TRN2", target_bir_lowering=False, num_devices=1)
    given = {k: np.asarray(v) for k, v in inputs.items()}
    arrays, args = {}, {}
    for name, value in layout(given).items():
        value = np.ascontiguousarray(value)
        arrays[name + "_dram"] = value
        args[name] = nc.dram_tensor(name + "_dram", value.shape, mybir.dt.from_np(value.dtype),
                                    kind="ExternalInput").ap()
    args["out"] = nc.dram_tensor("out_dram", [P, T], F32, kind="ExternalOutput").ap()
    build(nc, args, FIRST, STAGES)
    r = run_bass_kernel_spmd(nc, [arrays], core_ids=[0])
    return np.ascontiguousarray(r.results[0]["out_dram"].T).reshape(B, S, D)
```

```python
import numpy as np
import concourse.bass as bass
from concourse import mybir
from contextlib import ExitStack, contextmanager, nullcontext

F32 = mybir.dt.float32
BF16 = mybir.dt.bfloat16
ACT = mybir.ActivationFunctionType
ALU = mybir.AluOpType
AX = mybir.AxisListType

B, S, D = 4, 512, 128
T = B * S
CH = 512
NC = T // CH
P = 128
L0_LAYERS, L1_LAYERS = 4, 2


class Memory:
    pass


@contextmanager
def stage(nc, names):
    with ExitStack() as held:
        sems = {n: held.enter_context(nc.semaphore(n)) for n in names.split()}
        with nc.Block() as block:
            yield block, sems
        for sem in sems.values():
            nc.gpsimd.sem_clear(sem)
        nc.all_engine_barrier()


class Chain:

    def __init__(self, eng, sem, per_round=0, round_=0):
        self.eng, self.sem, self.n, self.base = eng, sem, 0, round_ * per_round
        self.per_round = per_round

    def add(self, ins):
        ins.then_inc(self.sem, 1)
        self.n += 1
        return self.n

    def wait(self, n=None):
        self.eng.wait_ge(self.sem, self.base + (self.n if n is None else n))

    def link(self, ins):
        self.add(ins)
        self.wait()

    def close(self):
        assert self.n == self.per_round, (self.n, self.per_round)


def load_columns(nc, pairs):
    with stage(nc, "loaded") as (block, s):
        @block.sync
        def _(sp):
            for out, src in pairs:
                sp.dma_start(out, src).then_inc(s["loaded"], 16)
            sp.wait_ge(s["loaded"], 16 * len(pairs))


def norm_stage(nc, m, src, dst, eps, rms=False, weight=None, bias=None, clip=None,
               residual=None, add=None):
    pre = clip or residual is not None or add is not None
    xc, sq, rstd = m.tmp1, m.tmp2, m.tmp3
    mean_bank, var_bank = (lambda c: m.psum[:, c, :]), (lambda c: m.psum[:, 4 + c, :])
    col = lambda t, c: t[:, c * CH:(c + 1) * CH]
    with stage(nc, "clipped mean_ready centred squared var_ready log_ready rstd_ready v_step") as (block, s):
        @block.tensor
        def _(pe):
            if not rms:
                for c in range(NC):
                    if pre:
                        pe.wait_ge(s["clipped"], c + 1)
                    nc.tensor.matmul(mean_bank(c), m.mean_w[:], col(src, c), start=True, stop=True)\
                        .then_inc(s["mean_ready"], 1)
            for c in range(NC):
                pe.wait_ge(s["squared"], c + 1)
                nc.tensor.matmul(var_bank(c), m.mean_w[:], col(sq, c), start=True, stop=True)\
                    .then_inc(s["var_ready"], 1)

        @block.scalar
        def _(act):
            nc.scalar.preload_act_table_set("natural_log_exp_and_others")
            for c in range(NC):
                if rms and clip:
                    act.wait_ge(s["clipped"], c + 1)
                elif not rms:
                    act.wait_ge(s["centred"], c + 1)
                nc.scalar.activation(col(sq, c), col(src if rms else xc, c), ACT.Square).then_inc(s["squared"], 1)
            for c in range(NC):
                act.wait_ge(s["var_ready"], c + 1)
                nc.scalar.activation(col(rstd, c), var_bank(c), ACT.Ln, bias=m.eps[eps]).then_inc(s["log_ready"], 1)
                act.wait_ge(s["log_ready"], c + 1)
                nc.scalar.activation(col(rstd, c), col(rstd, c), ACT.Exp, scale=-0.5).then_inc(s["rstd_ready"], 1)

        @block.vector
        def _(dve):
            step = Chain(dve, s["v_step"])
            if pre:
                for c in range(NC):
                    if clip:
                        last = nc.vector.tensor_scalar(col(src, c), col(src, c), clip, -clip, ALU.min, ALU.max)
                    if clip and residual is not None:
                        step.link(last)
                    if residual is not None:
                        last = nc.vector.tensor_tensor(col(src, c), col(src, c), col(residual, c), ALU.add)
                    if add is not None:
                        last = nc.vector.tensor_scalar(col(src, c), col(src, c), add, None, ALU.add)
                    last.then_inc(s["clipped"], 1)
            for c in range(NC):
                if not rms:
                    dve.wait_ge(s["mean_ready"], c + 1)
                    nc.vector.tensor_tensor(col(xc, c), col(src, c), mean_bank(c), ALU.subtract)\
                        .then_inc(s["centred"], 1)
            if pre:
                dve.wait_ge(s["clipped"], NC)
            if not rms:
                dve.wait_ge(s["centred"], NC)
            for c in range(NC):
                dve.wait_ge(s["rstd_ready"], c + 1)
                if rms:
                    nc.vector.scalar_tensor_tensor(col(dst, c), col(src, c), weight, col(rstd, c), ALU.mult, ALU.mult)
                elif weight is None:
                    nc.vector.tensor_tensor(col(dst, c), col(xc, c), col(rstd, c), ALU.mult)
                else:
                    step.link(nc.vector.tensor_tensor(col(rstd, c), col(xc, c), col(rstd, c), ALU.mult))
                    nc.vector.tensor_scalar(col(dst, c), col(rstd, c), weight, bias, ALU.mult, ALU.add)


def linear_attention_stage(nc, m, a):
    H, HD = 16, 8
    NT = S // P
    w, wo, bo = m.big[:, 0:384], m.big[:, 384:512], m.cols[:, 0:1]
    q = m.tmp1[:, 0:CH]
    qe = m.tmp1[:, CH:2 * CH]
    kv = m.tmp2[:].rearrange("p (t n) -> p t n", t=8)
    ke = m.tmp3[:, 0:CH].rearrange("p (t n) -> p t n", t=NT)
    kvm = m.tmp3[:, 512:640]
    ksm = m.tmp3[:, 640:768]
    rden = m.tmp3[:, 1024:1536]
    o = m.tmp3[:, 1536:2048]
    load_columns(nc, [(w, a["l0a_wqkv"]), (wo, a["l0a_wout"]), (bo, a["l0a_bout"])])
    with stage(nc, "q_ps kv_ps q_min q_exp k_min k_exp q_done k_done v_step sums_ps sums_done "
                   "num_ps o_done y_ps y_done") as (block, s):
        @block.tensor
        def _(pe):
            for b in range(B):
                x = m.x[:, b * CH:(b + 1) * CH]
                if b:
                    pe.wait_ge(s["q_done"], b)
                nc.tensor.matmul(m.psum[:, 0, :], w[:, 0:128], x, start=True, stop=True).then_inc(s["q_ps"], 1)
                if b:
                    pe.wait_ge(s["k_done"], b)
                for t in range(NT):
                    last = nc.tensor.matmul(m.psum[:, 1 + t // 2, (t % 2) * 256:(t % 2) * 256 + 256],
                                            x[:, t * P:(t + 1) * P], w[:, 128:384], start=True, stop=True)
                last.then_inc(s["kv_ps"], 1)
                pe.wait_ge(s["k_done"], b + 1)
                for t in range(NT):
                    nc.tensor.matmul(m.psum[:, 3, 0:128], kv[:, t, 0:128], kv[:, t, 128:256],
                                     start=t == 0, stop=t == NT - 1)
                for t in range(NT):
                    last = nc.tensor.matmul(m.psum[:, 4, 0:128], kv[:, t, 0:128], m.ones[:],
                                            start=t == 0, stop=t == NT - 1)
                last.then_inc(s["sums_ps"], 1)
                pe.wait_ge(s["sums_done"], b + 1)
                pe.wait_ge(s["q_done"], b + 1)
                nc.tensor.matmul(m.psum[:, 5, :], ksm, q, start=True, stop=True)
                nc.tensor.matmul(m.psum[:, 6, :], kvm, q, start=True, stop=True).then_inc(s["num_ps"], 1)
                pe.wait_ge(s["o_done"], b + 1)
                nc.tensor.matmul(m.psum[:, 7, :], wo, o, start=True, stop=True).then_inc(s["y_ps"], 1)

        @block.scalar
        def _(act):
            nc.scalar.preload_act_table_set("natural_log_exp_and_others")
            for b in range(B):
                act.wait_ge(s["q_min"], b + 1)
                nc.scalar.activation(qe, qe, ACT.Exp).then_inc(s["q_exp"], 1)
                act.wait_ge(s["k_min"], b + 1)
                nc.scalar.activation(ke, ke, ACT.Exp).then_inc(s["k_exp"], 1)

        @block.vector
        def _(dve):
            step = Chain(dve, s["v_step"])
            kps = m.psum[:, 1:3, :].rearrange("p g (t n) -> p (g t) n", t=2)
            for b in range(B):
                dve.wait_ge(s["q_ps"], b + 1)
                if b:
                    dve.wait_ge(s["num_ps"], b)
                nc.vector.tensor_scalar(qe, m.psum[:, 0, :], 0.0, None, ALU.min).then_inc(s["q_min"], 1)
                dve.wait_ge(s["kv_ps"], b + 1)
                nc.vector.tensor_scalar(ke, kps[:, :, 0:128], 0.0, None, ALU.min).then_inc(s["k_min"], 1)
                nc.vector.tensor_copy(kv[:, 0:NT, 128:256], kps[:, :, 128:256])
                dve.wait_ge(s["q_exp"], b + 1)
                nc.vector.scalar_tensor_tensor(q, m.psum[:, 0, :], 0.0, qe, ALU.max, ALU.add).then_inc(s["q_done"], 1)
                dve.wait_ge(s["k_exp"], b + 1)
                nc.vector.scalar_tensor_tensor(kv[:, 0:NT, 0:128], kps[:, :, 0:128], 0.0, ke, ALU.max, ALU.add)\
                    .then_inc(s["k_done"], 1)
                dve.wait_ge(s["sums_ps"], b + 1)
                nc.vector.tensor_tensor(kvm, m.psum[:, 3, 0:128], m.block8[:], ALU.mult)
                nc.vector.tensor_tensor(ksm, m.psum[:, 4, 0:128], m.block8[:], ALU.mult).then_inc(s["sums_done"], 1)
                dve.wait_ge(s["num_ps"], b + 1)
                step.link(nc.vector.tensor_scalar(rden, m.psum[:, 5, :], 1e-6, None, ALU.add))
                step.link(nc.vector.reciprocal(rden, rden))
                if b:
                    dve.wait_ge(s["y_ps"], b)
                nc.vector.tensor_tensor(o, m.psum[:, 6, :], rden, ALU.mult).then_inc(s["o_done"], 1)
                dve.wait_ge(s["y_ps"], b + 1)
                nc.vector.scalar_tensor_tensor(m.s[:, b * CH:(b + 1) * CH], m.psum[:, 7, :], bo,
                                               m.x[:, b * CH:(b + 1) * CH], ALU.add, ALU.add)


class SoftmaxShape:

    def __init__(self, rows, stacks, causal, rope, q_scale, y_scale):
        self.rows, self.stacks, self.causal, self.rope = rows, stacks, causal, rope
        self.q_scale, self.y_scale = q_scale, y_scale
        self.per_stack = P // rows
        self.side_by_side = self.per_stack
        self.v_cols = rows if rope else P
        at = 0
        self.at = {}
        for name, width in (("k", P), ("kr", P * rope), ("q", P * stacks), ("qr", P * stacks * rope),
                            ("v", self.v_cols), ("wo", P * stacks)):
            self.at[name] = at
            at += width
        self.cols = at


GROUPS = 4
UNITS = 16


def softmax_attention_stage(nc, m, sh, weights, first_group):
    NT = S // P
    tiles = lambda u: (tile(u) + 1) if sh.causal else NT
    C = sh.side_by_side
    head = lambda u: u // (C * NT) * C + u % C
    tile = lambda u: u % (C * NT) // C
    stack = lambda u: head(u) // sh.per_stack
    rows = lambda u: slice(head(u) % sh.per_stack * sh.rows, (head(u) % sh.per_stack + 1) * sh.rows)
    per_stack_units = sh.per_stack * NT
    PROJ = sh.stacks + 2
    V_STEPS = (1 + sh.stacks) * (1 if sh.rope else 0)
    T_BANK, O_BANK, W_BANK = 3, 5, 6
    steps = GROUPS * B
    FREE = 8
    TL, VL = 3, 4
    PROJ_AT = [8, 10, 12, 14][-PROJ:]

    def col(slot, name, k=0, width=P):
        return m.w[:, slot, sh.at[name] + k * P:sh.at[name] + k * P + width]

    hb = lambda slot: m.hb[:, slot, :]
    kT = lambda slot: m.tmp1[:, slot * CH:(slot + 1) * CH]
    qT = lambda slot, k: m.tmp2[:, (2 * slot + k) * CH:(2 * slot + k + 1) * CH]
    v = lambda slot: m.tmp1[:, 1024 + slot * CH:1024 + slot * CH + NT * sh.v_cols].rearrange("p (t n) -> p t n", t=NT)
    ropes = lambda i: m.tmp3[:, i * CH:(i + 1) * CH]
    oT = lambda k: m.tmp4[:, k * CH:(k + 1) * CH]
    pT = lambda u: m.gates[:, u % (2 * C) // 4, u % 4 * CH:u % 4 * CH + tiles(u) * P]
    bank = lambda u: u % 3 if u < UNITS - 1 else 1
    s_before = lambda u: next(d for d in range(1, UNITS) if bank((u - d) % UNITS) == bank(u))
    scores_ps = lambda u: m.psum[:, bank(u), 0:tiles(u) * P]
    p = lambda u: m.p[:, u % 4, 0:tiles(u) * P]
    neg_max, row_sum, row_inv = m.small[:, 0:16], m.small[:, 16:32], m.small[:, 32:48]

    with stage(nc, "loaded0 loaded1 proj_ps proj_done s_ready max_ready exp_done inv_ready p_ready t_ready "
                   "pt_by_act pt_by_dve pv_done o_done y_ready y_done v_step") as (block, s):
        loaded = (s["loaded0"], s["loaded1"])

        def unit_of(n, j):
            return (n, j) if j < UNITS else (n + 1, j - UNITS)

        def wait_pt(eng, n, u):
            eng.wait_ge((s["pt_by_act"], s["pt_by_dve"])[u % 2], n * (UNITS // 2) + u // 2 + 1 + FREE)

        @block.sync
        def _(sp):
            def load(g, b, slot):
                sp.dma_start(m.w[:, slot, 0:sh.cols], weights[bass.ds(first_group + g, 1)].rearrange("o p n -> p (o n)"))\
                    .then_inc(loaded[slot], 16)
                sp.dma_start(hb(slot), m.h[:, bass.ds(b * CH, CH)]).then_inc(loaded[slot], 16)

            for slot in range(2):
                load(0, slot, slot)
            with sp.Fori(0, GROUPS) as g:
                for slot in range(2):
                    sp.wait_ge(s["y_ready"], 4 * g + slot + 1 + 1)
                    load(g, 2 + slot, slot)
                for slot in range(2):
                    sp.wait_ge(s["y_ready"], 4 * g + slot + 3 + 1)
                    load(g + 1, slot, slot)
            for slot in range(2):
                sp.wait_ge(loaded[slot], 32 * (2 * GROUPS + 1))

        @block.tensor
        def _(pe):
            def project(n, r, slot, k):
                if k == 0:
                    pe.wait_ge(loaded[slot], 32 * r + 32)
                    if not isinstance(n, int):
                        pe.wait_ge(s["y_done"], n)
                else:
                    pe.wait_ge(s["proj_done"], PROJ * n + k)
                if k == PROJ - 1:
                    for t in range(NT):
                        last = nc.tensor.matmul(m.psum[:, W_BANK, t * sh.v_cols:(t + 1) * sh.v_cols],
                                                hb(slot)[:, t * P:(t + 1) * P],
                                                col(slot, "v", width=sh.v_cols), start=True, stop=True)
                else:
                    a, b = ("k", 0) if k == 0 else ("q", k - 1)
                    last = nc.tensor.matmul(m.psum[:, W_BANK, :], col(slot, a, b), hb(slot), start=True, stop=True)
                    if sh.rope:
                        last = nc.tensor.matmul(m.psum[:, W_BANK + 1, :], col(slot, a + "r", b), hb(slot),
                                                start=True, stop=True)
                last.then_inc(s["proj_ps"], 1)

            def scores(n, u, slot):
                if u == 0:
                    pe.wait_ge(s["proj_done"], PROJ * n + PROJ)
                pe.wait_ge(s["exp_done"], UNITS * n + u - s_before(u) + 1 + FREE)
                out, w = scores_ps(u), tiles(u) * P
                last = nc.tensor.matmul(out, qT(slot, stack(u))[rows(u), tile(u) * P:(tile(u) + 1) * P],
                                        kT(slot)[rows(u), 0:w], start=True, stop=not sh.causal)
                if sh.causal:
                    last = nc.tensor.matmul(out[:, w - P:w], m.ident_bf[:], m.causal_bf[:], start=False, stop=True)
                last.then_inc(s["s_ready"], 1)

            def transposes(n, u):
                pe.wait_ge(s["p_ready"], UNITS * n + u + 1)
                pe.wait_ge((s["pt_by_act"], s["pt_by_dve"])[u % 2], n * (UNITS // 2) + u // 2 + FREE)
                for t in range(tiles(u)):
                    last = nc.tensor.transpose(m.psum[:, T_BANK + u % 2, t * P:(t + 1) * P],
                                               p(u)[:, t * P:(t + 1) * P], m.ident[:])
                last.then_inc(s["t_ready"], 1)

            def values(n, u, slot):
                if (u + 1) % C:
                    return
                units = range(u + 1 - C, u + 1)
                if units[0] % per_stack_units == 0:
                    pe.wait_ge(s["o_done"], sh.stacks * n + stack(u) + 1)
                for i in units[-2:]:
                    wait_pt(pe, n, i)
                for t in range(tiles(u)):
                    for i in units:
                        c = slice(0, sh.rows) if sh.rope else rows(i)
                        last = nc.tensor.matmul(m.psum[rows(i), O_BANK, tile(i) * P:(tile(i) + 1) * P],
                                                v(slot)[:, t, c], pT(i)[:, t * P:(t + 1) * P],
                                                start=t == 0, stop=t == tiles(i) - 1)
                last.then_inc(s["pv_done"], C)

            for k in range(PROJ):
                project(0, 0, 0, k)
            for j in range(VL):
                scores(0, j, 0)
                if j >= TL:
                    transposes(0, j - TL)
            with pe.Fori(0, steps // 2) as r:
                for slot in range(2):
                    n = 2 * r + slot
                    for j in range(VL, UNITS + VL):
                        n_j, u = unit_of(n, j)
                        scores(n_j, u, slot if j < UNITS else 1 - slot)
                        transposes(*unit_of(n, j - TL))
                        values(n, j - VL, slot)
                        if j in PROJ_AT:
                            project(n + 1, r + slot, 1 - slot, PROJ_AT.index(j))
                    for k in range(sh.stacks):
                        pe.wait_ge(s["o_done"], sh.stacks * n + k + 2)
                        last = nc.tensor.matmul(m.psum[:, W_BANK, :], col(slot, "wo", k), oT(k),
                                                start=k == 0, stop=k == sh.stacks - 1)
                    last.then_inc(s["y_ready"], 1)

        @block.scalar
        def _(act):
            nc.scalar.preload_act_table_set("natural_log_exp_and_others")
            def exponential(n, u):
                act.wait_ge(s["max_ready"], UNITS * n + u + 1)
                act.wait_ge(s["t_ready"], UNITS * n + u - 3 + FREE)
                nc.scalar.activation(p(u), scores_ps(u), ACT.Exp,
                                     bias=neg_max[:, u:u + 1], accum_out=row_sum[:, u:u + 1])\
                    .then_inc(s["exp_done"], 1)

            def evacuate(n, u):
                act.wait_ge(s["t_ready"], UNITS * n + u + 1 + FREE)
                act.wait_ge(s["pv_done"], UNITS * n + u - 2 * C + 1 + FREE)
                nc.scalar.copy(pT(u), m.psum[:, T_BANK + u % 2, 0:tiles(u) * P]).then_inc(s["pt_by_act"], 1)

            act.sem_inc(s["exp_done"], FREE)
            act.sem_inc(s["pt_by_act"], FREE)
            for j in range(VL):
                exponential(0, j)
                if j >= TL and (j - TL) % 2 == 0:
                    evacuate(0, j - TL)
            with act.Fori(0, steps // 2) as r:
                for slot in range(2):
                    n = 2 * r + slot
                    for j in range(VL, UNITS + VL):
                        exponential(*unit_of(n, j))
                        if (j - TL) % 2 == 0:
                            evacuate(*unit_of(n, j - TL))

        @block.gpsimd
        def _(pool):
            def normalise(n, u):
                pool.wait_ge(s["inv_ready"], UNITS * n + u + 1)
                nc.gpsimd.tensor_tensor(p(u), p(u), row_inv[:, u:u + 1].to_broadcast([P, tiles(u) * P]), ALU.mult)\
                    .then_inc(s["p_ready"], 1)

            for j in range(VL - 1):
                normalise(0, j)
            with pool.Fori(0, steps // 2) as r:
                for slot in range(2):
                    for j in range(VL - 1, UNITS + VL - 1):
                        normalise(*unit_of(2 * r + slot, j))

        @block.vector
        def _(dve):
            w0, w1 = m.psum[:, W_BANK, :], m.psum[:, W_BANK + 1, :]

            def projected(n, slot, k, chain):
                dve.wait_ge(s["proj_ps"], PROJ * n + k + 1)
                if k == PROJ - 1:
                    last = nc.vector.tensor_copy(v(slot), w0[:, 0:NT * sh.v_cols].rearrange("p (t n) -> p t n", t=NT))
                elif sh.rope:
                    out, tab = (kT(slot), 0) if k == 0 else (qT(slot, k - 1), 2)
                    nc.vector.tensor_tensor(out, w0, ropes(tab), ALU.mult)
                    chain.link(nc.vector.tensor_tensor(m.rot[:], w1, ropes(tab + 1), ALU.mult))
                    last = nc.vector.tensor_tensor(out, out, m.rot[:], ALU.add)
                elif k == 0:
                    last = nc.vector.tensor_copy(kT(slot), w0)
                else:
                    last = nc.vector.tensor_scalar(qT(slot, k - 1), w0, sh.q_scale, None, ALU.mult)
                last.then_inc(s["proj_done"], 1)

            def maximum(n, u):
                dve.wait_ge(s["s_ready"], UNITS * n + u + 1)
                nc.vector.tensor_reduce(neg_max[:, u:u + 1], scores_ps(u), AX.X, ALU.max, negate=True)\
                    .then_inc(s["max_ready"], 1)

            def inverse(n, u):
                dve.wait_ge(s["exp_done"], UNITS * n + u + 1 + FREE)
                nc.vector.reciprocal(row_inv[:, u:u + 1], row_sum[:, u:u + 1]).then_inc(s["inv_ready"], 1)

            def evacuate(n, u):
                dve.wait_ge(s["t_ready"], UNITS * n + u + 1 + FREE)
                dve.wait_ge(s["pv_done"], UNITS * n + u - 2 * C + 1 + FREE)
                nc.vector.tensor_copy(pT(u), m.psum[:, T_BANK + u % 2, 0:tiles(u) * P]).then_inc(s["pt_by_dve"], 1)

            def step(r, slot, b):
                n = 2 * r + slot
                chain = Chain(dve, s["v_step"], V_STEPS, n + 1)
                for j in range(VL, UNITS + VL):
                    maximum(*unit_of(n, j))
                    inverse(*unit_of(n, j - 1))
                    if (j - TL) % 2 == 1:
                        evacuate(*unit_of(n, j - TL))
                    if j - 1 in PROJ_AT:
                        projected(n + 1, 1 - slot, PROJ_AT.index(j - 1), chain)
                    last = j == UNITS + VL - 1
                    if (j - VL) % per_stack_units == 0 and j > VL or last:
                        u = UNITS - 1 if last else j - VL - 1
                        dve.wait_ge(s["pv_done"], UNITS * n + u + 1 + FREE)
                        if stack(u) == 0:
                            dve.wait_ge(s["y_ready"], n + 1)
                        nc.vector.tensor_copy(oT(stack(u)), m.psum[:, O_BANK, :]).then_inc(s["o_done"], 1)
                dve.wait_ge(s["y_ready"], n + 1 + 1)
                xb = m.x[:, bass.ds(b * CH, CH)]
                nc.vector.scalar_tensor_tensor(xb, w0, sh.y_scale, xb, ALU.mult, ALU.add).then_inc(s["y_done"], 1)
                dve.wait_ge(s["y_done"], n + 2)
                chain.close()

            for name, credit in (("o_done", 1), ("y_done", 1), ("y_ready", 1), ("t_ready", FREE), ("pv_done", FREE),
                                 ("pt_by_dve", FREE)):
                dve.sem_inc(s[name], credit)
            chain = Chain(dve, s["v_step"], V_STEPS)
            for k in range(PROJ):
                projected(0, 0, k, chain)
            chain.close()
            for j in range(VL):
                maximum(0, j)
                if j:
                    inverse(0, j - 1)
                if j >= TL and (j - TL) % 2 == 1:
                    evacuate(0, j - TL)
            with dve.Fori(0, GROUPS) as g:
                for b in range(B):
                    step(2 * g + b // 2, b % 2, b)


NE, NT_ALL = 8, T // P


def router_stage(nc, m, kind, weights, scratch):
    v3 = lambda k: m.big[:, k * 128:(k + 1) * 128].rearrange("p (t e) -> p t e", e=NE)
    lg, eq, cand, oh1, oh2, l2 = (v3(k) for k in range(6))
    comb = m.big[:, 768:896]
    col = lambda k: m.small[:, 64 + 16 * k:80 + 16 * k]
    m1, m2, first, d, w1, w2, z, p1, p2 = (col(k) for k in range(9))
    over_e = lambda c: c.rearrange("p (t o) -> p t o", o=1).to_broadcast([P, NT_ALL, NE])
    iota = m.iota8.rearrange("p (o e) -> p o e", o=1).to_broadcast([P, NT_ALL, NE])
    n_w = 512 if kind == "norm" else NE
    load_columns(nc, [(m.w[:, 0, 0:n_w], weights)])
    with stage(nc, "logits squared sums root top exps probs comb comb_t comb_s stored v_step a_step") as (block, s):
        @block.tensor
        def _(pe):
            for t in range(NT_ALL):
                out = m.psum[:, 0, t * NE:(t + 1) * NE]
                if kind == "norm":
                    out = m.psum[:, t % 4, :]
                    if t >= 4:
                        pe.wait_ge(s["squared"], t - 3)
                nc.tensor.matmul(out, m.h[:, t * P:(t + 1) * P], m.w[:, 0, 0:n_w], start=True, stop=True)\
                    .then_inc(s["logits"], 1)
            pe.wait_ge(s["comb"], 1)
            nc.tensor.transpose(m.psum[:, 4, 0:128], comb, m.ident[:]).then_inc(s["comb_t"], 1)

        @block.scalar
        def _(act):
            if kind == "norm":
                for t in range(NT_ALL):
                    act.wait_ge(s["logits"], t + 1)
                    if t >= 4:
                        act.wait_ge(s["sums"], t - 3)
                    nc.scalar.activation(m.tmp1[:, t % 4 * CH:t % 4 * CH + CH], m.psum[:, t % 4, :], ACT.Square)\
                        .then_inc(s["squared"], 1)
                act.wait_ge(s["sums"], NT_ALL)
                nc.scalar.activation(lg, lg, ACT.Sqrt).then_inc(s["root"], 1)
            act.wait_ge(s["top"], 1)
            if kind == "double":
                nc.scalar.activation(eq, eq, ACT.Exp)
            nc.scalar.activation(d, d, ACT.Exp).then_inc(s["exps"], 1)
            if kind == "double":
                act.wait_ge(s["probs"], 1)
                nc.scalar.activation(d, d, ACT.Exp).then_inc(s["exps"], 1)

        @block.vector
        def _(dve):
            link = Chain(dve, s["v_step"]).link
            if kind == "norm":
                for t in range(NT_ALL):
                    dve.wait_ge(s["squared"], t + 1)
                    sq = m.tmp1[:, t % 4 * CH:t % 4 * CH + CH].rearrange("p (e r) -> p e r", e=NE)
                    nc.vector.tensor_reduce(lg[:, t, :], sq, AX.X, ALU.add).then_inc(s["sums"], 1)
                dve.wait_ge(s["root"], 1)
            else:
                dve.wait_ge(s["logits"], NT_ALL)
                link(nc.vector.tensor_copy(lg, m.psum[:, 0, 0:128].rearrange("p (t e) -> p t e", e=NE)))

            def best(src, largest, onehot):
                link(nc.vector.tensor_reduce(largest, src, AX.X, ALU.max))
                link(nc.vector.tensor_tensor(eq, src, over_e(largest), ALU.is_ge))
                link(nc.vector.tensor_tensor(cand, eq, iota, ALU.mult))
                link(nc.vector.tensor_reduce(first, cand, AX.X, ALU.min))
                link(nc.vector.tensor_tensor(onehot, cand, over_e(first), ALU.is_equal))

            best(lg, m1, oh1)
            link(nc.vector.scalar_tensor_tensor(l2, oh1, -1e30, lg, ALU.mult, ALU.add))
            best(l2, m2, oh2)
            if kind == "double":
                link(nc.vector.tensor_tensor(eq, lg, over_e(m1), ALU.subtract))
            link(nc.vector.tensor_tensor(d, m2, m1, ALU.subtract))
            dve.sem_inc(s["top"], 1)
            dve.wait_ge(s["exps"], 1)
            if kind == "double":
                link(nc.vector.tensor_reduce(z, eq, AX.X, ALU.add))
                link(nc.vector.reciprocal(p1, z))
                link(nc.vector.tensor_tensor(p2, d, p1, ALU.mult))
                link(nc.vector.tensor_tensor(d, p2, p1, ALU.subtract))
                dve.sem_inc(s["probs"], 1)
                dve.wait_ge(s["exps"], 2)
            link(nc.vector.tensor_scalar(w1, d, 1.0, None, ALU.add))
            link(nc.vector.reciprocal(w1, w1))
            link(nc.vector.tensor_tensor(w2, d, w1, ALU.mult))
            link(nc.vector.tensor_tensor(oh1, oh1, over_e(w1), ALU.mult))
            link(nc.vector.tensor_tensor(oh2, oh2, over_e(w2), ALU.mult))
            nc.vector.tensor_tensor(comb.rearrange("p (e t) -> p t e", e=NE), oh1, oh2, ALU.add).then_inc(s["comb"], 1)
            dve.wait_ge(s["comb_t"], 1)
            nc.vector.tensor_copy(m.big[:, 896:1024], m.psum[:, 4, 0:128]).then_inc(s["comb_s"], 1)

        @block.sync
        def _(sp):
            sp.wait_ge(s["comb_s"], 1)
            sp.dma_start(scratch.rearrange("e (t k) -> (e t) k", k=P), m.big[:, 896:1024]).then_inc(s["stored"], 16)
            sp.wait_ge(s["stored"], 16)


class ExpertShape:

    def __init__(self, kind):
        self.kind = kind
        self.tiles = {"gated": 2, "lowrank": 2, "gelu": 4, "ffn": 4}[kind]
        wide = self.tiles * P
        parts = {"gated": (("g", wide), ("u", wide), ("d", wide)),
                 "lowrank": (("a", 64), ("g", wide), ("u", wide), ("d", wide)),
                 "gelu": (("g", wide), ("d", wide), ("b1", 4), ("b2", 1))}[{"ffn": "gelu"}.get(kind, kind)]
        self.at, at = {}, 0
        for name, width in parts:
            self.at[name] = at
            at += width
        self.cols = at


def experts_stage(nc, m, sh, weights, first, scratch):
    FT, LAG = sh.tiles, 2
    U = NC * FT
    PAIRS = 2 if sh.kind == "lowrank" else 3
    gelu, low = sh.kind in ("gelu", "ffn"), sh.kind == "lowrank"
    single = sh.kind == "ffn"
    SLOTS = 1 if single else 2
    rounds = lambda eng: nullcontext(0) if single else eng.Fori(0, NE // 2)
    per_load = 16 if single else 32
    w = lambda slot, name, f=0, width=P: m.w[:, slot, sh.at[name] + f * P:sh.at[name] + f * P + width]
    h = lambda c: m.h[:, c * CH:(c + 1) * CH]
    g_bank = lambda k: m.psum[:, 2 * (k % PAIRS), :]
    u_bank = lambda k: m.psum[:, 2 * (k % PAIRS) + 1, :]
    y_bank = lambda c: m.psum[:, 6 + c % 2, :]
    low_bank = lambda c: m.psum[0:64, 4 + c % 2, :]
    low_sb = lambda c: m.tmp4[0:64, c % 2 * CH:(c % 2 + 1) * CH]
    gate_act = lambda k: m.tmp1[:, k % 3 * CH:(k % 3 + 1) * CH]
    hidden = lambda k: m.tmp2[:, k % 3 * CH:(k % 3 + 1) * CH]
    part = lambda c: m.tmp3[:, c % 2 * CH:(c % 2 + 1) * CH]
    with stage(nc, "loaded0 loaded1 low_ps low_done gu_ps act_done h_done y_mm y_done acc_done") as (block, s):
        loaded = (s["loaded0"], s["loaded1"])

        @block.sync
        def _(sp):
            def load(e, slot):
                sp.dma_start(m.w[:, slot, 0:sh.cols], weights[bass.ds(first + e, 1)].rearrange("o p n -> p (o n)"))\
                    .then_inc(loaded[slot], 16)
                if single:
                    return
                sp.dma_start(m.gates[:, slot, :], scratch[bass.ds(e, 1)].to_broadcast([P, T])).then_inc(loaded[slot], 16)

            for slot in range(SLOTS):
                load(slot, slot)
            if single:
                return
            with sp.Fori(0, NE // 2 - 1) as r:
                for slot in range(2):
                    sp.wait_ge(s["acc_done"], NC * (2 * r + slot + 1) + 1)
                    load(2 * r + 2 + slot, slot)

        @block.tensor
        def _(pe):
            with rounds(pe) as r:
                for slot in range(SLOTS):
                    e = 2 * r + slot
                    pe.wait_ge(loaded[slot], per_load * r + per_load)

                    def low_rank(c):
                        if c >= 2:
                            pe.wait_ge(s["low_done"], NC * e + c - 1)
                        nc.tensor.matmul(low_bank(c), w(slot, "a", width=64), h(c), start=True, stop=True)\
                            .then_inc(s["low_ps"], 1)

                    for k in range(U + LAG):
                        c, f = k // FT, k % FT
                        if k < U:
                            if low and f == 0:
                                if c == 0:
                                    low_rank(0)
                                if c + 1 < NC:
                                    low_rank(c + 1)
                                pe.wait_ge(s["low_done"], NC * e + c + 1)
                            if k >= PAIRS:
                                pe.wait_ge(s["h_done"], U * e + k - PAIRS + 1)
                            if low:
                                last = nc.tensor.matmul(g_bank(k), w(slot, "g", f)[0:64], low_sb(c), start=True, stop=True)
                            else:
                                last = nc.tensor.matmul(g_bank(k), w(slot, "g", f), h(c), start=True, stop=True)
                            if not gelu:
                                last = nc.tensor.matmul(u_bank(k), w(slot, "u", f), h(c), start=True, stop=True)
                            last.then_inc(s["gu_ps"], 1)
                        k -= LAG
                        if k >= 0:
                            c, f = k // FT, k % FT
                            if f == 0:
                                pe.wait_ge(s["y_done"], NC * e + max(c - 1, 0) + 1)
                            pe.wait_ge(s["h_done"], U * e + k + 1)
                            nc.tensor.matmul(y_bank(c), w(slot, "d", f), hidden(k), start=f == 0, stop=f == FT - 1)\
                                .then_inc(s["y_mm"], 1)

        @block.scalar
        def _(act):
            with rounds(act) as r:
                for slot in range(SLOTS):
                    e = 2 * r + slot
                    for k in range(U):
                        act.wait_ge(s["gu_ps"], U * e + k + 1)
                        if gelu:
                            if k >= 3:
                                act.wait_ge(s["y_mm"], U * e + k - 2)
                            nc.scalar.activation(hidden(k), g_bank(k), ACT.Silu if single else ACT.Gelu, bias=w(slot, "b1")[:, k % FT:k % FT + 1])\
                                .then_inc(s["h_done"], 1)
                        else:
                            if k >= 3:
                                act.wait_ge(s["h_done"], U * e + k - 2)
                            nc.scalar.activation(gate_act(k), g_bank(k), ACT.Silu).then_inc(s["act_done"], 1)

        @block.vector
        def _(dve):
            dve.sem_inc(s["y_done"], 1)
            dve.sem_inc(s["acc_done"], 1)
            with rounds(dve) as r:
                for slot in range(SLOTS):
                    e = 2 * r + slot

                    def low_copy(c):
                        dve.wait_ge(s["low_ps"], NC * e + c + 1)
                        if c >= 2:
                            dve.wait_ge(s["gu_ps"], U * e + (c - 1) * FT)
                        nc.vector.tensor_copy(low_sb(c), low_bank(c)).then_inc(s["low_done"], 1)

                    for k in range(U + LAG):
                        if low and k < U and k % FT == 0:
                            if k == 0:
                                low_copy(0)
                            elif k // FT >= 1:
                                low_copy(k // FT)
                        if k < U and not gelu:
                            dve.wait_ge(s["act_done"], U * e + k + 1)
                            if k >= 3:
                                dve.wait_ge(s["y_mm"], U * e + k - 2)
                            nc.vector.tensor_tensor(hidden(k), gate_act(k), u_bank(k), ALU.mult).then_inc(s["h_done"], 1)
                        j = k - LAG
                        if j >= 0 and j % FT == FT - 1:
                            c = j // FT
                            dve.wait_ge(s["y_mm"], U * e + j + 1)
                            if c >= 2:
                                dve.wait_ge(s["acc_done"], NC * e + c)
                            else:
                                dve.wait_ge(s["acc_done"], NC * e + 1)
                            gate = m.gates[:, slot, c * CH:(c + 1) * CH]
                            if single:
                                last = nc.vector.tensor_scalar(part(c), y_bank(c), w(slot, "b2", width=1), None, ALU.add)
                            elif gelu:
                                last = nc.vector.scalar_tensor_tensor(part(c), y_bank(c), w(slot, "b2", width=1), gate,
                                                                      ALU.add, ALU.mult)
                            else:
                                last = nc.vector.tensor_tensor(part(c), y_bank(c), gate, ALU.mult)
                            last.then_inc(s["y_done"], 1)

        @block.gpsimd
        def _(pool):
            with rounds(pool) as r:
                for slot in range(SLOTS):
                    e = 2 * r + slot
                    for c in range(NC):
                        pool.wait_ge(s["y_done"], NC * e + c + 2)
                        acc = m.x[:, c * CH:(c + 1) * CH]
                        nc.gpsimd.tensor_tensor(acc, acc, part(c), ALU.add).then_inc(s["acc_done"], 1)


class CausalShape:

    def __init__(self, retention):
        self.retention = retention
        self.rows = 32 if retention else 64
        self.heads = P // self.rows
        self.groups = 2 if retention else 8
        names = "q qr k kr v wg wo" if retention else "q k v wo"
        self.at = {n: i * P for i, n in enumerate(names.split())}
        self.early = self.at["wo"]
        self.cols = len(self.at) * P + (2 if retention else 0)


def causal_attention_stage(nc, m, sh, weights, first_group, decays=None):
    NT, HEADS, G, ret = S // P, sh.heads, sh.groups, sh.retention
    U = HEADS * NT
    C = HEADS
    head = lambda u: u % C
    tile = (lambda u: u // C) if ret else (lambda u: (0, 3, 1, 2)[u // C])
    width = lambda u: (NT - tile(u)) * P
    rows = lambda u: slice(head(u) * sh.rows, (head(u) + 1) * sh.rows)
    BANKS, O_BANK, STAT_BANK = (4 if ret else 2), 3, 4 if ret else 6
    S_BANKS = (0, 1, 2, 5)[:BANKS]
    QK_BANK, V_BANK = (6, 6) if ret else (4, 2)
    LAG, FREE = (4 if ret else 2), 8
    NORMS = 1 if ret else 2
    PROJ = 3 if ret else 2
    heads_of = lambda t: t.rearrange("p (h n) -> p h n", n=64)
    V_STEPS = 4
    steps = G * B
    late_load = 32 if ret else 16
    col = lambda slot, name: m.w[:, slot, sh.at[name]:sh.at[name] + P]
    wo = lambda slot: m.late[:, slot, 0:P]
    norm_column = lambda slot, i: m.late[:, slot, P + i:P + i + 1]
    hb = lambda slot: m.hb[:, slot, :]
    part = lambda t, i: t[:, i * CH:(i + 1) * CH]
    qT, kT = (lambda slot: part(m.tmp1, slot)), (lambda slot: part(m.tmp1, 2 + slot))
    v = lambda slot: part(m.tmp2, slot).rearrange("p (t n) -> p t n", t=NT)
    oT, gate = m.oT[:], lambda slot: part(m.tmp2, 2 + slot)
    sT_at = lambda u: (m.p[:, u % 4, :], part(m.big, u % 4))[u % (2 * C) // 4]
    sT = lambda u: sT_at(u)[:, 0:width(u)]
    sq, rstd = (lambda i: part(m.tmp3, i)), (lambda i: part(m.tmp3, 2 + i))
    stat_ps = lambda i: m.psum[:, STAT_BANK + i, :]
    s_bank = lambda u: m.psum[:, S_BANKS[u % BANKS], 0:width(u)]
    FRONT = {4: "q", 6: "k", 8: "v", 10: "gate"} if ret else {2: "qk", 3: "v", 5: "variances"}
    xpos = lambda i: part(m.tmp4, i)
    table = lambda slot, u: (part(m.gates[:, slot, :], head(u))[:, 0:width(u)] if ret
                             else m.tri[:, 0:width(u)])
    qk_ps = (m.psum[:, QK_BANK, :], m.psum[:, QK_BANK + 1, :])
    block_mean = m.block16 if ret else m.block64
    with stage(nc, "early0 early1 late0 late1 weights_centred proj_ps proj_done raw_ready mean_ps centred squared var_ps log_ready rstd_ready "
                   "normed s_ready s_done pv_done o_done gate_ps gate_done y_ready y_done v_step") as (block, s):
        early, late = (s["early0"], s["early1"]), (s["late0"], s["late1"])

        @block.sync
        def _(sp):
            packed = lambda g, c: weights[bass.ds(first_group + g, 1)][:, :, c].rearrange("o p n -> p (o n)")

            def load_early(g, b, slot):
                sp.dma_start(m.w[:, slot, 0:sh.early], packed(g, slice(0, sh.early))).then_inc(early[slot], 16)
                sp.dma_start(hb(slot), m.h[:, bass.ds(b * CH, CH)]).then_inc(early[slot], 16)

            def load_late(g, slot):
                sp.dma_start(m.late[:, slot, 0:sh.cols - sh.early], packed(g, slice(sh.early, sh.cols)))\
                    .then_inc(late[slot], 16)
                if ret:
                    sp.dma_start(m.gates[:, slot, :], decays[bass.ds(g, 1)].rearrange("o p n -> p (o n)"))\
                        .then_inc(late[slot], 16)

            for slot in range(2):
                load_early(0, slot, slot)
                load_late(0, slot)
            sp.wait_ge(s["proj_done"], PROJ)
            if ret:
                sp.wait_ge(s["gate_ps"], 1)
            load_early(0, 2, 0)
            with sp.Fori(0, G) as g:
                for b in range(B):
                    n = 4 * g + b
                    sp.wait_ge(s["proj_done"], PROJ * (n + 2))
                    if ret:
                        sp.wait_ge(s["gate_ps"], n + 2)
                    load_early(g + (b + 3) // B, (b + 3) % B, (b + 1) % 2)
                    sp.wait_ge(s["y_ready"], n + 1)
                    load_late(g + (b + 2) // B, b % 2)
            for slot in range(2):
                sp.wait_ge(early[slot], 32 * (2 * G + 2 - slot))
                sp.wait_ge(late[slot], late_load * (2 * G + 1))

        def unit_of(n, j):
            return (n, j) if j < U else (n + 1, j - U)

        @block.tensor
        def _(pe):
            def mean(n, i, raw):
                pe.wait_ge(s["raw_ready"], NORMS * n + i + 1)
                nc.tensor.matmul(stat_ps(i), block_mean, raw, start=True, stop=True).then_inc(s["mean_ps"], 1)

            def variance(n, i):
                pe.wait_ge(s["squared"], NORMS * n + i + 1)
                nc.tensor.matmul(stat_ps(i), block_mean, sq(i), start=True, stop=True).then_inc(s["var_ps"], 1)

            def front(n, r, slot, what):
                if what in ("q", "qk"):
                    if ret:
                        pe.wait_ge(early[slot], 32 * r + 32)
                    else:
                        pe.wait_ge(s["weights_centred"], n + 1)
                        if not isinstance(n, int):
                            pe.wait_ge(s["normed"], NORMS * n)
                    if not isinstance(n, int):
                        pe.wait_ge(s["y_done"], n)
                        if ret:
                            pe.wait_ge(s["gate_done"], n)
                if what in ("q", "k", "qk"):
                    if what == "k":
                        pe.wait_ge(s["proj_done"], PROJ * n + 1)
                    for bank, name in enumerate({"q": ("q", "qr"), "k": ("k", "kr"), "qk": ("q", "k")}[what]):
                        last = nc.tensor.matmul(m.psum[:, QK_BANK + bank, :], col(slot, name), hb(slot),
                                                start=True, stop=True)
                    last.then_inc(s["proj_ps"], 1)
                elif what == "v":
                    if ret:
                        pe.wait_ge(s["proj_done"], PROJ * n + PROJ - 1)
                    for t in range(NT):
                        last = nc.tensor.matmul(m.psum[:, V_BANK, t * P:(t + 1) * P], hb(slot)[:, t * P:(t + 1) * P],
                                                col(slot, "v"), start=True, stop=True)
                    last.then_inc(s["proj_ps"], 1)
                elif what == "gate":
                    nc.tensor.matmul(m.psum[:, QK_BANK + 1, :], col(slot, "wg"), hb(slot), start=True, stop=True)\
                        .then_inc(s["gate_ps"], 1)
                else:
                    for i in range(2):
                        variance(n, i)

            def scores(n, u, slot):
                if u == 0:
                    pe.wait_ge(s["proj_done"], PROJ * n + PROJ)
                    if not ret:
                        pe.wait_ge(s["normed"], NORMS * n + NORMS)
                pe.wait_ge(s["s_done"], U * n + u - BANKS + 1 + FREE)
                t = tile(u)
                nc.tensor.matmul(s_bank(u), kT(slot)[rows(u), t * P:(t + 1) * P],
                                 qT(slot)[rows(u), t * P:CH], start=True, stop=True).then_inc(s["s_ready"], 1)

            def values(n, u, slot):
                if (u + 1) % C:
                    return
                if u == C - 1:
                    pe.wait_ge(s["o_done"], n + 1)
                pe.wait_ge(s["s_done"], U * n + u + 1 + FREE)
                t = tile(u)
                for i in range(u + 1 - C, u + 1):
                    last = nc.tensor.matmul(m.psum[rows(i), O_BANK, t * P:CH], v(slot)[:, t, rows(i)], sT(i),
                                            start=u == C - 1, stop=u == U - 1)
                last.then_inc(s["pv_done"], C)

            for what in FRONT.values():
                front(0, 0, 0, what)
            for j in range(LAG):
                scores(0, j, 0)
            with pe.Fori(0, steps // 2) as r:
                for slot in range(2):
                    n = 2 * r + slot
                    for j in range(LAG, U + LAG):
                        scores(*unit_of(n, j), slot if j < U else 1 - slot)
                        values(n, j - LAG, slot)
                        if j in FRONT:
                            front(n + 1, r + slot, 1 - slot, FRONT[j])
                    if ret:
                        mean(n, 0, oT)
                        variance(n, 0)
                        pe.wait_ge(s["normed"], n + 1)
                    pe.wait_ge(s["o_done"], n + 2)
                    pe.wait_ge(s["proj_done"], PROJ * (n + 2))
                    pe.wait_ge(late[slot], late_load * (r + 1))
                    nc.tensor.matmul(m.psum[:, V_BANK, :], wo(slot), oT, start=True, stop=True)\
                        .then_inc(s["y_ready"], 1)

        @block.scalar
        def _(act):
            nc.scalar.preload_act_table_set("natural_log_exp_and_others")
            def norms(n, which, xs):
                for i, x in zip(which, xs):
                    if ret:
                        act.wait_ge(s["centred"], NORMS * n + i + 1)
                    elif i == 0:
                        act.wait_ge(s["proj_ps"], PROJ * n + 1)
                    nc.scalar.activation(sq(i), x, ACT.Square).then_inc(s["squared"], 1)
                for i in which:
                    act.wait_ge(s["var_ps"], NORMS * n + i + 1)
                    if not isinstance(n, int):
                        act.wait_ge(s["normed"], NORMS * n)
                    nc.scalar.activation(rstd(i), stat_ps(i), ACT.Ln, bias=m.eps5).then_inc(s["log_ready"], 1)
                    act.wait_ge(s["log_ready"], NORMS * n + i + 1)
                    nc.scalar.activation(rstd(i), rstd(i), ACT.Exp, scale=-0.5).then_inc(s["rstd_ready"], 1)

            def silu(n, slot):
                act.wait_ge(s["gate_ps"], n + 1)
                nc.scalar.activation(gate(slot), m.psum[:, QK_BANK + 1, :], ACT.Silu).then_inc(s["gate_done"], 1)

            if ret:
                silu(0, 0)
            else:
                norms(0, (0, 1), qk_ps)
            with act.Fori(0, steps // 2) as r:
                for slot in range(2):
                    n = 2 * r + slot
                    if ret:
                        silu(n + 1, 1 - slot)
                        nc.scalar.preload_act_table_set("natural_log_exp_and_others")
                        norms(n, (0,), (oT,))
                    else:
                        norms(n + 1, (0, 1), qk_ps)

        @block.vector
        def _(dve):
            w0, w1 = m.psum[:, QK_BANK, :], m.psum[:, QK_BANK + 1, :]
            out_ps = m.psum[:, V_BANK, :]

            def centre(n, i, x):
                dve.wait_ge(s["mean_ps"], NORMS * n + i + 1)
                nc.vector.tensor_tensor(x, x, stat_ps(i), ALU.subtract).then_inc(s["centred"], 1)

            def scale(n, i, src, x, weight, bias, chain, slot):
                dve.wait_ge(s["rstd_ready"], NORMS * n + i + 1)
                chain.link(nc.vector.tensor_tensor(x, src, rstd(i), ALU.mult))
                last = nc.vector.tensor_scalar(x, x, weight, bias, ALU.mult, ALU.add)
                if ret:
                    chain.link(last)
                    last = nc.vector.tensor_tensor(x, x, gate(slot), ALU.mult)
                last.then_inc(s["normed"], 1)

            def front(n, r, slot, what, chain):
                if what in ("q", "k"):
                    i = "qk".index(what)
                    out = (qT(slot), kT(slot))[i]
                    dve.wait_ge(s["proj_ps"], PROJ * n + i + 1)
                    nc.vector.tensor_tensor(out, w0, xpos(2 * i), ALU.mult)
                    chain.link(nc.vector.tensor_tensor(m.rot[:], w1, xpos(2 * i + 1), ALU.mult))
                    nc.vector.tensor_tensor(out, out, m.rot[:], ALU.add).then_inc(s["proj_done"], 1)
                elif what == "qk":
                    dve.wait_ge(early[slot], 32 * r + 32)
                    w = heads_of(m.w[:, slot, 0:2 * P])
                    sums = m.small[:, 0:4]
                    chain.link(nc.vector.tensor_reduce(sums, w, AX.X, ALU.add))
                    chain.link(nc.vector.tensor_scalar(sums, sums, 1.0 / 64, None, ALU.mult))
                    nc.vector.tensor_tensor(w, w, sums.rearrange("p (h o) -> p h o", o=1).to_broadcast([P, 4, 64]),
                                            ALU.subtract).then_inc(s["weights_centred"], 1)
                elif what == "v":
                    dve.wait_ge(s["proj_ps"], PROJ * n + PROJ)
                    nc.vector.tensor_copy(v(slot), out_ps.rearrange("p (t n) -> p t n", t=NT))\
                        .then_inc(s["proj_done"], 1 if ret else 2)
                elif what == "variances":
                    for i, x in enumerate((qT(slot), kT(slot))):
                        scale(n, i, qk_ps[i], x, m.cols[:, 8 + 2 * i:9 + 2 * i], m.cols[:, 9 + 2 * i:10 + 2 * i], chain, slot)

            def weigh(n, r, u, slot):
                if ret and u == 0:
                    dve.wait_ge(late[slot], late_load * r + late_load)
                dve.wait_ge(s["s_ready"], U * n + u + 1)
                dve.wait_ge(s["pv_done"], U * n + u - 2 * C + 1 + FREE)
                nc.vector.tensor_tensor(sT(u), s_bank(u), table(slot, u), ALU.mult).then_inc(s["s_done"], 1)

            def step(r, slot, b):
                n = 2 * r + slot
                chain = Chain(dve, s["v_step"], V_STEPS, n + 1)
                for j in range(LAG, U + LAG):
                    if j in FRONT and FRONT[j] == "qk":
                        front(n + 1, r + slot, 1 - slot, "qk", chain)
                    if j - 1 in FRONT and FRONT[j - 1] != "qk":
                        front(n + 1, r + slot, 1 - slot, FRONT[j - 1], chain)
                    n_j, u = unit_of(n, j)
                    weigh(n_j, r if j < U else r + slot, u, slot if j < U else 1 - slot)
                dve.wait_ge(s["pv_done"], U * n + U + FREE)
                nc.vector.tensor_copy(oT, m.psum[:, O_BANK, :]).then_inc(s["o_done"], 1)
                if ret:
                    dve.wait_ge(s["o_done"], n + 2)
                    dve.sem_inc(s["raw_ready"], 1)
                    centre(n, 0, oT)
                    dve.wait_ge(s["gate_done"], n + 1)
                    dve.wait_ge(s["centred"], n + 1)
                    scale(n, 0, oT, oT, norm_column(slot, 0), norm_column(slot, 1), chain, slot)
                dve.wait_ge(s["y_ready"], n + 1)
                xb = m.x[:, bass.ds(b * CH, CH)]
                nc.vector.tensor_tensor(xb, out_ps, xb, ALU.add).then_inc(s["y_done"], 1)
                dve.wait_ge(s["y_done"], n + 2)
                chain.close()

            dve.sem_inc(s["o_done"], 1)
            dve.sem_inc(s["y_done"], 1)
            for name in ("s_done", "pv_done"):
                dve.sem_inc(s[name], FREE)
            chain = Chain(dve, s["v_step"], V_STEPS)
            for what in FRONT.values():
                front(0, 0, 0, what, chain)
            if ret:
                chain.n += 2
                dve.sem_inc(s["v_step"], 2)
            chain.close()
            for j in range(LAG):
                weigh(0, 0, j, 0)
            with dve.Fori(0, G) as g:
                for b in range(B):
                    step(2 * g + b // 2, b % 2, b)


def sign_projection_stage(nc, m, a):
    w = m.big[:, 0:128]
    y = lambda c: m.tmp1[:, c * CH:(c + 1) * CH]
    x = lambda c: m.x[:, c * CH:(c + 1) * CH]
    load_columns(nc, [(w, a["l3f_w"]), (m.cols[:, 0:2], a["l3f_scale_bias"])])
    with stage(nc, "signs y_ps v_step") as (block, s):
        @block.tensor
        def _(pe):
            pe.wait_ge(s["signs"], 1)
            for c in range(NC):
                nc.tensor.matmul(m.psum[:, c, :], w, x(c), start=True, stop=True).then_inc(s["y_ps"], 1)

        @block.vector
        def _(dve):
            link = Chain(dve, s["v_step"]).link
            link(nc.vector.tensor_scalar(w, w, 0.0, 2.0, ALU.is_ge, ALU.mult))
            link(nc.vector.tensor_scalar(w, w, -1.0, None, ALU.add))
            dve.sem_inc(s["signs"], 1)
            for c in range(NC):
                dve.wait_ge(s["y_ps"], c + 1)
                link(nc.vector.tensor_scalar(y(c), m.psum[:, c, :], m.cols[:, 0:1], m.cols[:, 1:2], ALU.mult, ALU.add))
                link(nc.vector.tensor_scalar(y(c), y(c), 100.0, -100.0, ALU.min, ALU.max))
                nc.vector.tensor_tensor(m.s[:, c * CH:(c + 1) * CH], x(c), y(c), ALU.add)


def build(nc, a, first=1, stages=99):
    with ExitStack() as held:
        def sb(name, shape, dt=F32):
            return held.enter_context(nc.sbuf_tensor(name, shape, dt))
        m = Memory()
        m.x, m.s, m.h = (sb(n, [P, T]) for n in ("x", "s", "h"))
        m.tmp1, m.tmp2, m.tmp3 = (sb(n, [P, T]) for n in ("tmp1", "tmp2", "tmp3"))
        m.tmp4 = sb("tmp4", [P, T])
        m.w = sb("w", [P, 2, 1536])
        m.hb = sb("hb", [P, 2, CH])
        m.p = sb("p", [P, 4, CH])
        m.gates = sb("gates", [P, 2, T])
        m.oT = sb("oT", [P, CH])
        m.late = sb("late", [P, 2, 258])
        m.rot = sb("rot", [P, CH])
        m.small = sb("small", [P, 512])
        m.const_bf = sb("const_bf", [P, 256], BF16)
        m.ident_bf, m.causal_bf = m.const_bf[:, 0:128], m.const_bf[:, 128:256]
        m.big = sb("big", [P, 2048])
        m.cols = sb("cols", [P, 64])
        m.const = sb("const", [P, CONST_COLS])
        m.psum = held.enter_context(nc.psum_tensor("psum", [P, 8, CH], F32))
        part = lambda name: m.const[:, CONST_AT[name]:CONST_AT[name] + dict(CONST_PARTS)[name]]
        m.mean_w, m.ones, m.ident, m.block8, m.block16, m.block64 = (
            part(n) for n in ("mean_w", "ones", "ident", "block8", "block16", "block64"))
        m.tri, m.iota8, m.eps5, m.eps6 = (part(n) for n in ("tri", "iota8", "eps5", "eps6"))
        m.eps = {1e-5: m.eps5, 1e-6: m.eps6}
        scratch = nc.dram_tensor("gates_by_expert", [NE, T], F32, kind="Internal").ap()
        load_columns(nc, [(m.x[:], a["xT"]), (m.const[:], a["const"])])
        with stage(nc, "copied") as (block, s):
            @block.vector
            def _(dve):
                nc.vector.tensor_copy(m.ident_bf[:], m.ident[:])
                nc.vector.tensor_copy(m.causal_bf[:], part("causal"))
        if first <= 1 <= stages:
            linear_attention_stage(nc, m, a)
            norm_stage(nc, m, m.s, m.x, 1e-5)
        if first <= 2 <= stages:
            sh = SoftmaxShape(64, 2, True, True, 1.0, 1.0)
            load_columns(nc, [(m.s[:], m.x[:])])
            with nc.Fori(0, L0_LAYERS) as layer:
                load_columns(nc, [(m.cols[:, 0:2], a["l0f_ln"][bass.ds(layer, 1)].rearrange("o p n -> p (o n)")),
                                  (m.tmp3[:], a["l0f_rope"])])
                norm_stage(nc, m, m.x, m.h, 1e-5, rms=True, weight=m.cols[:, 0:1], clip=100.0)
                load_columns(nc, [(m.tmp3[:], a["l0f_rope"])])
                softmax_attention_stage(nc, m, sh, a["l0f_attn"], layer * GROUPS)
                norm_stage(nc, m, m.x, m.h, 1e-5, rms=True, weight=m.cols[:, 1:2], clip=100.0)
                router_stage(nc, m, "plain", a["l0f_wr"][bass.ds(layer, 1)].rearrange("o p n -> p (o n)"), scratch)
                experts_stage(nc, m, ExpertShape("gated"), a["l0f_experts"], layer * NE, scratch)
            norm_stage(nc, m, m.x, m.x, 1e-5, clip=100.0, residual=m.s)
        flat = lambda t, i: t[bass.ds(i, 1)].rearrange("o p n -> p (o n)")
        if first <= 3 <= stages:
            load_columns(nc, [(m.s[:], m.x[:])])
            with nc.Fori(0, L1_LAYERS) as layer:
                load_columns(nc, [(m.cols[:, 0:4], flat(a["l1a_ln"], layer))])
                norm_stage(nc, m, m.x, m.h, 1e-5, weight=m.cols[:, 0:1], bias=m.cols[:, 1:2])
                load_columns(nc, [(m.tmp4[:], a["l1a_xpos"])])
                causal_attention_stage(nc, m, CausalShape(True), a["l1a_attn"], layer * 2, a["l1a_decays"])
                norm_stage(nc, m, m.x, m.h, 1e-5, weight=m.cols[:, 2:3], bias=m.cols[:, 3:4])
                experts_stage(nc, m, ExpertShape("ffn"), a["l1a_ffn"], layer, scratch)
            norm_stage(nc, m, m.x, m.x, 1e-5, residual=m.s)
        if first <= 4 <= stages:
            load_columns(nc, [(m.h[:], m.x[:])])
            router_stage(nc, m, "norm", a["l1f_wa"], scratch)
            experts_stage(nc, m, ExpertShape("lowrank"), a["l1f_experts"], 0, scratch)
            norm_stage(nc, m, m.x, m.x, 1e-5)
        if first <= 5 <= stages:
            load_columns(nc, [(m.h[:], m.x[:]), (m.cols[:, 8:12], a["l2a_qk"])])
            causal_attention_stage(nc, m, CausalShape(False), a["l2a_attn"], 0)
            norm_stage(nc, m, m.x, m.x, 1e-5)
        if first <= 6 <= stages:
            load_columns(nc, [(m.h[:], m.x[:]), (m.s[:], m.x[:]), (m.cols[:, 0:5], a["l2f_cols"])])
            sh = SoftmaxShape(32, 1, False, False, 8.0 ** -0.5, 1.0)
            softmax_attention_stage(nc, m, sh, a["l2f_attn"], 0)
            norm_stage(nc, m, m.x, m.h, 1e-6, weight=m.cols[:, 1:2], bias=m.cols[:, 2:3], add=m.cols[:, 0:1])
            load_columns(nc, [(m.x[:], m.h[:])])
            router_stage(nc, m, "double", a["l2f_wr"], scratch)
            experts_stage(nc, m, ExpertShape("gelu"), a["l2f_experts"], 0, scratch)
            norm_stage(nc, m, m.x, m.x, 1e-6, weight=m.cols[:, 3:4], bias=m.cols[:, 4:5])
            norm_stage(nc, m, m.x, m.x, 1e-5, residual=m.s)
        if first <= 7 <= stages:
            load_columns(nc, [(m.h[:], m.x[:])])
            sh = SoftmaxShape(32, 1, False, False, 8.0 ** -0.5 / D, (S / (S - 1.0)) ** 0.5 / D)
            softmax_attention_stage(nc, m, sh, a["l3a_attn"], 0)
            norm_stage(nc, m, m.x, m.x, 1e-5)
        if first <= 8 <= stages:
            sign_projection_stage(nc, m, a)
            norm_stage(nc, m, m.s, m.x, 1e-5)
        with stage(nc, "stored") as (block, s):
            @block.sync
            def _(sp):
                sp.dma_start(a["out"], m.x[:]).then_inc(s["stored"], 16)
                sp.wait_ge(s["stored"], 16)


CONST_PARTS = [("mean_w", 128), ("ones", 128), ("ident", 128), ("block8", 128), ("eps5", 1), ("eps6", 1), ("iota8", 8),
               ("block16", 128), ("block64", 128), ("tri", 512), ("causal", 128)]
CONST_AT = {n: sum(w for _, w in CONST_PARTS[:i]) for i, (n, _) in enumerate(CONST_PARTS)}
CONST_COLS = sum(w for _, w in CONST_PARTS)


def constants():
    i = np.arange(P)
    parts = {
        "mean_w": np.full((P, P), 1.0 / D), "ones": np.ones((P, P)), "ident": np.eye(P),
        "block8": (i[:, None] // 8 == i[None, :] // 8) * 1.0,
        "block16": ((i[:, None] // 32 == i[None, :] // 32) & (i[:, None] % 32 < 16) & (i[None, :] % 32 < 16)) / 16.0,
        "block64": (i[:, None] // 64 == i[None, :] // 64) / 64.0,
        "tri": (np.arange(S)[None, :] >= i[:, None]) * 1.0,
        "causal": np.where(i[None, :] > i[:, None], -1e9, 0.0),
        "iota8": np.tile(np.arange(8.0) - 8, (P, 1)),
        "eps5": np.full((P, 1), 1e-5), "eps6": np.full((P, 1), 1e-6),
    }
    return np.concatenate([parts[n].reshape(P, w) for n, w in CONST_PARTS], 1).astype(np.float32)


def layout(i):
    return {
        "xT": i["L0_attn_x"].reshape(T, D).T,
        "const": constants(),
        "l0a_wqkv": i["L0_attn_w_qkv"].T, "l0a_wout": i["L0_attn_w_out"].T,
        "l0a_bout": i["L0_attn_b_out"].reshape(P, 1),
        "l0f_ln": np.stack([i["L0_ffn_ln1_w"], i["L0_ffn_ln2_w"]], 2),
        "l1a_ln": np.stack([i["L1_attn_ln1_w"], i["L1_attn_ln1_b"], i["L1_attn_ln2_w"], i["L1_attn_ln2_b"]], 2),
        "l1a_attn": retention_weights(i), "l1a_xpos": xpos_tables(), "l1a_decays": decay_tables(),
        "l1a_ffn": biased(i["L1_attn_ffn_w1"], i["L1_attn_ffn_w2"], i["L1_attn_ffn_b1"], i["L1_attn_ffn_b2"]),
        "l1f_wa": i["L1_ffn_W_A"].transpose(2, 0, 1).reshape(D, -1), "l1f_experts": l1f_weights(i),
        "l2a_attn": l2_attention_weights(i),
        "l2a_qk": columns(*(np.tile(i["L2_attn_" + n], 2) for n in ("q_gamma", "q_beta", "k_gamma", "k_beta"))),
        "l2f_attn": padded_attention_weights(i["L2_ffn_Wq"], i["L2_ffn_Wk"], i["L2_ffn_Wv"], i["L2_ffn_Wo"]),
        "l2f_cols": columns(*(i["L2_ffn_" + n] for n in ("bo", "ln1_g", "ln1_b", "ln2_g", "ln2_b"))),
        "l2f_wr": i["L2_ffn_Wr"],
        "l2f_experts": biased(i["L2_ffn_We1"], i["L2_ffn_We2"], i["L2_ffn_be1"], i["L2_ffn_be2"]),
        "l3a_attn": padded_attention_weights(*(i["L3_attn_w_qkv"].T[:, k * D:(k + 1) * D] for k in range(3)),
                                             i["L3_attn_w_o"].T),
        "l3f_w": i["L3_ffn_weights"].T, "l3f_scale_bias": columns(i["L3_ffn_scale"], i["L3_ffn_bias"]),
        "l0f_wr": i["L0_ffn_wr"],
        "l0f_experts": np.concatenate([i["L0_ffn_wg"], i["L0_ffn_wu"], rows_to_columns(i["L0_ffn_wd"])], 3)
        .reshape(L0_LAYERS * NE, P, -1),
        "l0f_attn": l0f_attention_weights(i), "l0f_rope": l0f_rope_tables(),
    }


def rows_to_columns(w):
    w = w.reshape(*w.shape[:-2], -1, P, w.shape[-1])
    return np.moveaxis(w, -3, -2).reshape(*w.shape[:-3], P, -1)


def l0f_attention_weights(i):
    L, HD = L0_LAYERS, 64
    d = np.arange(HD)
    turned = (d + HD // 2) % HD
    wq = i["L0_ffn_wq"].reshape(L, D, GROUPS, 4, HD)
    wk = i["L0_ffn_wk"].reshape(L, D, GROUPS, 1, HD)
    wv = i["L0_ffn_wv"].reshape(L, D, GROUPS, 1, HD)
    wo = i["L0_ffn_wo"].reshape(L, GROUPS, 2, 2 * HD, D).transpose(0, 3, 1, 2, 4)
    kk = np.concatenate([wk, wk], 3)
    parts = [kk, kk[..., turned], wq, wq[..., turned], wv]
    flat = [w.transpose(0, 2, 1, 3, 4).reshape(L * GROUPS, D, -1) for w in parts]
    flat.append(wo.transpose(0, 2, 1, 3, 4).reshape(L * GROUPS, P, -1))
    out = np.concatenate(flat, 2)
    return np.concatenate([out, out[:1]], 0)


def l0f_rope_tables():
    d = np.arange(P) % 64
    inv = (1.0 / np.float32(10000.0) ** (np.arange(0, 64, 2, dtype=np.float32) / np.float32(64))).astype(np.float32)
    ang = (np.arange(S, dtype=np.float32)[None, :] * inv[d % 32][:, None]).astype(np.float32)
    cos, sin = np.cos(ang), np.sin(ang) * np.where(d < 32, -1, 1)[:, None]
    return np.concatenate([cos, sin, cos / 8, sin / 8], 1).astype(np.float32)


def pad_heads(w, heads, head_dim, rows):
    w = w.reshape(*w.shape[:-1], heads, head_dim)
    w = np.concatenate([w, np.zeros((*w.shape[:-1], rows - head_dim), w.dtype)], -1)
    w = w.reshape(*w.shape[:-2], heads * rows // P, P)
    return np.moveaxis(w, -2, 0)


def padded_attention_weights(wq, wk, wv, wo):
    k, q, v = (pad_heads(w, 16, 8, 32) for w in (wk, wq, wv))
    o = np.moveaxis(pad_heads(wo.T, 16, 8, 32), -1, -2)
    out = np.concatenate([k, q, v, o], 2)
    return np.concatenate([out, out[:1]], 0)


def retention_weights(i):
    L = L1_LAYERS
    turned = np.arange(16) ^ 1
    flat = lambda w: w.transpose(0, 2, 1, 3)
    q, k, v = flat(i["L1_attn_WQ"]), flat(i["L1_attn_WK"]), flat(i["L1_attn_WV"])
    pad = lambda w: pad_heads(w.reshape(L, -1, D), 8, 16, 32)
    parts = [pad(q), pad(q[..., turned]), pad(k), pad(k[..., turned]), pad(v), pad(i["L1_attn_WG"]),
             pad(i["L1_attn_WO"].transpose(0, 2, 1)).swapaxes(-1, -2),
             pad(i["L1_attn_gn_w"][:, None]).swapaxes(-1, -2), pad(i["L1_attn_gn_b"][:, None]).swapaxes(-1, -2)]
    out = np.concatenate(parts, 3).transpose(1, 0, 2, 3).reshape(L * 2, P, -1)
    return np.concatenate([out, out[:1]], 0)


def xpos_tables():
    HD, half = 16, 8
    scale_vec = (np.arange(0, HD, 2) + 0.4 * HD) / (1.4 * HD)
    scale = scale_vec[None, :] ** (np.arange(S, dtype=np.float64) / 64)[:, None]
    ang = np.arange(S)[:, None] / 10000.0 ** (np.arange(half) / half)[None, :]
    sin, cos = np.sin(ang), np.cos(ang)
    sign = np.where(np.arange(HD) % 2 == 0, -1.0, 1.0)
    out = []
    for t, sg in ((cos * scale, 1), (sin * scale, sign), (cos / scale, 1), (sin / scale, sign)):
        t = (np.repeat(t, 2, axis=-1).astype(np.float32) * sg).T
        out.append(np.tile(np.concatenate([t, np.zeros((16, S))], 0), (4, 1)))
    return np.concatenate(out, 1).astype(np.float32)


def decay_tables():
    gammas = 1.0 - np.exp(np.linspace(np.log(1.0 / 32), np.log(1.0 / 64), 8))
    diff = (np.arange(S)[None, :] - np.arange(P)[:, None]).astype(np.float64)
    d = np.where(diff >= 0, gammas[:, None, None] ** np.maximum(diff, 0), 0.0)
    d = d.reshape(2, 4, P, S).transpose(0, 2, 1, 3).reshape(2, P, 4 * S).astype(np.float32)
    return np.concatenate([d, d[:1]], 0)


def l2_attention_weights(i):
    split = lambda w: w.T.reshape(D, 8, P).transpose(1, 0, 2)
    wo = i["L2_attn_Wo"].T.reshape(8, P, D)
    out = np.concatenate([split(i["L2_attn_Wq"]), split(i["L2_attn_Wk"]), split(i["L2_attn_Wv"]), wo], 2)
    return np.concatenate([out, out[:1]], 0)


def columns(*vectors):
    return np.stack([np.asarray(v).reshape(P) for v in vectors], 1)


def l1f_weights(i):
    swap = lambda w: w.transpose(0, 2, 1)
    wb = swap(i["L1_ffn_W_B"])
    wb = np.concatenate([wb, np.zeros_like(wb)], 1)
    return np.concatenate([swap(i["L1_ffn_W_A"]), wb, swap(i["L1_ffn_W_up"]),
                           rows_to_columns(swap(i["L1_ffn_W_down"]))], 2)


def biased(w1, w2, b1, b2):
    return np.concatenate([w1, rows_to_columns(w2), b1.reshape(-1, 4, P).transpose(0, 2, 1), b2[:, :, None]], 2)


STAGES = 99
FIRST = 1


def kernel(**inputs):
    import concourse.bacc as bacc
    from concourse.bass_utils import run_bass_kernel_spmd
    nc = bacc.Bacc("TRN2", target_bir_lowering=False, num_devices=1)
    given = {k: np.asarray(v) for k, v in inputs.items()}
    arrays, args = {}, {}
    for name, value in layout(given).items():
        value = np.ascontiguousarray(value)
        arrays[name + "_dram"] = value
        args[name] = nc.dram_tensor(name + "_dram", value.shape, mybir.dt.from_np(value.dtype),
                                    kind="ExternalInput").ap()
    args["out"] = nc.dram_tensor("out_dram", [P, T], F32, kind="ExternalOutput").ap()
    build(nc, args, FIRST, STAGES)
    r = run_bass_kernel_spmd(nc, [arrays], core_ids=[0])
    return np.ascontiguousarray(r.results[0]["out_dram"].T).reshape(B, S, D)
```

```python
import numpy as np
import concourse.bass as bass
from concourse import mybir
from contextlib import ExitStack, contextmanager, nullcontext

F32 = mybir.dt.float32
F32R = mybir.dt.float32r
BF16 = mybir.dt.bfloat16
ACT = mybir.ActivationFunctionType
ALU = mybir.AluOpType
AX = mybir.AxisListType

B, S, D = 4, 512, 128
T = B * S
CH = 512
NC = T // CH
P = 128
L0_LAYERS, L1_LAYERS = 4, 2


class Memory:
    pass


@contextmanager
def stage(nc, names):
    with ExitStack() as held:
        sems = {n: held.enter_context(nc.semaphore(n)) for n in names.split()}
        with nc.Block() as block:
            yield block, sems
        for sem in sems.values():
            nc.gpsimd.sem_clear(sem)
        nc.all_engine_barrier()


class Chain:

    def __init__(self, eng, sem, per_round=0, round_=0):
        self.eng, self.sem, self.n, self.base = eng, sem, 0, round_ * per_round
        self.per_round = per_round

    def add(self, ins):
        ins.then_inc(self.sem, 1)
        self.n += 1
        return self.n

    def wait(self, n=None):
        self.eng.wait_ge(self.sem, self.base + (self.n if n is None else n))

    def link(self, ins):
        self.add(ins)
        self.wait()

    def close(self):
        assert self.n == self.per_round, (self.n, self.per_round)


def load_columns(nc, pairs):
    with stage(nc, "loaded") as (block, s):
        @block.sync
        def _(sp):
            for out, src in pairs:
                sp.dma_start(out, src).then_inc(s["loaded"], 16)
            sp.wait_ge(s["loaded"], 16 * len(pairs))


def norm_stage(nc, m, src, dst, eps, rms=False, weight=None, bias=None, clip=None,
               residual=None, add=None, loads=(), copy=None):
    pre = clip or residual is not None or add is not None
    xc, sq, rstd = m.tmp1, m.tmp2, m.tmp3
    mean_bank, var_bank = (lambda c: m.psum[:, c, :]), (lambda c: m.psum[:, 4 + c, :])
    col = lambda t, c: t[:, c * CH:(c + 1) * CH]
    with stage(nc, "loaded copied normed clipped mean_ready centred squared var_ready log_ready rstd_ready v_step") \
            as (block, s):
        @block.sync
        def _(sp):
            for out, packed in loads:
                sp.dma_start(out, packed).then_inc(s["loaded"], 16)
            if copy is not None:
                for c in range(NC):
                    sp.wait_ge(s["normed"], c + 1)
                    sp.dma_start(col(copy, c), col(dst, c)).then_inc(s["copied"], 16)
                sp.wait_ge(s["copied"], 16 * NC)

        @block.tensor
        def _(pe):
            if not rms:
                for c in range(NC):
                    if pre:
                        pe.wait_ge(s["clipped"], c + 1)
                    nc.tensor.matmul(mean_bank(c), m.mean_w[:], col(src, c), start=True, stop=True)\
                        .then_inc(s["mean_ready"], 1)
            for c in range(NC):
                pe.wait_ge(s["squared"], c + 1)
                nc.tensor.matmul(var_bank(c), m.mean_w[:], col(sq, c), start=True, stop=True)\
                    .then_inc(s["var_ready"], 1)

        @block.scalar
        def _(act):
            nc.scalar.preload_act_table_set("natural_log_exp_and_others")
            for c in range(NC):
                if rms and clip:
                    act.wait_ge(s["clipped"], c + 1)
                elif not rms:
                    act.wait_ge(s["centred"], c + 1)
                nc.scalar.activation(col(sq, c), col(src if rms else xc, c), ACT.Square).then_inc(s["squared"], 1)
            for c in range(NC):
                act.wait_ge(s["var_ready"], c + 1)
                nc.scalar.activation(col(rstd, c), var_bank(c), ACT.Ln, bias=m.eps[eps]).then_inc(s["log_ready"], 1)
                act.wait_ge(s["log_ready"], c + 1)
                nc.scalar.activation(col(rstd, c), col(rstd, c), ACT.Exp, scale=-0.5).then_inc(s["rstd_ready"], 1)

        @block.vector
        def _(dve):
            step = Chain(dve, s["v_step"])
            if pre:
                for c in range(NC):
                    if clip:
                        last = nc.vector.tensor_scalar(col(src, c), col(src, c), clip, -clip, ALU.min, ALU.max)
                    if clip and residual is not None:
                        step.link(last)
                    if residual is not None:
                        last = nc.vector.tensor_tensor(col(src, c), col(src, c), col(residual, c), ALU.add)
                    if add is not None:
                        last = nc.vector.tensor_scalar(col(src, c), col(src, c), add, None, ALU.add)
                    last.then_inc(s["clipped"], 1)
            for c in range(NC):
                if not rms:
                    dve.wait_ge(s["mean_ready"], c + 1)
                    nc.vector.tensor_tensor(col(xc, c), col(src, c), mean_bank(c), ALU.subtract)\
                        .then_inc(s["centred"], 1)
            if pre:
                dve.wait_ge(s["clipped"], NC)
            if not rms:
                dve.wait_ge(s["centred"], NC)
            if loads:
                dve.wait_ge(s["loaded"], 16 * len(loads))
            for c in range(NC):
                dve.wait_ge(s["rstd_ready"], c + 1)
                if rms:
                    last = nc.vector.scalar_tensor_tensor(col(dst, c), col(src, c), weight, col(rstd, c), ALU.mult, ALU.mult)
                elif weight is None:
                    last = nc.vector.tensor_tensor(col(dst, c), col(xc, c), col(rstd, c), ALU.mult)
                else:
                    step.link(nc.vector.tensor_tensor(col(rstd, c), col(xc, c), col(rstd, c), ALU.mult))
                    last = nc.vector.tensor_scalar(col(dst, c), col(rstd, c), weight, bias, ALU.mult, ALU.add)
                last.then_inc(s["normed"], 1)


def linear_attention_stage(nc, m, a):
    H, HD = 16, 8
    NT = S // P
    w, wo, bo = m.big[:, 0:384], m.big[:, 384:512], m.cols[:, 0:1]
    q = m.tmp1[:, 0:CH]
    qe = m.tmp1[:, CH:2 * CH]
    kv = m.tmp2[:].rearrange("p (t n) -> p t n", t=8)
    ke = m.tmp3[:, 0:CH].rearrange("p (t n) -> p t n", t=NT)
    kvm = m.tmp3[:, 512:640]
    ksm = m.tmp3[:, 640:768]
    rden = m.tmp3[:, 1024:1536]
    o = m.tmp3[:, 1536:2048]
    load_columns(nc, [(w, a["l0a_wqkv"]), (wo, a["l0a_wout"]), (bo, a["l0a_bout"])])
    with stage(nc, "q_ps kv_ps q_min q_exp k_min k_exp q_done k_done v_step sums_ps sums_done "
                   "num_ps o_done y_ps y_done") as (block, s):
        @block.tensor
        def _(pe):
            for b in range(B):
                x = m.x[:, b * CH:(b + 1) * CH]
                if b:
                    pe.wait_ge(s["q_done"], b)
                nc.tensor.matmul(m.psum[:, 0, :], w[:, 0:128], x, start=True, stop=True).then_inc(s["q_ps"], 1)
                if b:
                    pe.wait_ge(s["k_done"], b)
                for t in range(NT):
                    last = nc.tensor.matmul(m.psum[:, 1 + t // 2, (t % 2) * 256:(t % 2) * 256 + 256],
                                            x[:, t * P:(t + 1) * P], w[:, 128:384], start=True, stop=True)
                last.then_inc(s["kv_ps"], 1)
                pe.wait_ge(s["k_done"], b + 1)
                for t in range(NT):
                    nc.tensor.matmul(m.psum[:, 3, 0:128], kv[:, t, 0:128], kv[:, t, 128:256],
                                     start=t == 0, stop=t == NT - 1)
                for t in range(NT):
                    last = nc.tensor.matmul(m.psum[:, 4, 0:128], kv[:, t, 0:128], m.ones[:],
                                            start=t == 0, stop=t == NT - 1)
                last.then_inc(s["sums_ps"], 1)
                pe.wait_ge(s["sums_done"], b + 1)
                pe.wait_ge(s["q_done"], b + 1)
                nc.tensor.matmul(m.psum[:, 5, :], ksm, q, start=True, stop=True)
                nc.tensor.matmul(m.psum[:, 6, :], kvm, q, start=True, stop=True).then_inc(s["num_ps"], 1)
                pe.wait_ge(s["o_done"], b + 1)
                nc.tensor.matmul(m.psum[:, 7, :], wo, o, start=True, stop=True).then_inc(s["y_ps"], 1)

        @block.scalar
        def _(act):
            nc.scalar.preload_act_table_set("natural_log_exp_and_others")
            for b in range(B):
                act.wait_ge(s["q_min"], b + 1)
                nc.scalar.activation(qe, qe, ACT.Exp).then_inc(s["q_exp"], 1)
                act.wait_ge(s["k_min"], b + 1)
                nc.scalar.activation(ke, ke, ACT.Exp).then_inc(s["k_exp"], 1)

        @block.vector
        def _(dve):
            step = Chain(dve, s["v_step"])
            kps = m.psum[:, 1:3, :].rearrange("p g (t n) -> p (g t) n", t=2)
            for b in range(B):
                dve.wait_ge(s["q_ps"], b + 1)
                if b:
                    dve.wait_ge(s["num_ps"], b)
                nc.vector.tensor_scalar(qe, m.psum[:, 0, :], 0.0, None, ALU.min).then_inc(s["q_min"], 1)
                dve.wait_ge(s["kv_ps"], b + 1)
                nc.vector.tensor_scalar(ke, kps[:, :, 0:128], 0.0, None, ALU.min).then_inc(s["k_min"], 1)
                nc.vector.tensor_copy(kv[:, 0:NT, 128:256], kps[:, :, 128:256])
                dve.wait_ge(s["q_exp"], b + 1)
                nc.vector.scalar_tensor_tensor(q, m.psum[:, 0, :], 0.0, qe, ALU.max, ALU.add).then_inc(s["q_done"], 1)
                dve.wait_ge(s["k_exp"], b + 1)
                nc.vector.scalar_tensor_tensor(kv[:, 0:NT, 0:128], kps[:, :, 0:128], 0.0, ke, ALU.max, ALU.add)\
                    .then_inc(s["k_done"], 1)
                dve.wait_ge(s["sums_ps"], b + 1)
                nc.vector.tensor_tensor(kvm, m.psum[:, 3, 0:128], m.block8[:], ALU.mult)
                nc.vector.tensor_tensor(ksm, m.psum[:, 4, 0:128], m.block8[:], ALU.mult).then_inc(s["sums_done"], 1)
                dve.wait_ge(s["num_ps"], b + 1)
                step.link(nc.vector.tensor_scalar(rden, m.psum[:, 5, :], 1e-6, None, ALU.add))
                step.link(nc.vector.reciprocal(rden, rden))
                if b:
                    dve.wait_ge(s["y_ps"], b)
                nc.vector.tensor_tensor(o, m.psum[:, 6, :], rden, ALU.mult).then_inc(s["o_done"], 1)
                dve.wait_ge(s["y_ps"], b + 1)
                nc.vector.scalar_tensor_tensor(m.s[:, b * CH:(b + 1) * CH], m.psum[:, 7, :], bo,
                                               m.x[:, b * CH:(b + 1) * CH], ALU.add, ALU.add)


class SoftmaxShape:

    def __init__(self, rows, stacks, causal, split, y_scale):
        self.rows, self.stacks, self.causal, self.split, self.y_scale = rows, stacks, causal, split, y_scale
        self.rope = not split
        self.per_stack = P // rows
        self.side_by_side = self.per_stack
        self.v_cols = rows if self.rope else P
        at = 0
        self.at = {}
        for name, width in (("k", P), ("kr", P * self.rope), ("q", P * stacks), ("qr", P * stacks * self.rope),
                            ("v", self.v_cols), ("wo", P * stacks)):
            self.at[name] = at
            at += width
        self.cols, self.early = at, self.at["wo"]


GROUPS = 4
UNITS = 16


def softmax_attention_stage(nc, m, sh, weights, first_group):
    NT = S // P
    tiles = lambda u: (tile(u) + 1) if sh.causal else NT
    C = sh.side_by_side
    head = lambda u: u // (C * NT) * C + u % C
    TILES = (0, 3, 1, 2) if sh.causal else range(NT)
    tile = lambda u: TILES[u % (C * NT) // C]
    stack = lambda u: head(u) // sh.per_stack
    rows = lambda u: slice(head(u) % sh.per_stack * sh.rows, (head(u) % sh.per_stack + 1) * sh.rows)
    per_stack_units = sh.per_stack * NT
    PROJ = sh.stacks + 2
    ROPES = PROJ - 1
    T_BANK, O_BANK, W_BANK = 3, 5, 6
    steps = GROUPS * B
    FREE = 8
    IL, TL, VL = (1, 3, 4) if sh.rope else (1, 3, 5)
    PROJ_AT = [8, 10, 12, 14] if sh.rope else [8, 11, 13]
    OUT_AT, ADD_AT = UNITS + VL + 1, UNITS + VL + 2
    START = ADD_AT + 1 - UNITS

    def col(slot, name, k=0, width=P):
        return m.w[:, slot, sh.at[name] + k * P:sh.at[name] + k * P + width]

    wo = lambda slot, k: m.late[:, slot, k * P:(k + 1) * P]
    hb = lambda slot: m.hb[:, slot, :]
    if sh.split:
        kT, qT = (lambda slot: m.parts[:, slot, :]), (lambda slot, k: m.parts[:, 2 + slot, :])
    else:
        kT = lambda slot: m.tmp1[:, slot * CH:(slot + 1) * CH]
        qT = lambda slot, k: m.tmp2[:, (2 * slot + k) * CH:(2 * slot + k + 1) * CH]
    rounded = lambda k: m.parts[:, 4 + k, :]
    split = lambda k: m.split["k" if k == 0 else sh.split]
    v = lambda slot: m.tmp1[:, 1024 + slot * CH:1024 + slot * CH + NT * sh.v_cols].rearrange("p (t n) -> p t n", t=NT)
    ropes = lambda i: m.positions[:, i * CH:(i + 1) * CH]
    rotated = lambda k: m.big[:, k * CH:(k + 1) * CH]
    oT = lambda k: m.tmp4[:, k * CH:(k + 1) * CH]
    pT = lambda u: m.gates[:, u % (2 * C) // 4, u % 4 * CH:u % 4 * CH + tiles(u) * P]
    if sh.rope:
        bank = lambda u: u % 3 if u < UNITS - 1 else 1
    else:
        bank = lambda u: (0, 1, 2, 7)[u % 4]
    s_before = lambda u: next(d for d in range(1, UNITS) if bank((u - d) % UNITS) == bank(u))
    scores_ps = lambda u: m.psum[:, bank(u), 0:tiles(u) * P]
    P_SLOTS = 4 if sh.rope else 8
    p_at = lambda u: m.p[:, u % 4, :] if u % P_SLOTS < 4 else m.big[:, u % 4 * CH:(u % 4 + 1) * CH]
    p = lambda u: p_at(u)[:, 0:tiles(u) * P]
    neg_max, row_sum, row_inv = m.small[:, 0:16], m.small[:, 16:32], m.small[:, 32:48]

    with stage(nc, "early0 early1 late0 late1 proj_ps rounded proj_read rope_done s_ready max_ready exp_done inv_ready p_ready t_ready "
                   "pt_by_act pt_by_dve pv_done o_done y_ready y_done") as (block, s):
        early, late = (s["early0"], s["early1"]), (s["late0"], s["late1"])

        def unit_of(n, j):
            return (n, j) if j < UNITS else (n + 1, j - UNITS)

        def wait_pt(eng, n, u):
            eng.wait_ge((s["pt_by_act"], s["pt_by_dve"])[u % 2], n * (UNITS // 2) + u // 2 + 1 + FREE)

        @block.sync
        def _(sp):
            packed = lambda g, c: weights[bass.ds(first_group + g, 1)][:, :, c].rearrange("o p n -> p (o n)")

            def load_early(g, b, slot):
                sp.dma_start(m.w[:, slot, 0:sh.early], packed(g, slice(0, sh.early))).then_inc(early[slot], 16)
                sp.dma_start(hb(slot), m.h[:, bass.ds(b * CH, CH)]).then_inc(early[slot], 16)

            def load_late(g, slot):
                sp.dma_start(m.late[:, slot, 0:sh.cols - sh.early], packed(g, slice(sh.early, sh.cols)))\
                    .then_inc(late[slot], 16)

            for slot in range(2):
                load_early(0, slot, slot)
                load_late(0, slot)
            sp.wait_ge(s["proj_read"], PROJ)
            load_early(0, 2, 0)
            with sp.Fori(0, GROUPS) as g:
                for b in range(B):
                    n = 4 * g + b
                    sp.wait_ge(s["proj_read"], PROJ * (n + 2))
                    load_early(g + (b + 3) // B, (b + 3) % B, (b + 1) % 2)
                    sp.wait_ge(s["y_ready"], n + 1 + 1)
                    load_late(g + (b + 2) // B, b % 2)
            for slot in range(2):
                sp.wait_ge(early[slot], 32 * (2 * GROUPS + 2 - slot))
                sp.wait_ge(late[slot], 16 * (2 * GROUPS + 1))

        @block.tensor
        def _(pe):
            def project(n, r, slot, k):
                if k == 0:
                    pe.wait_ge(early[slot], 32 * r + 32)
                    if not isinstance(n, int):
                        pe.wait_ge(s["y_done"], n)
                else:
                    pe.wait_ge(s["proj_read"], PROJ * n + k)
                if k == PROJ - 1:
                    for t in range(NT):
                        last = nc.tensor.matmul(m.psum[:, W_BANK, t * sh.v_cols:(t + 1) * sh.v_cols],
                                                hb(slot)[:, t * P:(t + 1) * P],
                                                col(slot, "v", width=sh.v_cols), start=True, stop=True)
                else:
                    a, b = ("k", 0) if k == 0 else ("q", k - 1)
                    last = nc.tensor.matmul(m.psum[:, W_BANK, :], col(slot, a, b), hb(slot), start=True, stop=True)
                    if sh.rope:
                        last = nc.tensor.matmul(m.psum[:, W_BANK + 1, :], col(slot, a + "r", b), hb(slot),
                                                start=True, stop=True)
                last.then_inc(s["proj_ps"], 1)

            def scores(n, u, slot):
                if u == 0:
                    if sh.rope:
                        pe.wait_ge(s["rope_done"], ROPES * n + ROPES)
                    pe.wait_ge(s["proj_read"], PROJ * n + PROJ)
                pe.wait_ge(s["exp_done"], UNITS * n + u - s_before(u) + 1 + FREE)
                out, w = scores_ps(u), tiles(u) * P
                last = nc.tensor.matmul(out, qT(slot, stack(u))[rows(u), tile(u) * P:(tile(u) + 1) * P],
                                        kT(slot)[rows(u), 0:w], start=True, stop=not sh.causal)
                if sh.causal:
                    last = nc.tensor.matmul(out[:, w - P:w], m.ident_bf[:], m.causal_bf[:], start=False, stop=True)
                last.then_inc(s["s_ready"], 1)

            def transposes(n, u):
                pe.wait_ge(s["p_ready"], UNITS * n + u + 1)
                pe.wait_ge((s["pt_by_act"], s["pt_by_dve"])[u % 2], n * (UNITS // 2) + u // 2 + FREE)
                for t in range(tiles(u)):
                    last = nc.tensor.transpose(m.psum[:, T_BANK + u % 2, t * P:(t + 1) * P],
                                               p(u)[:, t * P:(t + 1) * P], m.ident[:])
                last.then_inc(s["t_ready"], 1)

            def values(n, u, slot):
                if (u + 1) % C:
                    return
                units = range(u + 1 - C, u + 1)
                if units[0] % per_stack_units == 0:
                    pe.wait_ge(s["o_done"], sh.stacks * n + stack(u) + 1)
                for i in units[-2:]:
                    wait_pt(pe, n, i)
                for t in range(tiles(u)):
                    for i in units:
                        c = slice(0, sh.rows) if sh.rope else rows(i)
                        last = nc.tensor.matmul(m.psum[rows(i), O_BANK, tile(i) * P:(tile(i) + 1) * P],
                                                v(slot)[:, t, c], pT(i)[:, t * P:(t + 1) * P],
                                                start=t == 0, stop=t == tiles(i) - 1)
                last.then_inc(s["pv_done"], C)

            for k in range(PROJ):
                project(0, 0, 0, k)
            def position(n, r, slot, j):
                scores(*unit_of(n, j), slot if j < UNITS else 1 - slot)
                if j >= TL:
                    transposes(*unit_of(n, j - TL))
                if j >= VL:
                    values(*unit_of(n, j - VL), slot if j - VL < UNITS else 1 - slot)
                if j in PROJ_AT:
                    project(n + 1, r + slot, 1 - slot, PROJ_AT.index(j))
                if j == OUT_AT:
                    pe.wait_ge(late[slot], 16 * r + 16)
                    for k in range(sh.stacks):
                        pe.wait_ge(s["o_done"], sh.stacks * n + k + 2)
                        last = nc.tensor.matmul(m.psum[:, W_BANK, :], wo(slot, k), oT(k),
                                                start=k == 0, stop=k == sh.stacks - 1)
                    last.then_inc(s["y_ready"], 1)

            for j in range(START):
                position(0, 0, 0, j)
            with pe.Fori(0, steps // 2) as r:
                for slot in range(2):
                    for j in range(START, UNITS + START):
                        position(2 * r + slot, r, slot, j)

        @block.scalar
        def _(act):
            nc.scalar.preload_act_table_set("natural_log_exp_and_others")
            def exponential(n, u):
                act.wait_ge(s["max_ready"], UNITS * n + u + 1)
                act.wait_ge(s["t_ready"], UNITS * n + u - P_SLOTS + 1 + FREE)
                nc.scalar.activation(p(u), scores_ps(u), ACT.Exp,
                                     bias=neg_max[:, u:u + 1], accum_out=row_sum[:, u:u + 1])\
                    .then_inc(s["exp_done"], 1)

            def evacuate(n, u):
                act.wait_ge(s["t_ready"], UNITS * n + u + 1 + FREE)
                act.wait_ge(s["pv_done"], UNITS * n + u - 2 * C + 1 + FREE)
                nc.scalar.copy(pT(u), m.psum[:, T_BANK + u % 2, 0:tiles(u) * P]).then_inc(s["pt_by_act"], 1)

            def round_(n, k):
                act.wait_ge(s["proj_ps"], PROJ * n + k + 1)
                if not isinstance(n, int):
                    act.wait_ge(s["proj_read"], PROJ * (n - 1) + k + 1)
                nc.scalar.activation(rounded(k), m.psum[:, W_BANK, :], ACT.Identity, scale=split(k)[:, 0:1])\
                    .then_inc(s["rounded"], 1)

            act.sem_inc(s["exp_done"], FREE)
            act.sem_inc(s["pt_by_act"], FREE)
            if sh.split:
                round_(0, 0)
                round_(0, 1)
            for j in range(START):
                exponential(0, j)
                if j >= TL and (j - TL) % 2 == 0:
                    evacuate(0, j - TL)
            with act.Fori(0, steps // 2) as r:
                for slot in range(2):
                    n = 2 * r + slot
                    for j in range(START, UNITS + START):
                        exponential(*unit_of(n, j))
                        if sh.split and j - 1 in PROJ_AT[:2]:
                            round_(n + 1, PROJ_AT.index(j - 1))
                        if (j - TL) % 2 == 0:
                            evacuate(*unit_of(n, j - TL))

        @block.gpsimd
        def _(pool):
            def add_rotated(n, slot, k):
                pool.wait_ge(s["proj_read"], PROJ * n + k + 1)
                out = kT(slot) if k == 0 else qT(slot, k - 1)
                nc.gpsimd.tensor_tensor(out, out, rotated(k), ALU.add).then_inc(s["rope_done"], 1)

            def normalise(n, u):
                pool.wait_ge(s["inv_ready"], UNITS * n + u + 1)
                nc.gpsimd.tensor_tensor(p(u), p(u), row_inv[:, u:u + 1].to_broadcast([P, tiles(u) * P]), ALU.mult)\
                    .then_inc(s["p_ready"], 1)

            if sh.rope:
                for k in range(ROPES):
                    add_rotated(0, 0, k)
            for j in range(START - 1):
                normalise(0, j)
            with pool.Fori(0, steps // 2) as r:
                for slot in range(2):
                    for j in range(START - 1, UNITS + START - 1):
                        normalise(*unit_of(2 * r + slot, j))
                        if sh.rope and j - 1 in PROJ_AT[:ROPES]:
                            add_rotated(2 * r + slot + 1, 1 - slot, PROJ_AT.index(j - 1))

        @block.vector
        def _(dve):
            w0, w1 = m.psum[:, W_BANK, :], m.psum[:, W_BANK + 1, :]

            def projected(n, slot, k):
                dve.wait_ge(s["proj_ps"], PROJ * n + k + 1)
                if k == PROJ - 1:
                    last = nc.vector.tensor_copy(v(slot), w0[:, 0:NT * sh.v_cols].rearrange("p (t n) -> p t n", t=NT))
                elif sh.rope:
                    out, tab = (kT(slot), 0) if k == 0 else (qT(slot, k - 1), 2)
                    if not isinstance(n, int):
                        dve.wait_ge(s["rope_done"], ROPES * (n - 1) + k + 1)
                    nc.vector.tensor_tensor(out, w0, ropes(tab), ALU.mult)
                    last = nc.vector.tensor_tensor(rotated(k), w1, ropes(tab + 1), ALU.mult)
                else:
                    dve.wait_ge(s["rounded"], 2 * n + k + 1)
                    last = nc.vector.scalar_tensor_tensor(kT(slot) if k == 0 else qT(slot, k - 1), w0,
                                                          split(k)[:, 1:2], rounded(k), ALU.mult, ALU.add)
                last.then_inc(s["proj_read"], 1)

            def maximum(n, u):
                dve.wait_ge(s["s_ready"], UNITS * n + u + 1)
                nc.vector.tensor_reduce(neg_max[:, u:u + 1], scores_ps(u), AX.X, ALU.max, negate=True)\
                    .then_inc(s["max_ready"], 1)

            def inverse(n, u):
                dve.wait_ge(s["exp_done"], UNITS * n + u + 1 + FREE)
                nc.vector.reciprocal(row_inv[:, u:u + 1], row_sum[:, u:u + 1]).then_inc(s["inv_ready"], 1)

            def evacuate(n, u):
                dve.wait_ge(s["t_ready"], UNITS * n + u + 1 + FREE)
                dve.wait_ge(s["pv_done"], UNITS * n + u - 2 * C + 1 + FREE)
                nc.vector.tensor_copy(pT(u), m.psum[:, T_BANK + u % 2, 0:tiles(u) * P]).then_inc(s["pt_by_dve"], 1)

            def step(r, slot, b):
                n = 2 * r + slot
                for j in range(START, UNITS + START):
                    maximum(*unit_of(n, j))
                    inverse(*unit_of(n, j - IL))
                    if (j - TL) % 2 == 1:
                        evacuate(*unit_of(n, j - TL))
                    if j - 1 in PROJ_AT:
                        projected(n + 1, 1 - slot, PROJ_AT.index(j - 1))
                    if j <= UNITS + VL and (j - VL) % per_stack_units == 0:
                        u = j - VL - 1
                        dve.wait_ge(s["pv_done"], UNITS * n + u + 1 + FREE)
                        if stack(u) == 0:
                            dve.wait_ge(s["y_ready"], n + 1)
                        nc.vector.tensor_copy(oT(stack(u)), m.psum[:, O_BANK, :]).then_inc(s["o_done"], 1)
                    if j == ADD_AT:
                        dve.wait_ge(s["y_ready"], n + 1 + 1)
                        xb = m.x[:, bass.ds(b * CH, CH)]
                        nc.vector.scalar_tensor_tensor(xb, w0, sh.y_scale, xb, ALU.mult, ALU.add)\
                            .then_inc(s["y_done"], 1)
                        dve.wait_ge(s["y_done"], n + 2)

            for name, credit in (("o_done", 1), ("y_done", 1), ("y_ready", 1), ("t_ready", FREE), ("pv_done", FREE),
                                 ("pt_by_dve", FREE)):
                dve.sem_inc(s[name], credit)
            for k in range(PROJ):
                projected(0, 0, k)
            for j in range(START):
                maximum(0, j)
                if j >= IL:
                    inverse(0, j - IL)
                if j >= TL and (j - TL) % 2 == 1:
                    evacuate(0, j - TL)
            with dve.Fori(0, GROUPS) as g:
                for b in range(B):
                    step(2 * g + b // 2, b % 2, b)


NE, NT_ALL = 8, T // P


def router_stage(nc, m, kind, weights, scratch):
    v3 = lambda k: m.big[:, k * 128:(k + 1) * 128].rearrange("p (t e) -> p t e", e=NE)
    lg, eq, cand, oh1, oh2, l2 = (v3(k) for k in range(6))
    comb = m.big[:, 768:896]
    col = lambda k: m.small[:, 64 + 16 * k:80 + 16 * k]
    m1, m2, first, d, w1, w2, z, p1, p2 = (col(k) for k in range(9))
    over_e = lambda c: c.rearrange("p (t o) -> p t o", o=1).to_broadcast([P, NT_ALL, NE])
    iota = m.iota8.rearrange("p (o e) -> p o e", o=1).to_broadcast([P, NT_ALL, NE])
    n_w = 512 if kind == "norm" else NE
    load_columns(nc, [(m.w[:, 0, 0:n_w], weights)])
    with stage(nc, "logits squared sums root top exps probs comb comb_t comb_s stored v_step a_step") as (block, s):
        @block.tensor
        def _(pe):
            for t in range(NT_ALL):
                out = m.psum[:, 0, t * NE:(t + 1) * NE]
                if kind == "norm":
                    out = m.psum[:, t % 4, :]
                    if t >= 4:
                        pe.wait_ge(s["squared"], t - 3)
                nc.tensor.matmul(out, m.h[:, t * P:(t + 1) * P], m.w[:, 0, 0:n_w], start=True, stop=True)\
                    .then_inc(s["logits"], 1)
            pe.wait_ge(s["comb"], 1)
            nc.tensor.transpose(m.psum[:, 4, 0:128], comb, m.ident[:]).then_inc(s["comb_t"], 1)

        @block.scalar
        def _(act):
            if kind == "norm":
                for t in range(NT_ALL):
                    act.wait_ge(s["logits"], t + 1)
                    if t >= 4:
                        act.wait_ge(s["sums"], t - 3)
                    nc.scalar.activation(m.tmp1[:, t % 4 * CH:t % 4 * CH + CH], m.psum[:, t % 4, :], ACT.Square)\
                        .then_inc(s["squared"], 1)
                act.wait_ge(s["sums"], NT_ALL)
                nc.scalar.activation(lg, lg, ACT.Sqrt).then_inc(s["root"], 1)
            act.wait_ge(s["top"], 1)
            if kind == "double":
                nc.scalar.activation(eq, eq, ACT.Exp)
            nc.scalar.activation(d, d, ACT.Exp).then_inc(s["exps"], 1)
            if kind == "double":
                act.wait_ge(s["probs"], 1)
                nc.scalar.activation(d, d, ACT.Exp).then_inc(s["exps"], 1)

        @block.vector
        def _(dve):
            link = Chain(dve, s["v_step"]).link
            if kind == "norm":
                for t in range(NT_ALL):
                    dve.wait_ge(s["squared"], t + 1)
                    sq = m.tmp1[:, t % 4 * CH:t % 4 * CH + CH].rearrange("p (e r) -> p e r", e=NE)
                    nc.vector.tensor_reduce(lg[:, t, :], sq, AX.X, ALU.add).then_inc(s["sums"], 1)
                dve.wait_ge(s["root"], 1)
            else:
                dve.wait_ge(s["logits"], NT_ALL)
                link(nc.vector.tensor_copy(lg, m.psum[:, 0, 0:128].rearrange("p (t e) -> p t e", e=NE)))

            def best(src, largest, onehot):
                link(nc.vector.tensor_reduce(largest, src, AX.X, ALU.max))
                link(nc.vector.tensor_tensor(eq, src, over_e(largest), ALU.is_ge))
                link(nc.vector.tensor_tensor(cand, eq, iota, ALU.mult))
                link(nc.vector.tensor_reduce(first, cand, AX.X, ALU.min))
                link(nc.vector.tensor_tensor(onehot, cand, over_e(first), ALU.is_equal))

            best(lg, m1, oh1)
            link(nc.vector.scalar_tensor_tensor(l2, oh1, -1e30, lg, ALU.mult, ALU.add))
            best(l2, m2, oh2)
            if kind == "double":
                link(nc.vector.tensor_tensor(eq, lg, over_e(m1), ALU.subtract))
            link(nc.vector.tensor_tensor(d, m2, m1, ALU.subtract))
            dve.sem_inc(s["top"], 1)
            dve.wait_ge(s["exps"], 1)
            if kind == "double":
                link(nc.vector.tensor_reduce(z, eq, AX.X, ALU.add))
                link(nc.vector.reciprocal(p1, z))
                link(nc.vector.tensor_tensor(p2, d, p1, ALU.mult))
                link(nc.vector.tensor_tensor(d, p2, p1, ALU.subtract))
                dve.sem_inc(s["probs"], 1)
                dve.wait_ge(s["exps"], 2)
            link(nc.vector.tensor_scalar(w1, d, 1.0, None, ALU.add))
            link(nc.vector.reciprocal(w1, w1))
            link(nc.vector.tensor_tensor(w2, d, w1, ALU.mult))
            link(nc.vector.tensor_tensor(oh1, oh1, over_e(w1), ALU.mult))
            link(nc.vector.tensor_tensor(oh2, oh2, over_e(w2), ALU.mult))
            nc.vector.tensor_tensor(comb.rearrange("p (e t) -> p t e", e=NE), oh1, oh2, ALU.add).then_inc(s["comb"], 1)
            dve.wait_ge(s["comb_t"], 1)
            nc.vector.tensor_copy(m.big[:, 896:1024], m.psum[:, 4, 0:128]).then_inc(s["comb_s"], 1)

        @block.sync
        def _(sp):
            sp.wait_ge(s["comb_s"], 1)
            sp.dma_start(scratch.rearrange("e (t k) -> (e t) k", k=P), m.big[:, 896:1024]).then_inc(s["stored"], 16)
            sp.wait_ge(s["stored"], 16)


class ExpertShape:

    def __init__(self, kind):
        self.kind = kind
        self.tiles = {"gated": 2, "lowrank": 2, "gelu": 4, "ffn": 4}[kind]
        wide = self.tiles * P
        parts = {"gated": (("g", wide), ("u", wide), ("d", wide)),
                 "lowrank": (("a", 64), ("g", wide), ("u", wide), ("d", wide)),
                 "gelu": (("g", wide), ("d", wide), ("b1", 4), ("b2", 1))}[{"ffn": "gelu"}.get(kind, kind)]
        self.at, at = {}, 0
        for name, width in parts:
            self.at[name] = at
            at += width
        self.cols = at


def experts_stage(nc, m, sh, weights, first, scratch):
    split = sh.kind != "lowrank"
    FT, LAG = sh.tiles, {"gated": 3, "lowrank": 2}.get(sh.kind, 4)
    U = NC * FT
    PAIRS = 2 if sh.kind == "lowrank" else 3
    gelu, low = sh.kind in ("gelu", "ffn"), sh.kind == "lowrank"
    single = sh.kind == "ffn"
    SLOTS = 1 if single else 2
    rounds = lambda eng: nullcontext(0) if single else eng.Fori(0, NE // 2)
    per_load = 16 if single else 32
    w = lambda slot, name, f=0, width=P: m.w[:, slot, sh.at[name] + f * P:sh.at[name] + f * P + width]
    h = lambda c: m.h[:, c * CH:(c + 1) * CH]
    g_bank = lambda k: m.psum[:, 2 * (k % PAIRS), :]
    u_bank = lambda k: m.psum[:, 2 * (k % PAIRS) + 1, :]
    y_bank = lambda c: m.psum[:, 6 + c % 2, :]
    low_bank = lambda c: m.psum[0:64, 4 + c % 2, :]
    low_sb = lambda c: m.tmp4[0:64, c % 2 * CH:(c % 2 + 1) * CH]
    gate_act = lambda k: m.tmp1[:, k % 3 * CH:(k % 3 + 1) * CH]
    SLOTS_H = 4 if split else 3
    ring = lambda t, k: t[:, k % SLOTS_H * CH:(k % SLOTS_H + 1) * CH]
    hidden = lambda k: ring(m.tmp2, k)
    SLOTS_P = 3
    hidden_part = lambda i, k: m.parts[:, 3 * i + k % SLOTS_P, :]
    h_part = lambda i, c: m.h_parts[:, 4 * i + c, :]
    w_cols = sh.at["d"] + FT * P
    w_part = lambda i, slot, name, f: m.w_parts[:, 2 * slot + i, sh.at[name] + f * P:sh.at[name] + (f + 1) * P]
    PAIRED = ((0, 0), (0, 1), (1, 0))
    part = lambda c: m.tmp3[:, c % 2 * CH:(c % 2 + 1) * CH]
    with stage(nc, "loaded0 loaded1 low_ps low_done gu_ps act_done h_done y_mm y_done acc_done "
                   "w_rounded w_split h_rounded h_split hidden_rounded hidden_split") as (block, s):
        loaded = (s["loaded0"], s["loaded1"])

        @block.sync
        def _(sp):
            def load(e, slot):
                sp.dma_start(m.w[:, slot, 0:sh.cols], weights[bass.ds(first + e, 1)].rearrange("o p n -> p (o n)"))\
                    .then_inc(loaded[slot], 16)
                if single:
                    return
                sp.dma_start(m.gates[:, slot, :], scratch[bass.ds(e, 1)].to_broadcast([P, T])).then_inc(loaded[slot], 16)

            for slot in range(SLOTS):
                load(slot, slot)
            if single:
                return
            with sp.Fori(0, NE // 2 - 1) as r:
                for slot in range(2):
                    sp.wait_ge(s["acc_done"], NC * (2 * r + slot + 1) + 1)
                    load(2 * r + 2 + slot, slot)
            if split:
                sp.wait_ge(s["acc_done"], NC * (NE - 1) + 1)
                load(NE - 2, 0)

        @block.tensor
        def _(pe):
            with rounds(pe) as r:
                for slot in range(SLOTS):
                    e = 2 * r + slot
                    if split:
                        pe.wait_ge(s["w_split"], e + 1)
                    else:
                        pe.wait_ge(loaded[slot], per_load * r + per_load)

                    def product(bank, name, f, values, first, last):
                        for i, (a, b) in enumerate(PAIRED):
                            ins = nc.tensor.matmul(bank, w_part(a, slot, name, f), values(b),
                                                   start=first and i == 0, stop=last and i == 2)
                        return ins

                    def low_rank(c):
                        if c >= 2:
                            pe.wait_ge(s["low_done"], NC * e + c - 1)
                        nc.tensor.matmul(low_bank(c), w(slot, "a", width=64), h(c), start=True, stop=True)\
                            .then_inc(s["low_ps"], 1)

                    for k in range(U + LAG):
                        c, f = k // FT, k % FT
                        if k < U:
                            if low and f == 0:
                                if c == 0:
                                    low_rank(0)
                                if c + 1 < NC:
                                    low_rank(c + 1)
                                pe.wait_ge(s["low_done"], NC * e + c + 1)
                            if k >= PAIRS:
                                pe.wait_ge(s["h_done"], U * e + k - PAIRS + 1)
                            if split:
                                if slot == 0 and f == 0:
                                    pe.wait_ge(s["h_split"], c + 1)
                                last = product(g_bank(k), "g", f, lambda i: h_part(i, c), True, True)
                                if not gelu:
                                    last = product(u_bank(k), "u", f, lambda i: h_part(i, c), True, True)
                            elif low:
                                last = nc.tensor.matmul(g_bank(k), w(slot, "g", f)[0:64], low_sb(c), start=True, stop=True)
                            if not split:
                                last = nc.tensor.matmul(u_bank(k), w(slot, "u", f), h(c), start=True, stop=True)
                            last.then_inc(s["gu_ps"], 1)
                        k -= LAG
                        if k >= 0:
                            c, f = k // FT, k % FT
                            if f == 0:
                                pe.wait_ge(s["y_done"], NC * e + max(c - 1, 0) + 1)
                            if split:
                                pe.wait_ge(s["hidden_split"], U * e + k + 1)
                                last = product(y_bank(c), "d", f, lambda i: hidden_part(i, k), f == 0, f == FT - 1)
                            else:
                                pe.wait_ge(s["h_done"], U * e + k + 1)
                                last = nc.tensor.matmul(y_bank(c), w(slot, "d", f), hidden(k), start=f == 0,
                                                        stop=f == FT - 1)
                            last.then_inc(s["y_mm"], 1)

        @block.scalar
        def _(act):
            def round_weights(r, slot):
                act.wait_ge(loaded[slot], per_load * r + per_load)
                nc.scalar.copy(m.w_parts[:, 2 * slot, 0:w_cols], m.w[:, slot, 0:w_cols]).then_inc(s["w_rounded"], 1)

            def round_hidden(e, k):
                act.wait_ge(s["h_done"], U * e + k + 1)
                if k >= SLOTS_P:
                    act.wait_ge(s["y_mm"], U * e + k - SLOTS_P + 1)
                nc.scalar.copy(hidden_part(0, k), hidden(k)).then_inc(s["hidden_rounded"], 1)

            if split:
                for c in range(NC):
                    nc.scalar.copy(h_part(0, c), h(c)).then_inc(s["h_rounded"], 1)
                    if c == 0:
                        round_weights(0, 0)
            with rounds(act) as r:
                for slot in range(SLOTS):
                    e = 2 * r + slot
                    for k in range(U):
                        act.wait_ge(s["gu_ps"], U * e + k + 1)
                        if gelu:
                            if k >= SLOTS_H:
                                act.wait_ge(s["hidden_split"], U * e + k - SLOTS_H + 1)
                            nc.scalar.activation(hidden(k), g_bank(k), ACT.Silu if single else ACT.Gelu, bias=w(slot, "b1")[:, k % FT:k % FT + 1])\
                                .then_inc(s["h_done"], 1)
                        else:
                            if k >= 3:
                                act.wait_ge(s["h_done"], U * e + k - 2)
                            nc.scalar.activation(gate_act(k), g_bank(k), ACT.Silu).then_inc(s["act_done"], 1)
                        if split:
                            if k:
                                round_hidden(e, k - 1)
                            if k == U // 2 and not single:
                                round_weights(r + slot, 1 - slot)
                    if split:
                        round_hidden(e, U - 1)

        @block.vector
        def _(dve):
            dve.sem_inc(s["y_done"], 1)
            dve.sem_inc(s["acc_done"], 1)

            def rest_of_weights(e, slot):
                dve.wait_ge(s["w_rounded"], e + 1)
                nc.vector.tensor_tensor(m.w_parts[:, 2 * slot + 1, 0:w_cols], m.w[:, slot, 0:w_cols],
                                        m.w_parts[:, 2 * slot, 0:w_cols], ALU.subtract).then_inc(s["w_split"], 1)

            def rest_of_hidden(e, k):
                dve.wait_ge(s["hidden_rounded"], U * e + k + 1)
                nc.vector.tensor_tensor(hidden_part(1, k), hidden(k), hidden_part(0, k), ALU.subtract)\
                    .then_inc(s["hidden_split"], 1)

            if split:
                for c in range(NC):
                    dve.wait_ge(s["h_rounded"], c + 1)
                    nc.vector.tensor_tensor(h_part(1, c), h(c), h_part(0, c), ALU.subtract).then_inc(s["h_split"], 1)
                    if c == 0:
                        rest_of_weights(0, 0)
            with rounds(dve) as r:
                for slot in range(SLOTS):
                    e = 2 * r + slot

                    def low_copy(c):
                        dve.wait_ge(s["low_ps"], NC * e + c + 1)
                        if c >= 2:
                            dve.wait_ge(s["gu_ps"], U * e + (c - 1) * FT)
                        nc.vector.tensor_copy(low_sb(c), low_bank(c)).then_inc(s["low_done"], 1)

                    for k in range(U + LAG):
                        if low and k < U and k % FT == 0:
                            if k == 0:
                                low_copy(0)
                            elif k // FT >= 1:
                                low_copy(k // FT)
                        if k < U and not gelu:
                            dve.wait_ge(s["act_done"], U * e + k + 1)
                            if split and k >= SLOTS_H:
                                dve.wait_ge(s["hidden_split"], U * e + k - SLOTS_H + 1)
                            if not split and k >= 3:
                                dve.wait_ge(s["y_mm"], U * e + k - 2)
                            nc.vector.tensor_tensor(hidden(k), gate_act(k), u_bank(k), ALU.mult).then_inc(s["h_done"], 1)
                        if split and 1 <= k <= U:
                            rest_of_hidden(e, k - 1)
                        if split and k == U // 2 + 1 and not single:
                            rest_of_weights(e + 1, 1 - slot)
                        j = k - LAG
                        if j >= 0 and j % FT == FT - 1:
                            c = j // FT
                            dve.wait_ge(s["y_mm"], U * e + j + 1)
                            if c >= 2:
                                dve.wait_ge(s["acc_done"], NC * e + c)
                            else:
                                dve.wait_ge(s["acc_done"], NC * e + 1)
                            gate = m.gates[:, slot, c * CH:(c + 1) * CH]
                            if single:
                                last = nc.vector.tensor_scalar(part(c), y_bank(c), w(slot, "b2", width=1), None, ALU.add)
                            elif gelu:
                                last = nc.vector.scalar_tensor_tensor(part(c), y_bank(c), w(slot, "b2", width=1), gate,
                                                                      ALU.add, ALU.mult)
                            else:
                                last = nc.vector.tensor_tensor(part(c), y_bank(c), gate, ALU.mult)
                            last.then_inc(s["y_done"], 1)

        @block.gpsimd
        def _(pool):
            with rounds(pool) as r:
                for slot in range(SLOTS):
                    e = 2 * r + slot
                    for c in range(NC):
                        pool.wait_ge(s["y_done"], NC * e + c + 2)
                        acc = m.x[:, c * CH:(c + 1) * CH]
                        nc.gpsimd.tensor_tensor(acc, acc, part(c), ALU.add).then_inc(s["acc_done"], 1)


class CausalShape:

    def __init__(self, retention):
        self.retention = retention
        self.rows = 32 if retention else 64
        self.heads = P // self.rows
        self.groups = 2 if retention else 8
        names = "q qr k kr v wg wo" if retention else "q k v wo"
        self.at = {n: i * P for i, n in enumerate(names.split())}
        self.early = self.at["wo"]
        self.cols = len(self.at) * P + (2 if retention else 0)


def causal_attention_stage(nc, m, sh, weights, first_group, decays=None):
    NT, HEADS, G, ret = S // P, sh.heads, sh.groups, sh.retention
    U = HEADS * NT
    C = HEADS
    head = lambda u: u % C
    tile = (lambda u: u // C) if ret else (lambda u: (0, 3, 1, 2)[u // C])
    width = lambda u: (NT - tile(u)) * P
    rows = lambda u: slice(head(u) * sh.rows, (head(u) + 1) * sh.rows)
    BANKS, O_BANK, STAT_BANK = (4 if ret else 2), 3, 4 if ret else 6
    S_BANKS = (0, 1, 2, 5)[:BANKS]
    QK_BANK, V_BANK = (6, 6) if ret else (4, 2)
    LAG, FREE = (3 if ret else 2), 8
    NORMS = 1 if ret else 2
    PROJ = 3 if ret else 1
    heads_of = lambda t: t.rearrange("p (h n) -> p h n", n=64)
    V_STEPS = 4
    steps = G * B
    late_load = 32 if ret else 16
    col = lambda slot, name: m.w[:, slot, sh.at[name]:sh.at[name] + P]
    wo = lambda slot: m.late[:, slot, 0:P]
    norm_column = lambda slot, i: m.late[:, slot, P + i:P + i + 1]
    hb = lambda slot: m.hb[:, slot, :]
    part = lambda t, i: t[:, i * CH:(i + 1) * CH]
    qT, kT = (lambda slot: part(m.tmp1, slot)), (lambda slot: part(m.tmp1, 2 + slot))
    k_of = (lambda slot, h: m.by_head[:, 4 * slot + h, :]) if ret else (lambda slot, h: kT(slot)[rows(h)])
    q_of = (lambda slot, h: qT(slot)) if ret else (lambda slot, h: qT(slot)[rows(h)])
    v = lambda slot: part(m.tmp2, slot).rearrange("p (t n) -> p t n", t=NT)
    oT, gate = m.oT[:], lambda slot: part(m.tmp2, 2 + slot)
    sT_at = lambda u: (m.p[:, u % 4, :], part(m.big, u % 4))[u % (2 * C) // 4]
    sT = lambda u: sT_at(u)[:, 0:width(u)]
    sq, rstd = (lambda i: part(m.tmp3, i)), (lambda i: part(m.tmp3, 2 + i))
    stat_ps = lambda i: m.psum[:, STAT_BANK + i, :]
    s_bank = lambda u: m.psum[:, S_BANKS[u % BANKS], 0:width(u)]
    PE_FRONT = {10: "q", 12: "k", 14: "v", 15: "gate"} if ret else {1: "qk", 4: "variances", 5: "v"}
    DVE_FRONT = {11: "q", 13: "k", 15: "v"} if ret else {0: "weights", 5: "scale q", 6: "scale k", 7: "v"}
    PE_OUT = {LAG + 1: "mean", LAG + 2: "variance", LAG + 4: "out"} if ret else {LAG + 1: "out"}
    DVE_OUT = {LAG: "copy", LAG + 1: "centre", LAG + 3: "scale", LAG + 5: "add"} if ret else {LAG: "copy", LAG + 2: "add"}
    START = max(DVE_OUT) + 1
    xpos = lambda i: part(m.positions, i)
    table = lambda slot, u: (part(m.gates[:, slot, :], head(u))[:, 0:width(u)] if ret
                             else m.tri[:, 0:width(u)])
    qk_ps = (m.psum[:, QK_BANK, :], m.psum[:, QK_BANK + 1, :])
    block_mean = m.block16 if ret else m.block64
    with stage(nc, "early0 early1 late0 late1 weights_centred zeroed k_spread qk_ps proj_ps proj_done raw_ready mean_ps centred squared var_ps log_ready rstd_ready "
                   "normed s_ready s_done pv_done o_done gate_ps gate_done y_ready y_done v_step") as (block, s):
        early, late = (s["early0"], s["early1"]), (s["late0"], s["late1"])

        @block.sync
        def _(sp):
            packed = lambda g, c: weights[bass.ds(first_group + g, 1)][:, :, c].rearrange("o p n -> p (o n)")

            def load_early(g, b, slot):
                sp.dma_start(m.w[:, slot, 0:sh.early], packed(g, slice(0, sh.early))).then_inc(early[slot], 16)
                sp.dma_start(hb(slot), m.h[:, bass.ds(b * CH, CH)]).then_inc(early[slot], 16)

            def load_late(g, slot):
                sp.dma_start(m.late[:, slot, 0:sh.cols - sh.early], packed(g, slice(sh.early, sh.cols)))\
                    .then_inc(late[slot], 16)
                if ret:
                    sp.dma_start(m.gates[:, slot, :], decays[bass.ds(g, 1)].rearrange("o p n -> p (o n)"))\
                        .then_inc(late[slot], 16)

            for slot in range(2):
                load_early(0, slot, slot)
                load_late(0, slot)
            sp.wait_ge(s["proj_done"], PROJ)
            if ret:
                sp.wait_ge(s["gate_ps"], 1)
            load_early(0, 2, 0)
            with sp.Fori(0, G) as g:
                for b in range(B):
                    n = 4 * g + b
                    sp.wait_ge(s["proj_done"], PROJ * (n + 2))
                    if ret:
                        sp.wait_ge(s["gate_ps"], n + 2)
                    load_early(g + (b + 3) // B, (b + 3) % B, (b + 1) % 2)
                    sp.wait_ge(s["y_ready"], n + 1)
                    load_late(g + (b + 2) // B, b % 2)
            for slot in range(2):
                sp.wait_ge(early[slot], 32 * (2 * G + 2 - slot))
                sp.wait_ge(late[slot], late_load * (2 * G + 1))

        def unit_of(n, j):
            return (n, j) if j < U else (n + 1, j - U)

        def next_of(n, r, slot, j):
            return (n + 1, r + slot, 1 - slot) if j < U else (n + 2, r + 1, slot)

        first = lambda n: isinstance(n, int) and n == 0

        @block.tensor
        def _(pe):
            def mean(n, i, raw):
                pe.wait_ge(s["raw_ready"], NORMS * n + i + 1)
                nc.tensor.matmul(stat_ps(i), block_mean, raw, start=True, stop=True).then_inc(s["mean_ps"], 1)

            def variance(n, i):
                pe.wait_ge(s["squared"], NORMS * n + i + 1)
                nc.tensor.matmul(stat_ps(i), block_mean, sq(i), start=True, stop=True).then_inc(s["var_ps"], 1)

            def front(n, r, slot, what):
                if what == "qk":
                    pe.wait_ge(s["weights_centred"], n + 1)
                    if not first(n):
                        pe.wait_ge(s["normed"], NORMS * n)
                if what == "q":
                    pe.wait_ge(early[slot], 32 * r + 32)
                    if not first(n):
                        pe.wait_ge(s["gate_done"], n)
                if what == ("q" if ret else "v") and not first(n):
                    pe.wait_ge(s["y_done"], n)
                if what in ("q", "k", "qk"):
                    if what == "k":
                        pe.wait_ge(s["proj_done"], PROJ * n + 1)
                    for bank, name in enumerate({"q": ("q", "qr"), "k": ("k", "kr"), "qk": ("q", "k")}[what]):
                        last = nc.tensor.matmul(m.psum[:, QK_BANK + bank, :], col(slot, name), hb(slot),
                                                start=True, stop=True)
                    last.then_inc(s["proj_ps" if ret else "qk_ps"], 1)
                elif what == "v":
                    if ret:
                        pe.wait_ge(s["proj_done"], PROJ * n + PROJ - 1)
                    for t in range(NT):
                        last = nc.tensor.matmul(m.psum[:, V_BANK, t * P:(t + 1) * P], hb(slot)[:, t * P:(t + 1) * P],
                                                col(slot, "v"), start=True, stop=True)
                    last.then_inc(s["proj_ps"], 1)
                elif what == "gate":
                    nc.tensor.matmul(m.psum[:, QK_BANK + 1, :], col(slot, "wg"), hb(slot), start=True, stop=True)\
                        .then_inc(s["gate_ps"], 1)
                else:
                    for i in range(2):
                        variance(n, i)

            def scores(n, u, slot):
                if u == 0:
                    if ret:
                        pe.wait_ge(s["proj_done"], PROJ * n + 2)
                    else:
                        pe.wait_ge(s["normed"], NORMS * n + NORMS)
                if ret and u < HEADS:
                    pe.wait_ge(s["k_spread"], HEADS * n + u + 1)
                pe.wait_ge(s["s_done"], U * n + u - BANKS + 1 + FREE)
                t = tile(u)
                nc.tensor.matmul(s_bank(u), k_of(slot, head(u))[:, t * P:(t + 1) * P],
                                 q_of(slot, head(u))[:, t * P:CH], start=True, stop=True).then_inc(s["s_ready"], 1)

            def values(n, u, slot):
                if (u + 1) % C:
                    return
                if u == C - 1:
                    pe.wait_ge(s["o_done"], n + 1)
                    pe.wait_ge(s["proj_done"], PROJ * n + PROJ)
                pe.wait_ge(s["s_done"], U * n + u + 1 + FREE)
                t = tile(u)
                for i in range(u + 1 - C, u + 1):
                    last = nc.tensor.matmul(m.psum[rows(i), O_BANK, t * P:CH], v(slot)[:, t, rows(i)], sT(i),
                                            start=u == C - 1, stop=u == U - 1)
                last.then_inc(s["pv_done"], C)

            def position(n, r, slot, j):
                scores(*unit_of(n, j), slot if j < U else 1 - slot)
                if j >= LAG:
                    values(*unit_of(n, j - LAG), slot if j - LAG < U else 1 - slot)
                if j % U in PE_FRONT:
                    front(*next_of(n, r, slot, j), PE_FRONT[j % U])
                what = PE_OUT.get(j - U)
                if what == "mean":
                    mean(n, 0, oT)
                elif what == "variance":
                    variance(n, 0)
                elif what == "out":
                    if ret:
                        pe.wait_ge(s["normed"], n + 1)
                    pe.wait_ge(s["o_done"], n + 2)
                    pe.wait_ge(s["proj_done"], PROJ * (n + 2))
                    pe.wait_ge(late[slot], late_load * (r + 1))
                    nc.tensor.matmul(m.psum[:, V_BANK, :], wo(slot), oT, start=True, stop=True)\
                        .then_inc(s["y_ready"], 1)

            for what in PE_FRONT.values():
                front(0, 0, 0, what)
            for j in range(START):
                position(0, 0, 0, j)
            with pe.Fori(0, steps // 2) as r:
                for slot in range(2):
                    for j in range(START, U + START):
                        position(2 * r + slot, r, slot, j)
            pe.wait_ge(s["s_done"], U * steps + START + FREE)
            for i in range(C):
                nc.tensor.matmul(m.psum[rows(i), O_BANK, 0:P], v(0)[:, 0, rows(i)], sT(i)[:, 0:P],
                                 start=False, stop=True)

        @block.scalar
        def _(act):
            nc.scalar.preload_act_table_set("natural_log_exp_and_others")
            def norms(n, which, xs):
                for i, x in zip(which, xs):
                    if ret:
                        act.wait_ge(s["centred"], NORMS * n + i + 1)
                    elif i == 0:
                        act.wait_ge(s["qk_ps"], n + 1)
                    nc.scalar.activation(sq(i), x, ACT.Square).then_inc(s["squared"], 1)
                for i in which:
                    act.wait_ge(s["var_ps"], NORMS * n + i + 1)
                    if not ret and not first(n):
                        act.wait_ge(s["normed"], NORMS * n)
                    nc.scalar.activation(rstd(i), stat_ps(i), ACT.Ln, bias=m.eps5).then_inc(s["log_ready"], 1)
                    act.wait_ge(s["log_ready"], NORMS * n + i + 1)
                    nc.scalar.activation(rstd(i), rstd(i), ACT.Exp, scale=-0.5).then_inc(s["rstd_ready"], 1)

            def silu(n, slot):
                act.wait_ge(s["gate_ps"], n + 1)
                nc.scalar.activation(gate(slot), m.psum[:, QK_BANK + 1, :], ACT.Silu).then_inc(s["gate_done"], 1)

            def spread_k(n, slot):
                act.wait_ge(s["proj_done"], PROJ * n + 2)
                if not first(n):
                    act.wait_ge(s["s_ready"], U * (n - 1) + 1)
                for h in range(HEADS):
                    nc.scalar.copy(k_of(slot, h)[rows(h)], kT(slot)[rows(h)]).then_inc(s["k_spread"], 1)

            if ret:
                act.wait_ge(s["zeroed"], 2 * HEADS)
                spread_k(0, 0)
                silu(0, 0)
            else:
                norms(0, (0, 1), qk_ps)
                norms(1, (0, 1), qk_ps)
            with act.Fori(0, steps // 2) as r:
                for slot in range(2):
                    n = 2 * r + slot
                    if ret:
                        spread_k(n + 1, 1 - slot)
                        silu(n + 1, 1 - slot)
                        nc.scalar.preload_act_table_set("natural_log_exp_and_others")
                        norms(n, (0,), (oT,))
                    else:
                        norms(n + 2, (0, 1), qk_ps)

        if ret:
            @block.gpsimd
            def _(pool):
                for i in range(2 * HEADS):
                    nc.gpsimd.memset(m.by_head[:, i, :], 0.0).then_inc(s["zeroed"], 1)

        @block.vector
        def _(dve):
            w0, w1 = m.psum[:, QK_BANK, :], m.psum[:, QK_BANK + 1, :]
            out_ps = m.psum[:, V_BANK, :]

            def centre(n, i, x):
                dve.wait_ge(s["mean_ps"], NORMS * n + i + 1)
                nc.vector.tensor_tensor(x, x, stat_ps(i), ALU.subtract).then_inc(s["centred"], 1)

            def scale(n, i, src, x, weight, bias, chain, slot):
                dve.wait_ge(s["rstd_ready"], NORMS * n + i + 1)
                chain.link(nc.vector.tensor_tensor(x, src, rstd(i), ALU.mult))
                last = nc.vector.tensor_scalar(x, x, weight, bias, ALU.mult, ALU.add)
                if ret:
                    chain.link(last)
                    last = nc.vector.tensor_tensor(x, x, gate(slot), ALU.mult)
                last.then_inc(s["normed"], 1)

            def front(n, r, slot, what, chain):
                if what in ("q", "k"):
                    i = "qk".index(what)
                    out = (qT(slot), kT(slot))[i]
                    dve.wait_ge(s["proj_ps"], PROJ * n + i + 1)
                    nc.vector.tensor_tensor(out, w0, xpos(2 * i), ALU.mult)
                    chain.link(nc.vector.tensor_tensor(m.rot[:], w1, xpos(2 * i + 1), ALU.mult))
                    nc.vector.tensor_tensor(out, out, m.rot[:], ALU.add).then_inc(s["proj_done"], 1)
                elif what == "weights":
                    dve.wait_ge(early[slot], 32 * r + 32)
                    w = heads_of(m.w[:, slot, 0:2 * P])
                    sums = m.small[:, 0:4]
                    chain.link(nc.vector.tensor_reduce(sums, w, AX.X, ALU.add))
                    chain.link(nc.vector.tensor_scalar(sums, sums, 1.0 / 64, None, ALU.mult))
                    nc.vector.tensor_tensor(w, w, sums.rearrange("p (h o) -> p h o", o=1).to_broadcast([P, 4, 64]),
                                            ALU.subtract).then_inc(s["weights_centred"], 1)
                elif what == "v":
                    dve.wait_ge(s["proj_ps"], PROJ * n + PROJ)
                    nc.vector.tensor_copy(v(slot), out_ps.rearrange("p (t n) -> p t n", t=NT))\
                        .then_inc(s["proj_done"], 1)
                else:
                    i, x = {"scale q": (0, qT(slot)), "scale k": (1, kT(slot))}[what]
                    scale(n, i, qk_ps[i], x, m.cols[:, 8 + 2 * i:9 + 2 * i], m.cols[:, 9 + 2 * i:10 + 2 * i], chain, slot)

            def weigh(n, r, u, slot):
                if ret and u == 0:
                    dve.wait_ge(late[slot], late_load * r + late_load)
                dve.wait_ge(s["s_ready"], U * n + u + 1)
                dve.wait_ge(s["pv_done"], U * n + u - 2 * C + 1 + FREE)
                nc.vector.tensor_tensor(sT(u), s_bank(u), table(slot, u), ALU.mult).then_inc(s["s_done"], 1)

            def position(n, r, slot, j, b, chain):
                if j % U in DVE_FRONT:
                    front(*next_of(n, r, slot, j), DVE_FRONT[j % U], chain)
                n_j, u = unit_of(n, j)
                weigh(n_j, r if j < U else r + slot, u, slot if j < U else 1 - slot)
                what = DVE_OUT.get(j - U)
                if what == "copy":
                    dve.wait_ge(s["pv_done"], U * n + U + FREE)
                    nc.vector.tensor_copy(oT, m.psum[:, O_BANK, :]).then_inc(s["o_done"], 1)
                    if ret:
                        dve.wait_ge(s["o_done"], n + 2)
                        dve.sem_inc(s["raw_ready"], 1)
                elif what == "centre":
                    centre(n, 0, oT)
                elif what == "scale":
                    dve.wait_ge(s["gate_done"], n + 1)
                    dve.wait_ge(s["centred"], n + 1)
                    scale(n, 0, oT, oT, norm_column(slot, 0), norm_column(slot, 1), chain, slot)
                elif what == "add":
                    dve.wait_ge(s["y_ready"], n + 1)
                    xb = m.x[:, bass.ds(b * CH, CH)]
                    nc.vector.tensor_tensor(xb, out_ps, xb, ALU.add).then_inc(s["y_done"], 1)
                    dve.wait_ge(s["y_done"], n + 2)

            def step(r, slot, b):
                n = 2 * r + slot
                chain = Chain(dve, s["v_step"], V_STEPS, n + 2)
                for j in range(START, U + START):
                    position(n, r, slot, j, b, chain)
                chain.close()

            dve.sem_inc(s["o_done"], 1)
            dve.sem_inc(s["y_done"], 1)
            for name in ("s_done", "pv_done"):
                dve.sem_inc(s[name], FREE)
            chain = Chain(dve, s["v_step"], 2 * V_STEPS)
            for what in DVE_FRONT.values():
                front(0, 0, 0, what, chain)
            for j in range(START):
                position(0, 0, 0, j, 0, chain)
            dve.sem_inc(s["v_step"], 2 * V_STEPS - chain.n)
            with dve.Fori(0, G) as g:
                for b in range(B):
                    step(2 * g + b // 2, b % 2, b)


def sign_projection_stage(nc, m, a):
    w = m.big[:, 0:128]
    y = lambda c: m.tmp1[:, c * CH:(c + 1) * CH]
    x = lambda c: m.x[:, c * CH:(c + 1) * CH]
    load_columns(nc, [(w, a["l3f_w"]), (m.cols[:, 0:2], a["l3f_scale_bias"])])
    with stage(nc, "signs y_ps v_step") as (block, s):
        @block.tensor
        def _(pe):
            pe.wait_ge(s["signs"], 1)
            for c in range(NC):
                nc.tensor.matmul(m.psum[:, c, :], w, x(c), start=True, stop=True).then_inc(s["y_ps"], 1)

        @block.vector
        def _(dve):
            link = Chain(dve, s["v_step"]).link
            link(nc.vector.tensor_scalar(w, w, 0.0, 2.0, ALU.is_ge, ALU.mult))
            link(nc.vector.tensor_scalar(w, w, -1.0, None, ALU.add))
            dve.sem_inc(s["signs"], 1)
            for c in range(NC):
                dve.wait_ge(s["y_ps"], c + 1)
                link(nc.vector.tensor_scalar(y(c), m.psum[:, c, :], m.cols[:, 0:1], m.cols[:, 1:2], ALU.mult, ALU.add))
                link(nc.vector.tensor_scalar(y(c), y(c), 100.0, -100.0, ALU.min, ALU.max))
                nc.vector.tensor_tensor(m.s[:, c * CH:(c + 1) * CH], x(c), y(c), ALU.add)


def build(nc, a, first=1, stages=99):
    with ExitStack() as held:
        def sb(name, shape, dt=F32):
            return held.enter_context(nc.sbuf_tensor(name, shape, dt))
        m = Memory()
        m.x, m.s, m.h = (sb(n, [P, T]) for n in ("x", "s", "h"))
        m.tmp1, m.tmp2, m.tmp3 = (sb(n, [P, T]) for n in ("tmp1", "tmp2", "tmp3"))
        m.tmp4 = sb("tmp4", [P, T])
        m.w = sb("w", [P, 2, 1536])
        m.hb = sb("hb", [P, 2, CH])
        m.p = sb("p", [P, 4, CH])
        m.gates = sb("gates", [P, 2, T])
        m.oT = sb("oT", [P, CH])
        m.late = sb("late", [P, 2, 258])
        m.rot = sb("rot", [P, CH])
        m.small = sb("small", [P, 512])
        m.const_bf = sb("const_bf", [P, 256], BF16)
        m.ident_bf, m.causal_bf = m.const_bf[:, 0:128], m.const_bf[:, 128:256]
        m.big = sb("big", [P, 2048])
        m.cols = sb("cols", [P, 64])
        m.w_parts = sb("w_parts", [P, 4, 1024], F32R)
        m.h_parts = sb("h_parts", [P, 8, CH], F32R)
        m.by_head = sb("by_head", [P, 8, CH])
        m.positions = sb("positions", [P, T])
        m.parts = sb("parts", [P, 6, CH], F32R)
        m.const = sb("const", [P, CONST_COLS])
        m.psum = held.enter_context(nc.psum_tensor("psum", [P, 8, CH], F32))
        part = lambda name: m.const[:, CONST_AT[name]:CONST_AT[name] + dict(CONST_PARTS)[name]]
        m.mean_w, m.ones, m.ident, m.block8, m.block16, m.block64 = (
            part(n) for n in ("mean_w", "ones", "ident", "block8", "block16", "block64"))
        m.tri, m.iota8, m.eps5, m.eps6 = (part(n) for n in ("tri", "iota8", "eps5", "eps6"))
        m.split = {n: part("split_" + n) for n in ("k", "q2", "q3")}
        m.eps = {1e-5: m.eps5, 1e-6: m.eps6}
        scratch = nc.dram_tensor("gates_by_expert", [NE, T], F32, kind="Internal").ap()
        load_columns(nc, [(m.x[:], a["xT"]), (m.const[:], a["const"])])
        with stage(nc, "copied") as (block, s):
            @block.vector
            def _(dve):
                nc.vector.tensor_copy(m.ident_bf[:], m.ident[:])
                nc.vector.tensor_copy(m.causal_bf[:], part("causal"))
        flat = lambda t, i: t[bass.ds(i, 1)].rearrange("o p n -> p (o n)")
        if first > 1:
            load_columns(nc, [(m.s[:], m.x[:]), (m.h[:], m.x[:])])
        if first <= 1 <= stages:
            linear_attention_stage(nc, m, a)
            norm_stage(nc, m, m.s, m.x, 1e-5)
        if first <= 2 <= stages:
            sh = SoftmaxShape(64, 2, True, None, 1.0)
            load_columns(nc, [(m.s[:], m.x[:]), (m.positions[:], a["l0f_rope"])])
            with nc.Fori(0, L0_LAYERS) as layer:
                norm_stage(nc, m, m.x, m.h, 1e-5, rms=True, weight=m.cols[:, 0:1], clip=100.0,
                           loads=[(m.cols[:, 0:2], flat(a["l0f_ln"], layer))])
                softmax_attention_stage(nc, m, sh, a["l0f_attn"], layer * GROUPS)
                norm_stage(nc, m, m.x, m.h, 1e-5, rms=True, weight=m.cols[:, 1:2], clip=100.0)
                router_stage(nc, m, "plain", flat(a["l0f_wr"], layer), scratch)
                experts_stage(nc, m, ExpertShape("gated"), a["l0f_experts"], layer * NE, scratch)
            norm_stage(nc, m, m.x, m.x, 1e-5, clip=100.0, residual=m.s, copy=m.h)
        if first <= 3 <= stages:
            load_columns(nc, [(m.s[:], m.x[:]), (m.positions[:], a["l1a_xpos"])])
            with nc.Fori(0, L1_LAYERS) as layer:
                norm_stage(nc, m, m.x, m.h, 1e-5, weight=m.cols[:, 0:1], bias=m.cols[:, 1:2],
                           loads=[(m.cols[:, 0:4], flat(a["l1a_ln"], layer))])
                causal_attention_stage(nc, m, CausalShape(True), a["l1a_attn"], layer * 2, a["l1a_decays"])
                norm_stage(nc, m, m.x, m.h, 1e-5, weight=m.cols[:, 2:3], bias=m.cols[:, 3:4])
                experts_stage(nc, m, ExpertShape("ffn"), a["l1a_ffn"], layer, scratch)
            norm_stage(nc, m, m.x, m.x, 1e-5, residual=m.s, copy=m.h)
        if first <= 4 <= stages:
            router_stage(nc, m, "norm", a["l1f_wa"], scratch)
            experts_stage(nc, m, ExpertShape("lowrank"), a["l1f_experts"], 0, scratch)
            norm_stage(nc, m, m.x, m.x, 1e-5, copy=m.h)
        if first <= 5 <= stages:
            load_columns(nc, [(m.cols[:, 8:12], a["l2a_qk"])])
            causal_attention_stage(nc, m, CausalShape(False), a["l2a_attn"], 0)
            norm_stage(nc, m, m.x, m.x, 1e-5, copy=m.h)
        if first <= 6 <= stages:
            load_columns(nc, [(m.s[:], m.x[:]), (m.cols[:, 0:5], a["l2f_cols"])])
            softmax_attention_stage(nc, m, SoftmaxShape(32, 1, False, "q2", 1.0), a["l2f_attn"], 0)
            norm_stage(nc, m, m.x, m.h, 1e-6, weight=m.cols[:, 1:2], bias=m.cols[:, 2:3], add=m.cols[:, 0:1], copy=m.x)
            router_stage(nc, m, "double", a["l2f_wr"], scratch)
            experts_stage(nc, m, ExpertShape("gelu"), a["l2f_experts"], 0, scratch)
            norm_stage(nc, m, m.x, m.x, 1e-6, weight=m.cols[:, 3:4], bias=m.cols[:, 4:5])
            norm_stage(nc, m, m.x, m.x, 1e-5, residual=m.s, copy=m.h)
        if first <= 7 <= stages:
            sh = SoftmaxShape(32, 1, False, "q3", (S / (S - 1.0)) ** 0.5 / D)
            softmax_attention_stage(nc, m, sh, a["l3a_attn"], 0)
            norm_stage(nc, m, m.x, m.x, 1e-5)
        if first <= 8 <= stages:
            sign_projection_stage(nc, m, a)
            norm_stage(nc, m, m.s, m.x, 1e-5)
        with stage(nc, "stored") as (block, s):
            @block.sync
            def _(sp):
                sp.dma_start(a["out"], m.x[:]).then_inc(s["stored"], 16)
                sp.wait_ge(s["stored"], 16)


CONST_PARTS = [("mean_w", 128), ("ones", 128), ("ident", 128), ("block8", 128), ("eps5", 1), ("eps6", 1), ("iota8", 8),
               ("block16", 128), ("block64", 128), ("tri", 512), ("causal", 128),
               ("split_k", 2), ("split_q2", 2), ("split_q3", 2)]
CONST_AT = {n: sum(w for _, w in CONST_PARTS[:i]) for i, (n, _) in enumerate(CONST_PARTS)}
CONST_COLS = sum(w for _, w in CONST_PARTS)


def constants():
    i = np.arange(P)

    def split(rounded, scale):
        return np.stack([np.where(rounded, scale, -scale), np.where(rounded, 0.0, scale)], 1)

    parts = {
        "split_k": split(i % 16 < 8, 1.0), "split_q2": split(i % 32 < 16, 8.0 ** -0.5),
        "split_q3": split(i % 32 < 16, 8.0 ** -0.5 / D),
        "mean_w": np.full((P, P), 1.0 / D), "ones": np.ones((P, P)), "ident": np.eye(P),
        "block8": (i[:, None] // 8 == i[None, :] // 8) * 1.0,
        "block16": ((i[:, None] // 32 == i[None, :] // 32) & (i[:, None] % 32 < 16) & (i[None, :] % 32 < 16)) / 16.0,
        "block64": (i[:, None] // 64 == i[None, :] // 64) / 64.0,
        "tri": (np.arange(S)[None, :] >= i[:, None]) * 1.0,
        "causal": np.where(i[None, :] > i[:, None], -1e9, 0.0),
        "iota8": np.tile(np.arange(8.0) - 8, (P, 1)),
        "eps5": np.full((P, 1), 1e-5), "eps6": np.full((P, 1), 1e-6),
    }
    return np.concatenate([parts[n].reshape(P, w) for n, w in CONST_PARTS], 1).astype(np.float32)


def layout(i):
    return {
        "xT": i["L0_attn_x"].reshape(T, D).T,
        "const": constants(),
        "l0a_wqkv": i["L0_attn_w_qkv"].T, "l0a_wout": i["L0_attn_w_out"].T,
        "l0a_bout": i["L0_attn_b_out"].reshape(P, 1),
        "l0f_ln": np.stack([i["L0_ffn_ln1_w"], i["L0_ffn_ln2_w"]], 2),
        "l1a_ln": np.stack([i["L1_attn_ln1_w"], i["L1_attn_ln1_b"], i["L1_attn_ln2_w"], i["L1_attn_ln2_b"]], 2),
        "l1a_attn": retention_weights(i), "l1a_xpos": xpos_tables(), "l1a_decays": decay_tables(),
        "l1a_ffn": biased(i["L1_attn_ffn_w1"], i["L1_attn_ffn_w2"], i["L1_attn_ffn_b1"], i["L1_attn_ffn_b2"]),
        "l1f_wa": i["L1_ffn_W_A"].transpose(2, 0, 1).reshape(D, -1), "l1f_experts": l1f_weights(i),
        "l2a_attn": l2_attention_weights(i),
        "l2a_qk": columns(*(np.tile(i["L2_attn_" + n], 2) for n in ("q_gamma", "q_beta", "k_gamma", "k_beta"))),
        "l2f_attn": padded_attention_weights(i["L2_ffn_Wq"], i["L2_ffn_Wk"], i["L2_ffn_Wv"], i["L2_ffn_Wo"]),
        "l2f_cols": columns(*(i["L2_ffn_" + n] for n in ("bo", "ln1_g", "ln1_b", "ln2_g", "ln2_b"))),
        "l2f_wr": i["L2_ffn_Wr"],
        "l2f_experts": biased(i["L2_ffn_We1"], i["L2_ffn_We2"], i["L2_ffn_be1"], i["L2_ffn_be2"]),
        "l3a_attn": padded_attention_weights(*(i["L3_attn_w_qkv"].T[:, k * D:(k + 1) * D] for k in range(3)),
                                             i["L3_attn_w_o"].T),
        "l3f_w": i["L3_ffn_weights"].T, "l3f_scale_bias": columns(i["L3_ffn_scale"], i["L3_ffn_bias"]),
        "l0f_wr": i["L0_ffn_wr"],
        "l0f_experts": np.concatenate([i["L0_ffn_wg"], i["L0_ffn_wu"], rows_to_columns(i["L0_ffn_wd"])], 3)
        .reshape(L0_LAYERS * NE, P, -1),
        "l0f_attn": l0f_attention_weights(i), "l0f_rope": l0f_rope_tables(),
    }


def rows_to_columns(w):
    w = w.reshape(*w.shape[:-2], -1, P, w.shape[-1])
    return np.moveaxis(w, -3, -2).reshape(*w.shape[:-3], P, -1)


def l0f_attention_weights(i):
    L, HD = L0_LAYERS, 64
    d = np.arange(HD)
    turned = (d + HD // 2) % HD
    wq = i["L0_ffn_wq"].reshape(L, D, GROUPS, 4, HD)
    wk = i["L0_ffn_wk"].reshape(L, D, GROUPS, 1, HD)
    wv = i["L0_ffn_wv"].reshape(L, D, GROUPS, 1, HD)
    wo = i["L0_ffn_wo"].reshape(L, GROUPS, 2, 2 * HD, D).transpose(0, 3, 1, 2, 4)
    kk = np.concatenate([wk, wk], 3)
    parts = [kk, kk[..., turned], wq, wq[..., turned], wv]
    flat = [w.transpose(0, 2, 1, 3, 4).reshape(L * GROUPS, D, -1) for w in parts]
    flat.append(wo.transpose(0, 2, 1, 3, 4).reshape(L * GROUPS, P, -1))
    out = np.concatenate(flat, 2)
    return np.concatenate([out, out[:1]], 0)


def l0f_rope_tables():
    d = np.arange(P) % 64
    inv = (1.0 / np.float32(10000.0) ** (np.arange(0, 64, 2, dtype=np.float32) / np.float32(64))).astype(np.float32)
    ang = (np.arange(S, dtype=np.float32)[None, :] * inv[d % 32][:, None]).astype(np.float32)
    cos, sin = np.cos(ang), np.sin(ang) * np.where(d < 32, -1, 1)[:, None]
    return np.concatenate([cos, sin, cos / 8, sin / 8], 1).astype(np.float32)


def repeat_heads(w, heads, head_dim, rows):
    w = w.reshape(*w.shape[:-1], heads, head_dim)
    w = np.concatenate([w] * (rows // head_dim), -1)
    w = w.reshape(*w.shape[:-2], heads * rows // P, P)
    return np.moveaxis(w, -2, 0)


def pad_heads(w, heads, head_dim, rows):
    w = w.reshape(*w.shape[:-1], heads, head_dim)
    w = np.concatenate([w, np.zeros((*w.shape[:-1], rows - head_dim), w.dtype)], -1)
    w = w.reshape(*w.shape[:-2], heads * rows // P, P)
    return np.moveaxis(w, -2, 0)


def padded_attention_weights(wq, wk, wv, wo):
    k, q, v = repeat_heads(wk, 16, 8, 32), repeat_heads(wq, 16, 8, 32), pad_heads(wv, 16, 8, 32)
    o = np.moveaxis(pad_heads(wo.T, 16, 8, 32), -1, -2)
    out = np.concatenate([k, q, v, o], 2)
    return np.concatenate([out, out[:1]], 0)


def retention_weights(i):
    L = L1_LAYERS
    turned = np.arange(16) ^ 1
    flat = lambda w: w.transpose(0, 2, 1, 3)
    q, k, v = flat(i["L1_attn_WQ"]), flat(i["L1_attn_WK"]), flat(i["L1_attn_WV"])
    pad = lambda w: pad_heads(w.reshape(L, -1, D), 8, 16, 32)
    parts = [pad(q), pad(q[..., turned]), pad(k), pad(k[..., turned]), pad(v), pad(i["L1_attn_WG"]),
             pad(i["L1_attn_WO"].transpose(0, 2, 1)).swapaxes(-1, -2),
             pad(i["L1_attn_gn_w"][:, None]).swapaxes(-1, -2), pad(i["L1_attn_gn_b"][:, None]).swapaxes(-1, -2)]
    out = np.concatenate(parts, 3).transpose(1, 0, 2, 3).reshape(L * 2, P, -1)
    return np.concatenate([out, out[:1]], 0)


def xpos_tables():
    HD, half = 16, 8
    scale_vec = (np.arange(0, HD, 2) + 0.4 * HD) / (1.4 * HD)
    scale = scale_vec[None, :] ** (np.arange(S, dtype=np.float64) / 64)[:, None]
    ang = np.arange(S)[:, None] / 10000.0 ** (np.arange(half) / half)[None, :]
    sin, cos = np.sin(ang), np.cos(ang)
    sign = np.where(np.arange(HD) % 2 == 0, -1.0, 1.0)
    out = []
    for t, sg in ((cos * scale, 1), (sin * scale, sign), (cos / scale, 1), (sin / scale, sign)):
        t = (np.repeat(t, 2, axis=-1).astype(np.float32) * sg).T
        out.append(np.tile(np.concatenate([t, np.zeros((16, S))], 0), (4, 1)))
    return np.concatenate(out, 1).astype(np.float32)


def decay_tables():
    gammas = 1.0 - np.exp(np.linspace(np.log(1.0 / 32), np.log(1.0 / 64), 8))
    diff = (np.arange(S)[None, :] - np.arange(P)[:, None]).astype(np.float64)
    d = np.where(diff >= 0, gammas[:, None, None] ** np.maximum(diff, 0), 0.0)
    d = d.reshape(2, 4, P, S).transpose(0, 2, 1, 3).reshape(2, P, 4 * S).astype(np.float32)
    return np.concatenate([d, d[:1]], 0)


def l2_attention_weights(i):
    split = lambda w: w.T.reshape(D, 8, P).transpose(1, 0, 2)
    wo = i["L2_attn_Wo"].T.reshape(8, P, D)
    out = np.concatenate([split(i["L2_attn_Wq"]), split(i["L2_attn_Wk"]), split(i["L2_attn_Wv"]), wo], 2)
    return np.concatenate([out, out[:1]], 0)


def columns(*vectors):
    return np.stack([np.asarray(v).reshape(P) for v in vectors], 1)


def l1f_weights(i):
    swap = lambda w: w.transpose(0, 2, 1)
    wb = swap(i["L1_ffn_W_B"])
    wb = np.concatenate([wb, np.zeros_like(wb)], 1)
    return np.concatenate([swap(i["L1_ffn_W_A"]), wb, swap(i["L1_ffn_W_up"]),
                           rows_to_columns(swap(i["L1_ffn_W_down"]))], 2)


def biased(w1, w2, b1, b2):
    return np.concatenate([w1, rows_to_columns(w2), b1.reshape(-1, 4, P).transpose(0, 2, 1), b2[:, :, None]], 2)


STAGES = 99
FIRST = 1


def kernel(**inputs):
    import concourse.bacc as bacc
    from concourse.bass_utils import run_bass_kernel_spmd
    nc = bacc.Bacc("TRN2", target_bir_lowering=False, num_devices=1)
    given = {k: np.asarray(v) for k, v in inputs.items()}
    arrays, args = {}, {}
    for name, value in layout(given).items():
        value = np.ascontiguousarray(value)
        arrays[name + "_dram"] = value
        args[name] = nc.dram_tensor(name + "_dram", value.shape, mybir.dt.from_np(value.dtype),
                                    kind="ExternalInput").ap()
    args["out"] = nc.dram_tensor("out_dram", [P, T], F32, kind="ExternalOutput").ap()
    build(nc, args, FIRST, STAGES)
    r = run_bass_kernel_spmd(nc, [arrays], core_ids=[0])
    return np.ascontiguousarray(r.results[0]["out_dram"].T).reshape(B, S, D)
```
